# Optimizing a Trainium2 kernel written in Bass

```python
import numpy as np
import jax
import jax.numpy as jnp

def _softmax(x, axis=-1):
    return jax.nn.softmax(x, axis=axis)

def _gelu(x):
    return jax.nn.gelu(x, approximate=True)

def _silu(x):
    return jax.nn.silu(x)

def _sigmoid(x):
    return jax.nn.sigmoid(x)

def _layernorm(x, axis=-1, eps=1e-05):
    m = jnp.mean(x, axis=axis, keepdims=True)
    v = jnp.var(x, axis=axis, keepdims=True)
    return (x - m) / jnp.sqrt(v + eps)

def _scatter_add(tgt, idx, src, axis=0):
    return tgt.at[idx].add(src)

def _segment_sum(src, seg, n):
    return jax.ops.segment_sum(src, seg, n)
kernel_name = 'mk_perceiver_d2_seqx_r8_276f8c'

def setup_inputs(seed: int=0):
    np.random.seed(seed)
    _w = jnp.asarray

    def _rec_inputs():
        import jax
        import jax.numpy as jnp
        _rk = jax.random.key(seed)
        x = -0.0003929 + 0.9999 * jax.random.normal(jax.random.fold_in(_rk, 1), (8, 64, 512), jnp.float32)
        _lenS = 64 - jax.random.randint(jax.random.fold_in(_rk, 7), (8,), 0, max(1, 64 // 4) + 1, jnp.int32)
        _lenS2 = 1601 - jax.random.randint(jax.random.fold_in(_rk, 8), (8,), 0, max(1, 1601 // 4) + 1, jnp.int32)
        _ctx_4096P = jax.random.normal(jax.random.fold_in(_rk, 11), (8, 16, 512), jnp.float32)
        _ctx_4096c = jax.random.dirichlet(jax.random.fold_in(_rk, 511), 0.3 * jnp.ones((16,), jnp.float32), (8, 1601))
        _ctx_4096t = jnp.einsum('bsk,bkd->bsd', _ctx_4096c, _ctx_4096P)
        _ctx_4096t = _ctx_4096t * jax.lax.rsqrt(jnp.mean(jnp.square(_ctx_4096t)) + 1e-12) * 0.953939
        ctx_4096 = 2.81802e-05 + 1.00001 * (_ctx_4096t + 0.3 * jax.random.normal(jax.random.fold_in(_rk, 611), (8, 1601, 512), jnp.float32))
        return (x, ctx_4096)
    x, ctx_4096 = _rec_inputs()

    def _L0_xattn_setup():
        import jax, jax.numpy as jnp
        import numpy as np
        HID = 512
        NHEAD = 32
        NKV = 8
        HDIM = 128
        G = NHEAD // NKV
        key = jax.random.key(seed)
        ks = jax.random.split(key, 6)
        s = 0.02
        B, L = (2, 256)
        return {'query': jax.random.normal(ks[0], (B, L, HID), jnp.float32), 'kv': jax.random.normal(ks[1], (B, L, HID), jnp.float32), 'Wq': jax.random.normal(ks[2], (HID, NHEAD * HDIM), jnp.float32) * s, 'bq': jnp.zeros((NHEAD * HDIM,), jnp.float32), 'Wkv': jax.random.normal(ks[3], (HID, 2 * NKV * HDIM), jnp.float32) * s, 'bkv': jnp.zeros((2 * NKV * HDIM,), jnp.float32), 'Wo': jax.random.normal(ks[4], (NHEAD * HDIM, HID), jnp.float32) * s, 'bo': jnp.zeros((HID,), jnp.float32)}
    _L0_xattn_all = _L0_xattn_setup()
    _L0_xattn_in = {k: v for k, v in _L0_xattn_all.items() if k in ('Wq', 'bq', 'Wkv', 'bkv', 'Wo', 'bo')}
    del _L0_xattn_all

    def _L0_attn_setup():
        import jax, jax.numpy as jnp
        import numpy as np
        H = 512
        D_IN = 1024
        N = 16
        K = 4
        R = 32
        EPS = 1e-06

        def rms_forward(x, eps=EPS):
            xf = x.astype(jnp.float32)
            var = jnp.mean(xf * xf, axis=-1, keepdims=True)
            return (xf * jax.lax.rsqrt(var + eps)).astype(x.dtype)
        key = jax.random.key(seed)
        ks = jax.random.split(key, 10)
        s = 0.02
        hidden_states = jax.random.normal(ks[0], (2, 128, H), dtype=jnp.float32)
        W_in = jax.random.normal(ks[1], (2 * D_IN, H), dtype=jnp.float32) * s
        conv_w = jax.random.normal(ks[2], (D_IN, K), dtype=jnp.float32) * 0.2
        conv_b = jax.random.normal(ks[3], (D_IN,), dtype=jnp.float32) * 0.02
        W_x = jax.random.normal(ks[4], (R + 2 * N, D_IN), dtype=jnp.float32) * s
        W_dt = jax.random.normal(ks[5], (D_IN, R), dtype=jnp.float32) * s
        b_dt = jax.random.normal(ks[6], (D_IN,), dtype=jnp.float32) * 0.02
        A_log = jnp.log(jnp.broadcast_to(jnp.arange(1, N + 1, dtype=jnp.float32)[None, :], (D_IN, N)))
        D = jnp.ones((D_IN,), dtype=jnp.float32)
        W_out = jax.random.normal(ks[7], (H, D_IN), dtype=jnp.float32) * s
        return {'hidden_states': hidden_states, 'W_in': W_in, 'conv_w': conv_w, 'conv_b': conv_b, 'W_x': W_x, 'W_dt': W_dt, 'b_dt': b_dt, 'A_log': A_log, 'D': D, 'W_out': W_out}
    _L0_attn_all = _L0_attn_setup()
    _L0_attn_in = {k: v for k, v in _L0_attn_all.items() if k in ('W_in', 'conv_w', 'conv_b', 'W_x', 'W_dt', 'b_dt', 'A_log', 'D', 'W_out')}
    del _L0_attn_all

    def _L0_ffn_setup():
        import jax, jax.numpy as jnp
        import numpy as np
        THRESHOLD = 0.5

        def ternarize(w, threshold=THRESHOLD):
            mag = jnp.abs(w)
            mask = mag > threshold
            cnt = jnp.sum(mask)
            ssum = jnp.sum(jnp.where(mask, mag, 0.0))
            scale = jnp.where(cnt > 0, ssum / jnp.maximum(cnt, 1).astype(w.dtype), jnp.asarray(1.0, w.dtype))
            ternary = jnp.sign(w) * mask.astype(w.dtype)
            return ternary * scale
        key = jax.random.key(seed)
        k1, k2 = jax.random.split(key)
        B, S, D_IN, D_OUT = (8, 256, 512, 512)
        x = jax.random.normal(k1, (B, S, D_IN), dtype=jnp.float32)
        weight = 0.8 * jax.random.normal(k2, (D_OUT, D_IN), dtype=jnp.float32)
        bias = jnp.zeros((D_OUT,), dtype=jnp.float32)
        return {'x': x, 'weight': weight, 'bias': bias}
    _L0_ffn_all = _L0_ffn_setup()
    _L0_ffn_in = {k: v for k, v in _L0_ffn_all.items() if k in ('weight', 'bias')}
    del _L0_ffn_all

    def _L1_xattn_setup():
        import jax, jax.numpy as jnp
        import numpy as np
        key = jax.random.key(seed)
        k1, k2 = jax.random.split(key)
        B, Lq, Lk, D = (16, 128, 256, 512)
        query = jax.random.normal(k1, (B, Lq, D), dtype=jnp.float32)
        key_t = jax.random.normal(k2, (B, Lk, D), dtype=jnp.float32)
        return {'query': query, 'key': key_t}
    _L1_xattn_all = _L1_xattn_setup()
    _L1_xattn_in = {k: v for k, v in _L1_xattn_all.items() if k in ()}
    del _L1_xattn_all

    def _L1_attn_setup():
        import jax, jax.numpy as jnp
        import numpy as np
        NEG_INF = -1e+30

        def rotary_pos_emb(x):
            B, T, H, D = x.shape
            exponents = (jnp.arange(0, D, 2)[:D // 2] // D).astype(jnp.float32)
            freqs = 1.0 / jnp.power(jnp.float32(1000.0), exponents)
            theta = jnp.arange(T, dtype=jnp.float32)[:, None] * freqs[None, :]
            cos = jnp.cos(theta)[None, :, None, :]
            sin = jnp.sin(theta)[None, :, None, :]
            xr = x.astype(jnp.float32).reshape(B, T, H, D // 2, 2)
            x0, x1 = (xr[..., 0], xr[..., 1])
            out = jnp.stack([x0 * cos - x1 * sin, x0 * sin + x1 * cos], axis=-1)
            return out.reshape(B, T, H, D).astype(x.dtype)

        def attention_fwd(x, wq, wk, wv, wo, n_heads=32):
            B, T, C = x.shape
            hd = C // n_heads
            xq = (x @ wq.T).reshape(B, T, n_heads, hd)
            xk = (x @ wk.T).reshape(B, T, n_heads, hd)
            xv = (x @ wv.T).reshape(B, T, n_heads, hd)
            xq = rotary_pos_emb(xq)
            xk = rotary_pos_emb(xk)
            scale = hd ** (-0.5)
            scores = jnp.einsum('bqhd,bkhd->bhqk', xq, xk) * scale
            causal = jnp.tril(jnp.ones((T, T), dtype=bool))
            scores = jnp.where(causal[None, None], scores, NEG_INF)
            probs = jax.nn.softmax(scores.astype(jnp.float32), axis=-1).astype(xq.dtype)
            out = jnp.einsum('bhqk,bkhd->bqhd', probs, xv).reshape(B, T, C)
            return out @ wo.T
        key = jax.random.key(seed)
        ks = jax.random.split(key, 5)
        B, T, C = (2, 256, 512)
        s = 0.02
        return {'x': jax.random.normal(ks[0], (B, T, C), jnp.float32), 'wq': jax.random.normal(ks[1], (C, C), jnp.float32) * s, 'wk': jax.random.normal(ks[2], (C, C), jnp.float32) * s, 'wv': jax.random.normal(ks[3], (C, C), jnp.float32) * s, 'wo': jax.random.normal(ks[4], (C, C), jnp.float32) * s}
    _L1_attn_all = _L1_attn_setup()
    _L1_attn_in = {k: v for k, v in _L1_attn_all.items() if k in ('wq', 'wk', 'wv', 'wo')}
    del _L1_attn_all

    def _L1_ffn_setup():
        import jax, jax.numpy as jnp
        import numpy as np
        _TRIPLES = [(1, 2, 3), (1, 4, 5), (1, 7, 6), (2, 4, 6), (2, 5, 7), (3, 4, 7), (3, 6, 5)]

        def _oct_struct():
            S = np.zeros((8, 8, 8), np.float32)
            S[0, 0, 0] = 1.0
            for i in range(1, 8):
                S[0, i, i] = 1.0
                S[i, 0, i] = 1.0
                S[i, i, 0] = -1.0
            for a, b, c in _TRIPLES:
                for x, y, z in ((a, b, c), (b, c, a), (c, a, b)):
                    S[x, y, z] = 1.0
                    S[y, x, z] = -1.0
            return jnp.asarray(S)
        S_OCT = _oct_struct()
        N_EMBD = 512
        HIDDEN = 1366

        def ternary_dequant(W):
            scale = jnp.mean(jnp.abs(W))
            Wq = scale * jnp.clip(jnp.round(W / scale), -1.0, 1.0)
            return W + jax.lax.stop_gradient(Wq - W)

        def oct_ternary_linear(xp, W):
            Wq = ternary_dequant(W)
            M = jnp.einsum('jik,jod->koid', S_OCT, Wq)
            return jnp.einsum('...id,koid->...ko', xp, M)
        key = jax.random.key(seed)
        k1, k2, k3, k4 = jax.random.split(key, 4)
        B, T = (2, 256)
        d8, h8 = (N_EMBD // 8, HIDDEN // 8)
        std_in = 1.0 / np.sqrt(N_EMBD)
        std_h = 1.0 / np.sqrt(HIDDEN)
        return {'x': jax.random.normal(k1, (B, T, N_EMBD), jnp.float32), 'w_gate': jax.random.normal(k2, (8, h8, d8), jnp.float32) * std_in, 'w_up': jax.random.normal(k3, (8, h8, d8), jnp.float32) * std_in, 'w_down': jax.random.normal(k4, (8, d8, h8), jnp.float32) * std_h}
    _L1_ffn_all = _L1_ffn_setup()
    _L1_ffn_in = {k: v for k, v in _L1_ffn_all.items() if k in ('w_gate', 'w_up', 'w_down')}
    del _L1_ffn_all
    return {'x': x, 'ctx_4096': ctx_4096, 'L0_xattn_Wq': _L0_xattn_in['Wq'], 'L0_xattn_bq': _L0_xattn_in['bq'], 'L0_xattn_Wkv': _L0_xattn_in['Wkv'], 'L0_xattn_bkv': _L0_xattn_in['bkv'], 'L0_xattn_Wo': _L0_xattn_in['Wo'], 'L0_xattn_bo': _L0_xattn_in['bo'], 'L0_attn_W_in': _L0_attn_in['W_in'], 'L0_attn_conv_w': _L0_attn_in['conv_w'], 'L0_attn_conv_b': _L0_attn_in['conv_b'], 'L0_attn_W_x': _L0_attn_in['W_x'], 'L0_attn_W_dt': _L0_attn_in['W_dt'], 'L0_attn_b_dt': _L0_attn_in['b_dt'], 'L0_attn_A_log': _L0_attn_in['A_log'], 'L0_attn_D': _L0_attn_in['D'], 'L0_attn_W_out': _L0_attn_in['W_out'], 'L0_ffn_weight': _L0_ffn_in['weight'], 'L0_ffn_bias': _L0_ffn_in['bias'], 'L1_attn_wq': _L1_attn_in['wq'], 'L1_attn_wk': _L1_attn_in['wk'], 'L1_attn_wv': _L1_attn_in['wv'], 'L1_attn_wo': _L1_attn_in['wo'], 'L1_ffn_w_gate': _L1_ffn_in['w_gate'], 'L1_ffn_w_up': _L1_ffn_in['w_up'], 'L1_ffn_w_down': _L1_ffn_in['w_down']}

def reference(x, ctx_4096, L0_xattn_Wq, L0_xattn_bq, L0_xattn_Wkv, L0_xattn_bkv, L0_xattn_Wo, L0_xattn_bo, L0_attn_W_in, L0_attn_conv_w, L0_attn_conv_b, L0_attn_W_x, L0_attn_W_dt, L0_attn_b_dt, L0_attn_A_log, L0_attn_D, L0_attn_W_out, L0_ffn_weight, L0_ffn_bias, L1_attn_wq, L1_attn_wk, L1_attn_wv, L1_attn_wo, L1_ffn_w_gate, L1_ffn_w_up, L1_ffn_w_down):
    import jax
    import jax.numpy as jnp

    def _L0_xattn_ref(query, kv, Wq, bq, Wkv, bkv, Wo, bo):
        import jax, jax.numpy as jnp
        import numpy as np
        HID = 512
        NHEAD = 32
        NKV = 8
        HDIM = 128
        G = NHEAD // NKV
        B, L, _ = query.shape
        Lk = kv.shape[1]
        scale = jnp.asarray(1.0 / np.sqrt(HDIM), query.dtype)
        q = (query @ Wq + bq).reshape(B, L, NKV, G, HDIM)
        k_, v_ = jnp.split(kv @ Wkv + bkv, 2, axis=-1)
        k = k_.reshape(B, Lk, NKV, HDIM)
        v = v_.reshape(B, Lk, NKV, HDIM)
        scores = jnp.einsum('blkgd,bmkd->bkglm', q, k) * scale
        attn = jax.nn.softmax(scores, axis=-1)
        o = jnp.einsum('bkglm,bmkd->blkgd', attn, v).reshape(B, L, NHEAD * HDIM)
        return o @ Wo + bo

    def _L0_attn_ref(hidden_states, W_in, conv_w, conv_b, W_x, W_dt, b_dt, A_log, D, W_out):
        import jax, jax.numpy as jnp
        import numpy as np
        H = 512
        D_IN = 1024
        N = 16
        K = 4
        R = 32
        EPS = 1e-06

        def rms_forward(x, eps=EPS):
            xf = x.astype(jnp.float32)
            var = jnp.mean(xf * xf, axis=-1, keepdims=True)
            return (xf * jax.lax.rsqrt(var + eps)).astype(x.dtype)
        b, L, _ = hidden_states.shape
        proj = hidden_states @ W_in.T
        x, gate = (proj[..., :D_IN], proj[..., D_IN:])
        xpad = jnp.pad(x, ((0, 0), (K - 1, 0), (0, 0)))
        xc = conv_b
        for j in range(K):
            xc = xc + conv_w[:, j] * xpad[:, j:j + L, :]
        x = jax.nn.silu(xc)
        ssm = x @ W_x.T
        ts, Bm, Cm = (ssm[..., :R], ssm[..., R:R + N], ssm[..., R + N:])
        ts = rms_forward(ts)
        Bm = rms_forward(Bm)
        Cm = rms_forward(Cm)
        dt = jax.nn.softplus(ts @ W_dt.T + b_dt)
        A = -jnp.exp(A_log.astype(jnp.float32))

        def step(state, inp):
            dt_t, B_t, C_t, u_t = inp
            dA = jnp.exp(dt_t[..., None] * A)
            state = state * dA + (dt_t * u_t)[..., None] * B_t[:, None, :]
            y = jnp.einsum('bdn,bn->bd', state, C_t)
            return (state, y)
        init = jnp.zeros((b, D_IN, N), dtype=jnp.float32)
        xs = (dt.transpose(1, 0, 2), Bm.transpose(1, 0, 2), Cm.transpose(1, 0, 2), x.transpose(1, 0, 2))
        _, ys = jax.lax.scan(step, init, xs)
        y = ys.transpose(1, 0, 2) + x * D
        y = y * jax.nn.silu(gate)
        return y @ W_out.T

    def _L0_ffn_ref(x, weight, bias):
        import jax, jax.numpy as jnp
        import numpy as np
        THRESHOLD = 0.5

        def ternarize(w, threshold=THRESHOLD):
            mag = jnp.abs(w)
            mask = mag > threshold
            cnt = jnp.sum(mask)
            ssum = jnp.sum(jnp.where(mask, mag, 0.0))
            scale = jnp.where(cnt > 0, ssum / jnp.maximum(cnt, 1).astype(w.dtype), jnp.asarray(1.0, w.dtype))
            ternary = jnp.sign(w) * mask.astype(w.dtype)
            return ternary * scale
        w_t = ternarize(weight)
        return jnp.einsum('bsd,od->bso', x, w_t) + bias

    def _L1_xattn_ref(query, key):
        import jax, jax.numpy as jnp
        import numpy as np
        a = jnp.einsum('bqd,bkd->bqk', query, key)
        e = jax.nn.softmax(a, axis=-1)
        c = jnp.einsum('bqk,bkd->bqd', e, key)
        return c

    def _L1_attn_ref(x, wq, wk, wv, wo):
        import jax, jax.numpy as jnp
        import numpy as np
        NEG_INF = -1e+30

        def rotary_pos_emb(x):
            B, T, H, D = x.shape
            exponents = (jnp.arange(0, D, 2)[:D // 2] // D).astype(jnp.float32)
            freqs = 1.0 / jnp.power(jnp.float32(1000.0), exponents)
            theta = jnp.arange(T, dtype=jnp.float32)[:, None] * freqs[None, :]
            cos = jnp.cos(theta)[None, :, None, :]
            sin = jnp.sin(theta)[None, :, None, :]
            xr = x.astype(jnp.float32).reshape(B, T, H, D // 2, 2)
            x0, x1 = (xr[..., 0], xr[..., 1])
            out = jnp.stack([x0 * cos - x1 * sin, x0 * sin + x1 * cos], axis=-1)
            return out.reshape(B, T, H, D).astype(x.dtype)

        def attention_fwd(x, wq, wk, wv, wo, n_heads=32):
            B, T, C = x.shape
            hd = C // n_heads
            xq = (x @ wq.T).reshape(B, T, n_heads, hd)
            xk = (x @ wk.T).reshape(B, T, n_heads, hd)
            xv = (x @ wv.T).reshape(B, T, n_heads, hd)
            xq = rotary_pos_emb(xq)
            xk = rotary_pos_emb(xk)
            scale = hd ** (-0.5)
            scores = jnp.einsum('bqhd,bkhd->bhqk', xq, xk) * scale
            causal = jnp.tril(jnp.ones((T, T), dtype=bool))
            scores = jnp.where(causal[None, None], scores, NEG_INF)
            probs = jax.nn.softmax(scores.astype(jnp.float32), axis=-1).astype(xq.dtype)
            out = jnp.einsum('bhqk,bkhd->bqhd', probs, xv).reshape(B, T, C)
            return out @ wo.T
        return attention_fwd(x, wq, wk, wv, wo)

    def _L1_ffn_ref(x, w_gate, w_up, w_down):
        import jax, jax.numpy as jnp
        import numpy as np
        _TRIPLES = [(1, 2, 3), (1, 4, 5), (1, 7, 6), (2, 4, 6), (2, 5, 7), (3, 4, 7), (3, 6, 5)]

        def _oct_struct():
            S = np.zeros((8, 8, 8), np.float32)
            S[0, 0, 0] = 1.0
            for i in range(1, 8):
                S[0, i, i] = 1.0
                S[i, 0, i] = 1.0
                S[i, i, 0] = -1.0
            for a, b, c in _TRIPLES:
                for x, y, z in ((a, b, c), (b, c, a), (c, a, b)):
                    S[x, y, z] = 1.0
                    S[y, x, z] = -1.0
            return jnp.asarray(S)
        S_OCT = _oct_struct()
        N_EMBD = 512
        HIDDEN = 1366

        def ternary_dequant(W):
            scale = jnp.mean(jnp.abs(W))
            Wq = scale * jnp.clip(jnp.round(W / scale), -1.0, 1.0)
            return W + jax.lax.stop_gradient(Wq - W)

        def oct_ternary_linear(xp, W):
            Wq = ternary_dequant(W)
            M = jnp.einsum('jik,jod->koid', S_OCT, Wq)
            return jnp.einsum('...id,koid->...ko', xp, M)
        B, T, D = x.shape
        xp = x.reshape(B, T, 8, D // 8)
        gate = oct_ternary_linear(xp, w_gate).reshape(B, T, -1)
        up = oct_ternary_linear(xp, w_up).reshape(B, T, -1)
        h = jax.nn.silu(gate) * up
        hp = h.reshape(B, T, 8, h.shape[-1] // 8)
        out = oct_ternary_linear(hp, w_down).reshape(B, T, D)
        return out
    x = x + _L0_xattn_ref(_layernorm(x, axis=-1), ctx_4096, L0_xattn_Wq, L0_xattn_bq, L0_xattn_Wkv, L0_xattn_bkv, L0_xattn_Wo, L0_xattn_bo)
    x = x + _L0_attn_ref(_layernorm(x, axis=-1), L0_attn_W_in, L0_attn_conv_w, L0_attn_conv_b, L0_attn_W_x, L0_attn_W_dt, L0_attn_b_dt, L0_attn_A_log, L0_attn_D, L0_attn_W_out)
    x = x + _L0_ffn_ref(_layernorm(x, axis=-1), L0_ffn_weight, L0_ffn_bias)
    x = x + _L1_xattn_ref(_layernorm(x, axis=-1), ctx_4096)
    x = x + _L1_attn_ref(_layernorm(x, axis=-1), L1_attn_wq, L1_attn_wk, L1_attn_wv, L1_attn_wo)
    x = x + _L1_ffn_ref(_layernorm(x, axis=-1), L1_ffn_w_gate, L1_ffn_w_up, L1_ffn_w_down)
    return x

_drawn_inputs = setup_inputs


def setup_inputs(seed=0):
    import zlib

    import numpy as np

    out = dict(_drawn_inputs(seed))
    spreads = {'L0_xattn_bq': (0.0, 0.8),
     'L0_xattn_bkv': (0.0, 0.1),
     'L0_xattn_bo': (0.0, 0.1),
     'L0_attn_D': (1.0, 0.6),
     'L0_ffn_bias': (0.0, 0.8)}
    factors = {'L0_xattn_Wq': 3.704,
     'L0_attn_conv_b': 8.0,
     'L0_attn_W_dt': 8.0,
     'L0_attn_b_dt': 27.056,
     'L0_attn_A_log': 23.332,
     'L1_attn_wq': 8.0,
     'L1_attn_wk': 8.0,
     'L1_attn_wv': 8.0,
     'L1_attn_wo': 8.0,
     'L1_ffn_w_gate': 7.86,
     'L1_ffn_w_up': 7.561,
     'L1_ffn_w_down': 7.54}
    for name, (base, spread) in spreads.items():
        noise = np.random.default_rng([zlib.crc32(name.encode()), seed]).standard_normal(out[name].shape)
        drawn = base * np.exp(spread * noise) if base else spread * noise
        out[name] = jnp.asarray(drawn.astype(out[name].dtype))
    for name, factor in factors.items():
        out[name] = (out[name] * factor).astype(out[name].dtype)
    return out
```

```python
from contextlib import ExitStack

import numpy as np
import concourse.bass as bass
from concourse import mybir
from concourse.alu_op_type import AluOpType as ALU

F32 = mybir.dt.float32
F32R = mybir.dt.float32r
ACT = mybir.ActivationFunctionType
AX_X = mybir.AxisListType.X
P = 128


class Scope:

    def __init__(self, nc, name):
        self.nc, self.name, self.stack, self.sems = nc, name, ExitStack(), []

    def __enter__(self):
        self.stack.__enter__()
        return self

    def __exit__(self, *a):
        self.stack.__exit__(*a)
        if self.sems:
            self.nc.clear_and_free_semaphores(self.sems)
            self.nc.all_engine_barrier()

    def sb(self, name, shape, dt=F32):
        return self.stack.enter_context(self.nc.sbuf_tensor(f"{self.name}_{name}", shape, dt))

    def ps(self, name, shape):
        return self.stack.enter_context(self.nc.psum_tensor(f"{self.name}_{name}", shape, F32))

    def sem(self, name):
        self.sems.append(self.nc.alloc_semaphore(f"{self.name}_{name}"))
        return self.sems[-1]

    def block(self):
        return self.stack.enter_context(self.nc.Block())


def apart(eng, passed):
    eng.sem_inc(passed, 1)


def product(nc, out, left, right, first, last):
    nc.tensor.matmul(out, left[0], right[0], start=first, stop=False)
    nc.tensor.matmul(out, left[0], right[1], start=False, stop=False)
    return nc.tensor.matmul(out, left[1], right[0], start=False, stop=last)


def even_tiles(n, most=512):
    count = -(-n // most)
    step = -(-n // (2 * count)) * 2
    return [(c, min(step, n - c)) for c in range(0, n, step)]


def cross_attention(nc, ctx_t, wk, wv, bk, bv, ident, q_dram, o_dram):
    B, _, KC, S = ctx_t.shape
    NKV = wk.shape[0]
    D = wk.shape[3]
    NQ = q_dram.shape[3]
    NU = NQ // P
    SE = S + S % 2
    NC = -(-S // P)
    NG = -(-NC // 2)
    TILES = even_tiles(SE)
    NT = len(TILES)
    SCALE = float(D) ** -0.5
    NPT = 2
    LO_DVE = 1

    def rows(c):
        return min(P, S - c * P)

    KV_TILES = NKV * NT + NKV // 2 * NG
    S_TILES = NKV * NU * NT
    PAIRS = NKV * NG

    def kv_tile(j):
        return j * NT + (j + 1) // 2 * NG

    def projections(b, j, last):
        tiles = []
        if j % 2 == 0:
            tiles += [("v", j, g, kv_tile(j) + NT + g) for g in range(NG)]
        if not (last and j == NKV - 1):
            tiles += [("k", j + 1, t, kv_tile(j + 1) + t) for t in range(NT)]
        return tiles

    def kv_done(b, tiles):
        return b * KV_TILES + tiles + KV_TILES

    def drive(eng, first, group, tail):
        first()
        with eng.Fori(0, B - 1) as b:
            for j in range(1, NKV + 1):
                group(b, j, False)
        for j in range(1, NKV):
            group(B - 1, j, True)
        tail(B - 1)

    with Scope(nc, "xa") as sc:
        raw = sc.sb("ctx_raw", [P, KC, SE])
        ctx_hi, ctx_lo = sc.sb("ctx_hi", [P, KC, SE], F32R), sc.sb("ctx_lo", [P, KC, SE], F32R)
        wk_raw = sc.sb("wk_raw", [P, 2, KC, D])
        wk_hi, wk_lo = sc.sb("wk_hi", [P, 2, KC, D], F32R), sc.sb("wk_lo", [P, 2, KC, D], F32R)
        wv_raw = sc.sb("wv_raw", [P, KC, 2 * D])
        wv_hi, wv_lo = sc.sb("wv_hi", [P, KC, 2 * D], F32R), sc.sb("wv_lo", [P, KC, 2 * D], F32R)
        q_raw = sc.sb("q_raw", [P, 2, NQ])
        q_hi, q_lo = sc.sb("q_hi", [P, 2, NQ], F32R), sc.sb("q_lo", [P, 2, NQ], F32R)
        k_hi, k_lo = sc.sb("k_hi", [P, SE], F32R), sc.sb("k_lo", [P, SE], F32R)
        v_hi, v_lo = sc.sb("v_hi", [P, NC, 2 * D], F32R), sc.sb("v_lo", [P, NC, 2 * D], F32R)
        prob = sc.sb("prob", [P, 2, NU, SE])
        pt_hi, pt_lo = sc.sb("pt_hi", [P, NPT, 2, NQ], F32R), sc.sb("pt_lo", [P, NPT, 2, NQ], F32R)
        tmax = sc.sb("tmax", [P, NU, NT])
        nmax = sc.sb("nmax", [P, NU])
        den = sc.sb("den", [P, NU])
        rden = sc.sb("rden", [P, NU])
        o_sb = sc.sb("o_sb", [P, 2, NQ])
        bk_sb, bv_sb = sc.sb("bk_sb", [P, NKV]), sc.sb("bv_sb", [P, NKV])
        kv_ps = sc.ps("kv_ps", [P, 2, 512])
        s_ps = sc.ps("s_ps", [P, 2, 512])
        t_ps = sc.ps("t_ps", [P, 2, 512])
        o_ps = sc.ps("o_ps", [P, 2, 512])

        bias_in = sc.sem("bias_in")
        ctx_in = [sc.sem(f"ctx_in{t}") for t in range(NT)]
        wk_in = [sc.sem(f"wk_in{i}") for i in range(2)]
        wv_in = sc.sem("wv_in")
        q_in = [sc.sem(f"q_in{i}") for i in range(2)]
        pad_set = sc.sem("pad_set")
        passed = sc.sem("passed")
        ctx_hi_set = sc.sem("ctx_hi_set")
        ctx_lo_dve, ctx_lo_pool = sc.sem("ctx_lo_dve"), sc.sem("ctx_lo_pool")
        w_hi_set = sc.sem("w_hi_set")
        wk_split, wv_split, q_split = sc.sem("wk_split"), sc.sem("wv_split"), sc.sem("q_split")
        kv_full, kv_hi, kv_free = sc.sem("kv_full"), sc.sem("kv_hi"), sc.sem("kv_free")
        s_full, s_free = sc.sem("s_full"), sc.sem("s_free")
        nmax_set, exp_done, rden_set, prob_set = (
            sc.sem("nmax_set"), sc.sem("exp_done"), sc.sem("rden_set"), sc.sem("prob_set"))
        t_full, t_hi, t_free = sc.sem("t_full"), sc.sem("t_hi"), sc.sem("t_free")
        pt_free = sc.sem("pt_free")
        o_full, o_free = sc.sem("o_full"), sc.sem("o_free")
        o_out = [sc.sem(f"o_out{i}") for i in range(2)]
        block = sc.block()

        @block.sync
        def _(sp):
            def load_ctx(b):
                for t, (c, w) in enumerate(TILES):
                    w = min(w, S - c)
                    sp.dma_start(raw[:, :, c:c + w], ctx_t[b][:, :, c:c + w]).then_inc(ctx_in[t], 16)

            def group(b, j, last):
                n = b * NKV + j
                g = j % NKV
                sp.wait_ge(wk_split, n + 1)
                sp.dma_start(wk_raw[:, j % 2], wk[g]).then_inc(wk_in[j % 2], 16)
                sp.wait_ge(q_split, n + 1)
                sp.dma_start(q_raw[:, j % 2], q_dram[b + j // NKV, g]).then_inc(q_in[j % 2], 16)
                if j % 2 == 0:
                    sp.wait_ge(wv_split, b * (NKV // 2) + j // 2 + 1)
                    sp.dma_start(wv_raw[:, :, :], wv[g // 2]).then_inc(wv_in, 16)
                if j == 2 and not last:
                    sp.wait_ge(ctx_lo_dve, b * LO_DVE + LO_DVE)
                    sp.wait_ge(ctx_lo_pool, b * (NT - LO_DVE) + NT - LO_DVE)
                    load_ctx(b + 1)

            def first():
                group(0, 0, False)
                load_ctx(0)
                sp.dma_start(bk_sb[:, :], bk).then_inc(bias_in, 16)
                sp.dma_start(bv_sb[:, :], bv).then_inc(bias_in, 16)

            drive(sp, first, group, lambda b: None)

        @block.gpsimd
        def _(pool):
            def halves(hi, lo, src, count):
                apart(pool, passed)
                nc.gpsimd.tensor_scalar(hi, src, 1.0, 1.0, ALU.mult, ALU.mult).then_inc(w_hi_set, 1)
                pool.wait_ge(w_hi_set, count)
                return nc.gpsimd.tensor_tensor(lo, src, hi.bitcast(F32), ALU.subtract)

            def split_ctx(b, n):
                for t, (c, w) in enumerate(TILES):
                    pool.wait_ge(ctx_in[t], (n + 1) * 16)
                    if b is not None:
                        pool.wait_ge(kv_full, kv_done(b, kv_tile(NKV - 1) + t + 1))
                        apart(pool, passed)
                    nc.gpsimd.tensor_scalar(ctx_hi[:, :, c:c + w], raw[:, :, c:c + w], 1.0, 1.0,
                                            ALU.mult, ALU.mult).then_inc(ctx_hi_set, 1)
                for t, (c, w) in enumerate(TILES):
                    if t >= LO_DVE:
                        pool.wait_ge(ctx_hi_set, n * NT + t + 1)
                        nc.gpsimd.tensor_tensor(ctx_lo[:, :, c:c + w], raw[:, :, c:c + w],
                                                ctx_hi[:, :, c:c + w].bitcast(F32),
                                                ALU.subtract).then_inc(ctx_lo_pool, 1)

            def weights(b, j):
                k = b * (2 * NKV + NKV // 2) + 2 * j + (j + 1) // 2
                pool.wait_ge(wk_in[j % 2], (b * (NKV // 2) + j // 2 + 1) * 16)
                pool.wait_ge(kv_full, kv_done(b, kv_tile(j - 2) + NT))
                halves(wk_hi[:, j % 2], wk_lo[:, j % 2], wk_raw[:, j % 2], k + 1).then_inc(wk_split, 1)
                pool.wait_ge(q_in[j % 2], (b * (NKV // 2) + j // 2 + 1) * 16)
                pool.wait_ge(s_full, b * S_TILES + (j - 1) * NU * NT + S_TILES)
                halves(q_hi[:, j % 2], q_lo[:, j % 2], q_raw[:, j % 2], k + 2).then_inc(q_split, 1)
                if j % 2 == 0:
                    pool.wait_ge(wv_in, (b * (NKV // 2) + j // 2 + 1) * 16)
                    pool.wait_ge(kv_full, kv_done(b, kv_tile(j - 2) + NT + NG))
                    halves(wv_hi[:, :, :], wv_lo[:, :, :], wv_raw[:, :, :], k + 3).then_inc(wv_split, 1)

            def first():
                pool.sem_inc(wk_split, 2)
                pool.sem_inc(q_split, 2)
                pool.sem_inc(wv_split, 1)
                nc.gpsimd.memset(raw[:, :, SE - 1:SE], 0.0).then_inc(pad_set, 1)
                pool.wait_ge(pad_set, 1)
                weights(0, 0)
                split_ctx(None, 0)

            def group(b, j, last):
                weights(b, j)
                if j == NKV:
                    split_ctx(b, b + 1)

            drive(pool, first, group, lambda b: None)

        @block.tensor
        def _(pe):
            pe.sem_inc(kv_full, KV_TILES)
            pe.sem_inc(s_full, S_TILES)
            pe.sem_inc(pt_free, NPT)

            def key_tile(b, j, t, n):
                c, w = TILES[t]
                if t == 0:
                    pe.wait_ge(wk_split, b * NKV + j + 3)
                if j % NKV == 0:
                    at = b + j // NKV
                    pe.wait_ge(ctx_hi_set, at * NT + t + 1)
                    if t < LO_DVE:
                        pe.wait_ge(ctx_lo_dve, at * LO_DVE + t + 1)
                    else:
                        pe.wait_ge(ctx_lo_pool, at * (NT - LO_DVE) + t + 1 - LO_DVE)
                pe.wait_ge(kv_free, b * KV_TILES + n + 1)
                for kc in range(KC):
                    end = product(nc, kv_ps[:, n % 2, 0:w],
                                  (wk_hi[:, j % 2, kc], wk_lo[:, j % 2, kc]),
                                  (ctx_hi[:, kc, c:c + w], ctx_lo[:, kc, c:c + w]), kc == 0, kc == KC - 1)
                end.then_inc(kv_full, 1)

            def value_tile(b, j, g, n):
                if g == 0:
                    pe.wait_ge(wv_split, b * (NKV // 2) + j // 2 + 2)
                pe.wait_ge(kv_free, b * KV_TILES + n + 1)
                for c in range(2 * g, min(2 * g + 2, NC)):
                    for kc in range(KC):
                        s = slice(c * P, c * P + rows(c))
                        o = (c % 2) * 2 * D
                        end = product(nc, kv_ps[0:rows(c), n % 2, o:o + 2 * D],
                                      (ctx_hi[:, kc, s], ctx_lo[:, kc, s]),
                                      (wv_hi[:, kc, :], wv_lo[:, kc, :]), kc == 0, kc == KC - 1)
                end.then_inc(kv_full, 1)

            def project(b, j, last):
                for kind, at, t, n in projections(b, j, last):
                    (key_tile if kind == "k" else value_tile)(b, at, t, n)

            def score_tile(b, j, i):
                u, t = divmod(i, NT)
                c, w = TILES[t]
                n = j * NU * NT + i
                if i == 0:
                    pe.wait_ge(q_split, b * NKV + j + 3)
                if u == 0:
                    pe.wait_ge(kv_free, b * KV_TILES + kv_tile(j) + t + 3)
                pe.wait_ge(s_free, b * S_TILES + n + 1)
                us = slice(u * P, (u + 1) * P)
                product(nc, s_ps[:, n % 2, 0:w], (q_hi[:, j % 2, us], q_lo[:, j % 2, us]),
                        (k_hi[:, c:c + w], k_lo[:, c:c + w]), True, True).then_inc(s_full, 1)

            def transposes(b, j, g):
                n = j * NG + g
                if g == 0:
                    pe.wait_ge(prob_set, b * (NKV * NU) + j * NU + NU)
                pe.wait_ge(t_free, b * PAIRS + n + 1)
                for c in range(2 * g, min(2 * g + 2, NC)):
                    r = rows(c)
                    for u in range(NU):
                        o = (c % 2) * NQ + u * P
                        end = nc.tensor.transpose(t_ps[0:r, n % 2, o:o + P],
                                                  prob[:, j % 2, u, c * P:c * P + r], ident[:, :])
                end.then_inc(t_full, 1)

            def pv(b, j, g):
                n = j * NG + g
                if g == 0:
                    pe.wait_ge(o_free, b * NKV + j + 1)
                pe.wait_ge(t_free, b * PAIRS + n + 3)
                for c in range(2 * g, min(2 * g + 2, NC)):
                    r = rows(c)
                    d = slice((j % 2) * D, (j % 2 + 1) * D)
                    end = product(nc, o_ps[:, j % 2, 0:NQ], (v_hi[0:r, c, d], v_lo[0:r, c, d]),
                                  (pt_hi[0:r, n % NPT, c % 2], pt_lo[0:r, n % NPT, c % 2]), c == 0, c == NC - 1)
                end.then_inc(pt_free, 1)

            def first():
                for t in range(NT):
                    key_tile(0, 0, t, t)
                for i in range(NU * NT):
                    score_tile(0, 0, i)
                project(0, 0, False)

            def group(b, j, last):
                for i in range(max(NU * NT, NG)):
                    if i < NU * NT:
                        score_tile(b, j, i)
                    if 2 <= i < NG + 2:
                        pv(b, j - 1, i - 2)
                    if i < NG:
                        transposes(b, j - 1, i)
                for g in range(max(NU * NT, NG) - 2, NG):
                    pv(b, j - 1, g)
                project(b, j, last)

            def tail(b):
                for i in range(NG + 1):
                    if i < NG:
                        transposes(b, NKV - 1, i)
                    if i > 0:
                        pv(b, NKV - 1, i - 1)

            drive(pe, first, group, tail)

        @block.scalar
        def _(act):
            def key_tile(b, j, t, n):
                c, w = TILES[t]
                act.wait_ge(kv_full, kv_done(b, n + 1))
                nc.scalar.activation(k_hi[:, c:c + w], kv_ps[:, n % 2, 0:w], ACT.Identity,
                                     bias=bk_sb[:, j % NKV:j % NKV + 1]).then_inc(kv_hi, 1)

            def value_tile(b, j, g, n):
                act.wait_ge(kv_full, kv_done(b, n + 1))
                m = min(2, NC - 2 * g)
                r = rows(2 * g)
                nc.scalar.activation(v_hi[0:r, 2 * g:2 * g + m, :],
                                     kv_ps[0:r, n % 2, 0:m * 2 * D].rearrange("p (c d) -> p c d", c=m),
                                     ACT.Copy).then_inc(kv_hi, 1)

            def exponentials(b, j, u):
                act.wait_ge(nmax_set, b * (NKV * NU) + j * NU + u + 1)
                nc.scalar.activation(prob[:, j % 2, u, 0:S], prob[:, j % 2, u, 0:S], ACT.Exp, bias=nmax[:, u:u + 1],
                                     accum_out=den[:, u:u + 1]).then_inc(exp_done, 1)

            def softmax_and_project(b, j, last):
                exponentials(b, j, 0)
                tiles = projections(b, j, last)
                for i, (kind, at, t, n) in enumerate(tiles):
                    (key_tile if kind == "k" else value_tile)(b, at, t, n)
                    if 0 <= i < NU - 1:
                        exponentials(b, j, i + 1)
                if not tiles:
                    for u in range(1, NU):
                        exponentials(b, j, u)

            def attend(b, j):
                for g in range(NG):
                    n = j * NG + g
                    m = min(2, NC - 2 * g)
                    r = rows(2 * g)
                    act.wait_ge(t_full, b * PAIRS + n + 1)
                    act.wait_ge(pt_free, b * PAIRS + n + 1)
                    nc.scalar.activation(pt_hi[0:r, n % NPT, 0:m, :],
                                         t_ps[0:r, n % 2, 0:m * NQ].rearrange("p (c d) -> p c d", c=m),
                                         ACT.Copy).then_inc(t_hi, 1)
                act.wait_ge(pt_free, b * PAIRS + (j + 1) * NG + NPT)
                act.wait_ge(o_out[j % 2], (b * (NKV // 2) + j // 2 + 1) * 16)
                nc.scalar.activation(o_sb[:, j % 2], o_ps[:, j % 2, 0:NQ], ACT.Identity,
                                     bias=bv_sb[:, j:j + 1]).then_inc(o_free, 1)
                act.wait_ge(o_free, b * NKV + j + 3)
                act.dma_start(o_dram[b, j], o_sb[:, j % 2]).then_inc(o_out[j % 2], 16)

            def first():
                act.sem_inc(o_free, 2)
                act.sem_inc(o_out[0], 16)
                act.sem_inc(o_out[1], 16)
                act.wait_ge(bias_in, 32)
                for t in range(NT):
                    key_tile(0, 0, t, t)
                softmax_and_project(0, 0, False)

            def group(b, j, last):
                attend(b, j - 1)
                softmax_and_project(b, j, last)

            drive(act, first, group, lambda b: attend(b, NKV - 1))
            for i in range(2):
                act.wait_ge(o_out[i], (B * NKV // 2 + 1) * 16)

        @block.vector
        def _(dve):
            def split_ctx(b, t, kc):
                c, w = TILES[t]
                dve.wait_ge(ctx_hi_set, b * NT + t + 1)
                end = nc.vector.tensor_tensor(ctx_lo[:, kc, c:c + w], raw[:, kc, c:c + w],
                                              ctx_hi[:, kc, c:c + w].bitcast(F32), ALU.subtract)
                if kc == KC - 1:
                    end.then_inc(ctx_lo_dve, 1)

            def key_tile(b, j, t, n):
                c, w = TILES[t]
                dve.wait_ge(kv_hi, b * KV_TILES + n + 1)
                nc.vector.scalar_tensor_tensor(
                    out=k_lo[:, c:c + w], in0=kv_ps[:, n % 2, 0:w], scalar=bk_sb[:, j % NKV:j % NKV + 1],
                    in1=k_hi[:, c:c + w].bitcast(F32), op0=ALU.add, op1=ALU.subtract).then_inc(kv_free, 1)

            def value_tile(b, j, g, n):
                m = min(2, NC - 2 * g)
                r = rows(2 * g)
                dve.wait_ge(kv_hi, b * KV_TILES + n + 1)
                nc.vector.tensor_tensor(v_lo[0:r, 2 * g:2 * g + m, :],
                                        kv_ps[0:r, n % 2, 0:m * 2 * D].rearrange("p (c d) -> p c d", c=m),
                                        v_hi[0:r, 2 * g:2 * g + m, :].bitcast(F32),
                                        ALU.subtract).then_inc(kv_free, 1)

            def score_tile(b, j, i):
                u, t = divmod(i, NT)
                c, w = TILES[t]
                w = min(w, S - c)
                n = j * NU * NT + i
                dve.wait_ge(s_full, b * S_TILES + n + 1 + S_TILES)
                nc.vector.tensor_scalar(prob[:, j % 2, u, c:c + w], s_ps[:, n % 2, 0:w], SCALE, None,
                                        ALU.mult, ALU.max,
                                        accum_out=tmax[:, u, t:t + 1]).then_inc(s_free, 1)
                if t == NT - 1:
                    dve.wait_ge(s_free, b * S_TILES + (j * NU + u + 1) * NT + 2)
                    nc.vector.tensor_reduce(nmax[:, u:u + 1], tmax[:, u, :], AX_X, ALU.max,
                                            negate=True).then_inc(nmax_set, 1)

            def normalise(b, j, u):
                n = b * (NKV * NU) + j * NU + u + 1
                dve.wait_ge(exp_done, n)
                nc.vector.reciprocal(rden[:, u:u + 1], den[:, u:u + 1]).then_inc(rden_set, 1)
                dve.wait_ge(rden_set, n)
                nc.vector.tensor_scalar(prob[:, j % 2, u, 0:S], prob[:, j % 2, u, 0:S], rden[:, u:u + 1], None,
                                        ALU.mult).then_inc(prob_set, 1)

            def low_transposed(b, j, g):
                n = j * NG + g
                m = min(2, NC - 2 * g)
                r = rows(2 * g)
                dve.wait_ge(t_hi, b * PAIRS + n + 1)
                nc.vector.tensor_tensor(pt_lo[0:r, n % NPT, 0:m, :],
                                        t_ps[0:r, n % 2, 0:m * NQ].rearrange("p (c d) -> p c d", c=m),
                                        pt_hi[0:r, n % NPT, 0:m, :].bitcast(F32),
                                        ALU.subtract).then_inc(t_free, 1)

            def softmax_and_project(b, j, last):
                normalise(b, j, 0)
                tiles = projections(b, j, last)
                for i, (kind, at, t, n) in enumerate(tiles):
                    (key_tile if kind == "k" else value_tile)(b, at, t, n)
                    if 1 <= i < NU:
                        normalise(b, j, i)
                if not tiles:
                    for u in range(1, NU):
                        normalise(b, j, u)

            def first():
                dve.sem_inc(kv_free, 2)
                dve.sem_inc(s_free, 2)
                dve.sem_inc(t_free, 2)
                for t in range(LO_DVE):
                    for kc in range(KC):
                        split_ctx(0, t, kc)
                dve.wait_ge(bias_in, 32)
                for t in range(NT):
                    key_tile(0, 0, t, t)
                for i in range(NU * NT):
                    score_tile(0, 0, i)
                softmax_and_project(0, 0, False)

            def group(b, j, last):
                ctx_steps = [(t, kc) for t in range(LO_DVE) for kc in range(KC)]
                for i in range(max(NU * NT, NG)):
                    if i < NU * NT:
                        score_tile(b, j, i)
                    if i < NG:
                        low_transposed(b, j - 1, i)
                    if j == NKV - 1 and not last and i % 2 == 1 and ctx_steps:
                        split_ctx(b + 1, *ctx_steps.pop(0))
                if j == NKV - 1 and not last:
                    for t, kc in ctx_steps:
                        split_ctx(b + 1, t, kc)
                softmax_and_project(b, j, last)

            def tail(b):
                for g in range(NG):
                    low_transposed(b, NKV - 1, g)

            drive(dve, first, group, tail)


class Chain:

    def __init__(self, eng, sem, start=0):
        self.eng, self.sem, self.count = eng, sem, start

    def __call__(self, ins):
        self.count += 1
        ins.then_inc(self.sem, 1)
        self.eng.wait_ge(self.sem, self.count)


def layernorm_transposed(nc, name, x_sb, xt_hi, xt_lo, ident, eps=1e-5):
    _, RT, H = x_sb.shape
    KC = H // P
    with Scope(nc, name) as sc:
        xn = sc.sb("xn", [P, RT, H])
        stats = sc.sb("stats", [P, RT, 6])
        mv = sc.sb("mv", [P, RT, 2])
        std = sc.sb("std", [P, RT])
        rstd = sc.sb("rstd", [P, RT])
        eps_sb = sc.sb("eps", [P, 1])
        t_ps = sc.ps("t_ps", [P, RT, 512])
        own, var_set, std_set, xn_set, t_full, hi_set = (
            sc.sem(n) for n in ("own", "var_set", "std_set", "xn_set", "t_full", "hi_set"))
        block = sc.block()

        @block.vector
        def _(dve):
            step = Chain(dve, own)
            nc.vector.memset(eps_sb[:, :], eps).then_inc(own, 1)
            step.count = 1
            for r in range(RT):
                step(nc.vector.bn_stats(stats[:, r, :], x_sb[:, r, :]))
                nc.vector.bn_aggr(mv[:, r, :], stats[:, r, :]).then_inc(var_set, 1)
            for r in range(RT):
                dve.wait_ge(std_set, r + 1)
                step(nc.vector.reciprocal(rstd[:, r:r + 1], std[:, r:r + 1]))
                nc.vector.tensor_scalar(xn[:, r, :], x_sb[:, r, :], mv[:, r, 0:1], rstd[:, r:r + 1],
                                        ALU.subtract, ALU.mult).then_inc(xn_set, 1)
            for r in range(RT):
                dve.wait_ge(hi_set, r + 1)
                out = xt_lo[:, :, r * P:(r + 1) * P]
                nc.vector.tensor_tensor(out, t_ps[:, r, :].rearrange("p (k c) -> p k c", k=KC),
                                        xt_hi[:, :, r * P:(r + 1) * P].bitcast(F32), ALU.subtract)

        @block.scalar
        def _(act):
            for r in range(RT):
                act.wait_ge(var_set, r + 1)
                nc.scalar.activation(std[:, r:r + 1], mv[:, r, 1:2], ACT.Sqrt, bias=eps_sb[:, 0:1]).then_inc(std_set, 1)
            for r in range(RT):
                act.wait_ge(t_full, r + 1)
                nc.scalar.activation(xt_hi[:, :, r * P:(r + 1) * P],
                                     t_ps[:, r, :].rearrange("p (k c) -> p k c", k=KC),
                                     ACT.Copy).then_inc(hi_set, 1)

        @block.tensor
        def _(pe):
            for r in range(RT):
                pe.wait_ge(xn_set, r + 1)
                for k in range(KC):
                    end = nc.tensor.transpose(t_ps[:, r, k * P:(k + 1) * P], xn[:, r, k * P:(k + 1) * P], ident[:, :])
                end.then_inc(t_full, 1)


def queries(nc, xt_hi, xt_lo, wq, bq, q_dram):
    NKV, _, KC, GD = wq.shape
    D = P
    G = GD // D
    B = q_dram.shape[0]
    R = xt_hi.shape[2]
    with Scope(nc, "q") as sc:
        raw = sc.sb("raw", [P, 2, KC, GD])
        w_hi, w_lo = sc.sb("w_hi", [P, 2, KC, GD], F32R), sc.sb("w_lo", [P, 2, KC, GD], F32R)
        bq_sb = sc.sb("bq_sb", [P, NKV * G])
        q_sb = sc.sb("q_sb", [P, 2, B, G, R // B])
        q_ps = sc.ps("q_ps", [P, 4, 512])
        bias_in = sc.sem("bias_in")
        w_in = [sc.sem(f"w_in{i}") for i in range(2)]
        w_hi_set, w_lo_set = sc.sem("w_hi_set"), sc.sem("w_lo_set")
        q_full, q_set = sc.sem("q_full"), sc.sem("q_set")
        q_out = [sc.sem(f"q_out{i}") for i in range(2)]
        block = sc.block()

        @block.sync
        def _(sp):
            sp.dma_start(bq_sb[:, :], bq).then_inc(bias_in, 16)
            with sp.Fori(0, NKV // 2) as h:
                j0 = 2 * h
                for i in range(2):
                    sp.wait_ge(w_lo_set, j0 + i + 1)
                    sp.dma_start(raw[:, i], wq[j0 + i]).then_inc(w_in[i], 16)

        def evacuate(act, j0, i):
            act.wait_ge(q_out[i], (j0 + 2) * 8)
            for g in range(G):
                n = (j0 + i) * G + g
                act.wait_ge(q_full, n + 1 + 2 * G)
                nc.scalar.activation(q_sb[:, i, :, g, :], q_ps[:, g, :].rearrange("p (b l) -> p b l", b=B),
                                     ACT.Identity, bias=bq_sb[:, bass.ds(n, 1)]).then_inc(q_set, 1)
            act.wait_ge(q_set, (j0 + i + 1) * G + G)
            act.dma_start(q_dram[:, j0 + i].rearrange("b d n -> d b n"),
                          q_sb[:, i].rearrange("p b g l -> p b (g l)")).then_inc(q_out[i], 16)

        @block.scalar
        def _(act):
            act.sem_inc(q_out[0], 16)
            act.sem_inc(q_out[1], 16)
            act.wait_ge(bias_in, 16)
            with act.Fori(0, NKV // 2) as h:
                j0 = 2 * h
                for i in range(2):
                    act.wait_ge(w_in[i], (j0 + 2) * 8)
                    act.wait_ge(q_full, (j0 + i + 1) * G)
                    nc.scalar.activation(w_hi[:, i], raw[:, i], ACT.Copy).then_inc(w_hi_set, 1)
                    if i == 1:
                        evacuate(act, j0, 0)
                evacuate(act, j0, 1)
            for i in range(2):
                act.wait_ge(q_out[i], (NKV // 2 + 1) * 16)

        @block.vector
        def _(dve):
            dve.sem_inc(w_lo_set, 2)
            with dve.Fori(0, NKV // 2) as h:
                j0 = 2 * h
                for i in range(2):
                    dve.wait_ge(w_hi_set, j0 + i + 1)
                    nc.vector.tensor_tensor(w_lo[:, i], raw[:, i], w_hi[:, i].bitcast(F32),
                                            ALU.subtract).then_inc(w_lo_set, 1)

        @block.tensor
        def _(pe):
            pe.sem_inc(q_full, 2 * G)
            pe.sem_inc(q_set, G)
            with pe.Fori(0, NKV // 2) as h:
                j0 = 2 * h
                for i in range(2):
                    pe.wait_ge(w_lo_set, j0 + i + 3)
                    for g in range(G):
                        pe.wait_ge(q_set, (j0 + i) * G + g + 1)
                        for k in range(KC):
                            end = product(nc, q_ps[:, g, :],
                                          (w_hi[:, i, k, g * D:(g + 1) * D], w_lo[:, i, k, g * D:(g + 1) * D]),
                                          (xt_hi[:, k, :], xt_lo[:, k, :]), k == 0, k == KC - 1)
                        end.then_inc(q_full, 1)


def attention_output(nc, x_sb, o_dram, wo, bo):
    B, NKV, D, GL = o_dram.shape
    G, H = wo.shape[2:]
    L = GL // G
    RT = B * L // P
    with Scope(nc, "wo") as sc:
        o_raw, w_raw = sc.sb("o_raw", [P, 2, B, GL]), sc.sb("w_raw", [P, 2, G, H])
        o_hi, o_lo = sc.sb("o_hi", [P, 2, G, B * L], F32R), sc.sb("o_lo", [P, 2, G, B * L], F32R)
        w_hi, w_lo = sc.sb("w_hi", [P, 2, G, H], F32R), sc.sb("w_lo", [P, 2, G, H], F32R)
        bo_sb = sc.sb("bo_sb", [P, H])
        ps = sc.ps("ps", [P, RT, 512])
        bias_in = sc.sem("bias_in")
        a_in = [sc.sem(f"a_in{i}") for i in range(2)]
        hi_set, lo_set, used, done, x_set = (sc.sem(n) for n in ("hi_set", "lo_set", "used", "done", "x_set"))
        block = sc.block()

        def spread(i):
            return o_raw[:, i].rearrange("p b (g l) -> p g b l", g=G)

        def heads(t, i):
            return t[:, i].rearrange("p g (b l) -> p g b l", b=B)

        @block.sync
        def _(sp):
            sp.dma_start(bo_sb[:, :], bo.rearrange("(a n) -> a n", a=1).broadcast_to([P, H])).then_inc(bias_in, 16)
            with sp.Fori(0, NKV // 2) as h:
                j0 = 2 * h
                for i in range(2):
                    sp.wait_ge(lo_set, (j0 + i) * 2 + 2)
                    sp.dma_start(o_raw[:, i], o_dram[:, j0 + i].rearrange("b d n -> d b n")).then_inc(a_in[i], 16)
                    sp.dma_start(w_raw[:, i], wo[j0 + i]).then_inc(a_in[i], 16)

        @block.scalar
        def _(act):
            with act.Fori(0, NKV // 2) as h:
                j0 = 2 * h
                for i in range(2):
                    act.wait_ge(a_in[i], (j0 + 2) * 16)
                    act.wait_ge(used, j0 + i + 1)
                    for g in range(G):
                        nc.scalar.activation(heads(o_hi, i)[:, g], spread(i)[:, g], ACT.Copy)
                    nc.scalar.activation(w_hi[:, i], w_raw[:, i], ACT.Copy).then_inc(hi_set, 1)

        @block.vector
        def _(dve):
            dve.sem_inc(lo_set, 4)
            with dve.Fori(0, NKV // 2) as h:
                j0 = 2 * h
                for i in range(2):
                    dve.wait_ge(hi_set, j0 + i + 1)
                    for g in range(G):
                        end = nc.vector.tensor_tensor(heads(o_lo, i)[:, g], spread(i)[:, g],
                                                      heads(o_hi, i)[:, g].bitcast(F32), ALU.subtract)
                    end.then_inc(lo_set, 1)
                    nc.vector.tensor_tensor(w_lo[:, i], w_raw[:, i], w_hi[:, i].bitcast(F32),
                                            ALU.subtract).then_inc(lo_set, 1)
            dve.wait_ge(bias_in, 16)
            for r in range(RT):
                nc.vector.tensor_tensor(x_sb[:, r, :], x_sb[:, r, :], bo_sb[:, :], ALU.add).then_inc(x_set, 1)
            for r in range(RT):
                dve.wait_ge(done, r + 1)
                dve.wait_ge(x_set, r + 1)
                nc.vector.tensor_tensor(x_sb[:, r, :], ps[:, r, :], x_sb[:, r, :], ALU.add)

        @block.tensor
        def _(pe):
            pe.sem_inc(used, 2)

            def pair(j0, first, last):
                for i in range(2):
                    pe.wait_ge(lo_set, (j0 + i) * 2 + 6)
                    for g in range(G):
                        for r in range(RT):
                            rs = slice(r * P, (r + 1) * P)
                            end_of_all = last and i == 1 and g == G - 1
                            end = product(nc, ps[:, r, :], (o_hi[:, i, g, rs], o_lo[:, i, g, rs]),
                                          (w_hi[:, i, g, :], w_lo[:, i, g, :]),
                                          first and i == 0 and g == 0, end_of_all)
                            if end_of_all:
                                end.then_inc(done, 1)
                            elif g == G - 1 and r == RT - 1:
                                end.then_inc(used, 1)

            pair(0, True, False)
            with pe.Fori(1, NKV // 2 - 1) as h:
                pair(2 * h, False, False)
            pair(NKV - 2, False, True)


def mamba_project(nc, xt_hi, xt_lo, w_in, conv_w, conv_b, w_x, u_sb, gate_sb, ssm_sb, B):
    DC, _, _, KC, _ = w_in.shape
    K = conv_w.shape[2]
    N = w_x.shape[2]
    R = xt_hi.shape[2]
    RT = R // P
    L = R // B
    with Scope(nc, "mp") as sc:
        raw = sc.sb("raw", [P, 2, 2, KC, P])
        w_hi, w_lo = sc.sb("w_hi", [P, 2, 2, KC, P], F32R), sc.sb("w_lo", [P, 2, 2, KC, P], F32R)
        cw, cb = sc.sb("cw", [P, DC, K]), sc.sb("cb", [P, DC])
        wx_raw = sc.sb("wx_raw", [P, DC, N])
        wx_hi, wx_lo = sc.sb("wx_hi", [P, DC, N], F32R), sc.sb("wx_lo", [P, DC, N], F32R)
        xpad = sc.sb("xpad", [P, 2, B, L + K - 1])
        xc = sc.sb("xc", [P, 2, B, L])
        u_hi, u_lo = sc.sb("u_hi", [P, 2, R], F32R), sc.sb("u_lo", [P, 2, R], F32R)
        xg_ps = sc.ps("xg_ps", [P, 4, 512])
        ssm_ps = sc.ps("ssm_ps", [P, RT, 512])
        small_in = sc.sem("small_in")
        w_in_s = [sc.sem(f"w_in{i}") for i in range(2)]
        pad_set, wx_hi_set, wx_set, w_hi_set, w_lo_set = (
            sc.sem(n) for n in ("pad_set", "wx_hi_set", "wx_set", "w_hi_set", "w_lo_set"))
        xg_full, x_read, gate_read, conv, xc_set, u_set, u_hi_set, u_lo_set, ssm_full = (
            sc.sem(n) for n in ("xg_full", "x_read", "gate_read", "conv", "xc_set", "u_set", "u_hi_set", "u_lo_set",
                                "ssm_full"))
        block = sc.block()

        @block.sync
        def _(sp):
            sp.dma_start(cw[:, :, :], conv_w).then_inc(small_in, 16)
            sp.dma_start(cb[:, :], conv_b).then_inc(small_in, 16)
            sp.dma_start(wx_raw[:, :, :], w_x).then_inc(small_in, 16)
            for c in range(DC):
                if c >= 2:
                    sp.wait_ge(w_lo_set, c - 1)
                sp.dma_start(raw[:, c % 2], w_in[c]).then_inc(w_in_s[c % 2], 16)

        @block.gpsimd
        def _(pool):
            nc.gpsimd.memset(xpad[:, :, :, 0:K - 1], 0.0).then_inc(pad_set, 1)
            pool.wait_ge(small_in, 48)
            nc.gpsimd.tensor_scalar(wx_hi[:, :, :], wx_raw[:, :, :], 1.0, 1.0, ALU.mult, ALU.mult).then_inc(wx_hi_set, 1)
            pool.wait_ge(wx_hi_set, 1)
            nc.gpsimd.tensor_tensor(wx_lo[:, :, :], wx_raw[:, :, :], wx_hi[:, :, :].bitcast(F32),
                                    ALU.subtract).then_inc(wx_set, 1)

        @block.tensor
        def _(pe):
            def ssm(c):
                pe.wait_ge(u_lo_set, c + 1)
                if c == 0:
                    pe.wait_ge(wx_set, 1)
                for r in range(RT):
                    rs = slice(r * P, (r + 1) * P)
                    end = product(nc, ssm_ps[:, r, 0:N], (u_hi[:, c % 2, rs], u_lo[:, c % 2, rs]),
                                  (wx_hi[:, c, :], wx_lo[:, c, :]), c == 0, c == DC - 1)
                end.then_inc(ssm_full, 1)

            for c in range(DC):
                pe.wait_ge(w_lo_set, c + 1)
                for part in range(2):
                    if c >= 2:
                        pe.wait_ge((x_read, gate_read)[part], c - 1)
                    for k in range(KC):
                        end = product(nc, xg_ps[:, 2 * (c % 2) + part, :],
                                      (w_hi[:, c % 2, part, k], w_lo[:, c % 2, part, k]),
                                      (xt_hi[:, k, :], xt_lo[:, k, :]), k == 0, k == KC - 1)
                    end.then_inc(xg_full, 1)
                if c > 0:
                    ssm(c - 1)
            ssm(DC - 1)

        @block.scalar
        def _(act):
            def weights(c):
                act.wait_ge(w_in_s[c % 2], (c // 2 + 1) * 16)
                if c >= 2:
                    act.wait_ge(xg_full, 2 * (c - 1))
                nc.scalar.activation(w_hi[:, c % 2], raw[:, c % 2], ACT.Copy).then_inc(w_hi_set, 1)

            def silu(c):
                act.wait_ge(xc_set, c + 1)
                nc.scalar.activation(u_sb[:, c, :], xc[:, c % 2].rearrange("p b l -> p (b l)"),
                                     ACT.Silu).then_inc(u_set, 1)
                if c >= 2:
                    act.wait_ge(ssm_full, c - 1)
                act.wait_ge(u_set, c + 1)
                nc.scalar.activation(u_hi[:, c % 2], u_sb[:, c, :], ACT.Copy).then_inc(u_hi_set, 1)

            act.wait_ge(pad_set, 1)
            weights(0)
            for c in range(DC):
                if c + 1 < DC:
                    weights(c + 1)
                act.wait_ge(xg_full, 2 * c + 1)
                if c >= 2:
                    act.wait_ge(xc_set, c - 1)
                nc.scalar.activation(xpad[:, c % 2, :, K - 1:], xg_ps[:, 2 * (c % 2), :].rearrange("p (b l) -> p b l", b=B),
                                     ACT.Copy).then_inc(x_read, 1)
                act.wait_ge(xg_full, 2 * c + 2)
                nc.scalar.activation(gate_sb[:, c, :], xg_ps[:, 2 * (c % 2) + 1, :], ACT.Silu).then_inc(gate_read, 1)
                if c > 0:
                    silu(c - 1)
            silu(DC - 1)

        @block.vector
        def _(dve):
            step = Chain(dve, conv)

            def u_low(c):
                dve.wait_ge(u_hi_set, c + 1)
                nc.vector.tensor_tensor(u_lo[:, c % 2], u_sb[:, c, :], u_hi[:, c % 2].bitcast(F32),
                                        ALU.subtract).then_inc(u_lo_set, 1)

            dve.wait_ge(small_in, 48)
            for c in range(DC + 1):
                if c < DC:
                    dve.wait_ge(w_hi_set, c + 1)
                    nc.vector.tensor_tensor(w_lo[:, c % 2], raw[:, c % 2], w_hi[:, c % 2].bitcast(F32),
                                            ALU.subtract).then_inc(w_lo_set, 1)
                if c > 1:
                    u_low(c - 2)
                if c > 0:
                    a = c - 1
                    s = a % 2
                    dve.wait_ge(x_read, a + 1)
                    if a >= 2:
                        dve.wait_ge(u_set, a - 1)
                    step(nc.vector.tensor_scalar(xc[:, s], xpad[:, s, :, 0:L], cw[:, a, 0:1], cb[:, a:a + 1],
                                                 ALU.mult, ALU.add))
                    for j in range(1, K):
                        ins = nc.vector.scalar_tensor_tensor(out=xc[:, s], in0=xpad[:, s, :, j:j + L],
                                                             scalar=cw[:, a, j:j + 1], in1=xc[:, s],
                                                             op0=ALU.mult, op1=ALU.add)
                        if j < K - 1:
                            step(ins)
                        else:
                            ins.then_inc(xc_set, 1)
            u_low(DC - 1)
            dve.wait_ge(ssm_full, DC)
            for r in range(RT):
                nc.vector.tensor_copy(ssm_sb[:, r, :], ssm_ps[:, r, 0:N])


def mamba_parameters(nc, ssm_sb, w_dt, b_dt, ident, b_all, c_all, dt_sb, work, eps=1e-6):
    _, RT, N = ssm_sb.shape
    NS, DC, R = b_all.shape[1], dt_sb.shape[1], dt_sb.shape[2]
    RANK = N - 2 * NS
    with Scope(nc, "mr") as sc:
        sq = sc.sb("sq", [P, RT, N])
        ms = sc.sb("ms", [P, RT, 3])
        eps_sb = sc.sb("eps", [P, 1])
        nrm = sc.sb("nrm", [P, RT, N])
        n_hi, n_lo = sc.sb("n_hi", [N, R], F32R), sc.sb("n_lo", [N, R], F32R)
        sel = sc.sb("sel", [N, 2 * NS, P], F32R)
        wd_raw = sc.sb("wd_raw", [RANK, DC * P])
        wd_hi, wd_lo = sc.sb("wd_hi", [RANK, DC * P], F32R), sc.sb("wd_lo", [RANK, DC * P], F32R)
        bd = sc.sb("bd", [P, DC])
        t_ps = sc.ps("t_ps", [P, 512])
        bc_ps = sc.ps("bc_ps", [P, 4, 512])
        d_ps = sc.ps("d_ps", [P, 2, 512])
        small_in, own, ms_set, std_set, nrm_set, t_full, n_hi_set, n_lo_set, wd_hi_set, wd_set, sel_set = (
            sc.sem(n) for n in ("small_in", "own", "ms_set", "std_set", "nrm_set", "t_full", "n_hi_set", "n_lo_set",
                                "wd_hi_set", "wd_set", "sel_set"))
        bc_full, bc_even, bc_odd, d_full, d_abs, d_read, e_set, ln_set = (
            sc.sem(n) for n in ("bc_full", "bc_even", "bc_odd", "d_full", "d_abs", "d_read", "e_set", "ln_set"))
        block = sc.block()
        segments = [(0, RANK), (RANK, NS), (RANK + NS, NS)]

        @block.sync
        def _(sp):
            sp.dma_start(wd_raw[:, :], w_dt).then_inc(small_in, 16)
            sp.dma_start(bd[:, :], b_dt).then_inc(small_in, 16)

        @block.gpsimd
        def _(pool):
            nc.gpsimd.tensor_copy(sel[:, :, :], ident[0:N, RANK:N].unsqueeze(2).broadcast_to([N, 2 * NS, P])
                                  ).then_inc(sel_set, 1)
            pool.wait_ge(small_in, 32)
            nc.gpsimd.tensor_scalar(wd_hi[:, :], wd_raw[:, :], 1.0, 1.0, ALU.mult, ALU.mult).then_inc(wd_hi_set, 1)
            pool.wait_ge(wd_hi_set, 1)
            nc.gpsimd.tensor_tensor(wd_lo[:, :], wd_raw[:, :], wd_hi[:, :].bitcast(F32), ALU.subtract).then_inc(wd_set, 1)

        @block.vector
        def _(dve):
            step = Chain(dve, own)
            step(nc.vector.memset(eps_sb[:, :], eps))
            step(nc.vector.tensor_tensor(sq[:, :, :], ssm_sb[:, :, :], ssm_sb[:, :, :], ALU.mult))
            for i, (a, n) in enumerate(segments):
                step(nc.vector.tensor_reduce(ms[:, :, i:i + 1], sq[:, :, a:a + n], AX_X, ALU.add))
                nc.vector.tensor_scalar(ms[:, :, i], ms[:, :, i], 1.0 / n, None, ALU.mult).then_inc(ms_set, 1)
            dve.wait_ge(std_set, 1)
            step(nc.vector.reciprocal(ms[:, :, :], ms[:, :, :]))
            for i, (a, n) in enumerate(segments):
                nc.vector.tensor_tensor(nrm[:, :, a:a + n], ssm_sb[:, :, a:a + n],
                                        ms[:, :, i:i + 1].broadcast_to([P, RT, n]), ALU.mult).then_inc(nrm_set, 1)
            dve.wait_ge(n_hi_set, 1)
            nc.vector.tensor_tensor(n_lo[:, :], t_ps[0:N, :], n_hi[:, :].bitcast(F32), ALU.subtract).then_inc(n_lo_set, 1)
            for c in range(DC):
                dve.wait_ge(d_abs, c + 1)
                nc.vector.tensor_scalar(work[:, c, :], d_ps[:, c % 2, :], bd[:, c:c + 1], 0.0,
                                        ALU.add, ALU.max).then_inc(d_read, 1)
            for i in range(1, 2 * NS, 2):
                dve.wait_ge(bc_full, i + 1)
                nc.vector.tensor_copy((b_all, c_all)[i // NS][:, i % NS, :], bc_ps[:, i % 4, :]).then_inc(bc_odd, 1)
            dve.wait_ge(ln_set, 1)
            nc.vector.tensor_tensor(dt_sb[:, :, :], dt_sb[:, :, :], work[:, :, :], ALU.add)

        @block.tensor
        def _(pe):
            pe.wait_ge(nrm_set, 3)
            for r in range(RT):
                end = nc.tensor.transpose(t_ps[0:N, r * P:(r + 1) * P], nrm[:, r, :], ident[:, :])
            end.then_inc(t_full, 1)
            pe.wait_ge(n_lo_set, 1)
            pe.wait_ge(wd_set, 1)
            for c in range(DC):
                if c >= 2:
                    pe.wait_ge(d_read, c - 1)
                cs = slice(c * P, (c + 1) * P)
                product(nc, d_ps[:, c % 2, :], (wd_hi[:, cs], wd_lo[:, cs]), (n_hi[0:RANK, :], n_lo[0:RANK, :]),
                        True, True).then_inc(d_full, 1)
            pe.wait_ge(sel_set, 1)
            for i in range(2 * NS):
                if i >= 4:
                    pe.wait_ge((bc_even, bc_odd)[i % 2], i // 2 - 1)
                nc.tensor.matmul(bc_ps[:, i % 4, :], sel[:, i, :], n_hi[:, :], start=True, stop=False)
                nc.tensor.matmul(bc_ps[:, i % 4, :], sel[:, i, :], n_lo[:, :], start=False, stop=True).then_inc(bc_full, 1)

        @block.scalar
        def _(act):
            act.wait_ge(ms_set, 3)
            nc.scalar.activation(ms[:, :, :], ms[:, :, :], ACT.Sqrt, bias=eps_sb[:, 0:1]).then_inc(std_set, 1)
            act.wait_ge(t_full, 1)
            nc.scalar.activation(n_hi[:, :], t_ps[0:N, :], ACT.Copy).then_inc(n_hi_set, 1)
            act.wait_ge(small_in, 32)
            for c in range(DC):
                act.wait_ge(d_full, c + 1)
                nc.scalar.activation(dt_sb[:, c, :], d_ps[:, c % 2, :], ACT.Abs, bias=bd[:, c:c + 1]).then_inc(d_abs, 1)
            for i in range(0, 2 * NS, 2):
                act.wait_ge(bc_full, i + 1)
                nc.scalar.activation((b_all, c_all)[i // NS][:, i % NS, :], bc_ps[:, i % 4, :], ACT.Copy).then_inc(bc_even, 1)
            act.wait_ge(d_abs, DC)
            nc.scalar.activation(dt_sb[:, :, :], dt_sb[:, :, :], ACT.Exp, scale=-1.0).then_inc(e_set, 1)
            act.wait_ge(e_set, 1)
            nc.scalar.activation(dt_sb[:, :, :], dt_sb[:, :, :], ACT.Ln, bias=1.0).then_inc(ln_set, 1)


def mamba_scan(nc, u_sb, gate_sb, b_all, c_all, dt_sb, d_a, d_bu, a_log, d_skip, ident):
    DC, R = dt_sb.shape[1:]
    NS = b_all.shape[1]
    HN = d_a.shape[2]
    NH = NS // HN
    B, L = d_a.shape[3:]
    with Scope(nc, "ms") as sc:
        a_sb, dk = sc.sb("a_sb", [P, DC, NS]), sc.sb("dk", [P, DC])
        dtu = sc.sb("dtu", [P, 2, R])
        y_ps = sc.ps("y_ps", [P, 2, 512])
        small_in, own, a_exp, a_set, dtu_set, da_set, dbu_set, h_set, hc_set, y_full, y_set = (
            sc.sem(n) for n in ("small_in", "own", "a_exp", "a_set", "dtu_set", "da_set", "dbu_set", "h_set", "hc_set",
                                "y_full", "y_set"))
        block = sc.block()

        def flat(t, s):
            return t[:, s].rearrange("p n b l -> p (n b l)")

        def by_state(t, s):
            return t[:, s].rearrange("p n b l -> p n (b l)")

        @block.sync
        def _(sp):
            sp.dma_start(a_sb[:, :, :], a_log).then_inc(small_in, 16)
            sp.dma_start(dk[:, :], d_skip).then_inc(small_in, 16)

        @block.scalar
        def _(act):
            act.wait_ge(small_in, 32)
            nc.scalar.activation(a_sb[:, :, :], a_sb[:, :, :], ACT.Exp).then_inc(a_exp, 1)
            act.wait_ge(a_set, 1)
            for i in range(DC * NH):
                c, h = divmod(i, NH)
                if i >= 2:
                    act.wait_ge(h_set, i - 1)
                for n in range(HN):
                    end = nc.scalar.activation(d_a[:, i % 2, n, :, 1:L],
                                               dt_sb[:, c, :].rearrange("p (b l) -> p b l", b=B)[:, :, 1:L],
                                               ACT.Exp, scale=a_sb[:, c, h * HN + n:h * HN + n + 1])
                end.then_inc(da_set, 1)

        @block.gpsimd
        def _(pool):
            for i in range(DC * NH):
                c, h = divmod(i, NH)
                pool.wait_ge(dtu_set, c + 1)
                if i >= 2:
                    pool.wait_ge(y_full, i - 1)
                nc.gpsimd.tensor_tensor(by_state(d_bu, i % 2), b_all[:, h * HN:(h + 1) * HN, :],
                                        dtu[:, c % 2, :].unsqueeze(1).broadcast_to([P, HN, R]),
                                        ALU.mult).then_inc(dbu_set, 1)

        @block.vector
        def _(dve):
            step = Chain(dve, own)
            nc.vector.memset(d_a[:, :, :, :, 0:1], 0.0).then_inc(own, 1)
            step.count = 1
            dve.wait_ge(a_exp, 1)
            nc.vector.tensor_scalar(a_sb[:, :, :], a_sb[:, :, :], -1.0, None, ALU.mult).then_inc(a_set, 1)

            def weigh(c):
                if c >= 2:
                    dve.wait_ge(dbu_set, NH * (c - 1))
                nc.vector.tensor_tensor(dtu[:, c % 2, :], dt_sb[:, c, :], u_sb[:, c, :], ALU.mult).then_inc(dtu_set, 1)

            def output(c):
                dve.wait_ge(y_full, NH * (c + 1))
                step(nc.vector.scalar_tensor_tensor(out=u_sb[:, c, :], in0=u_sb[:, c, :], scalar=dk[:, c:c + 1],
                                                    in1=y_ps[:, c % 2, :], op0=ALU.mult, op1=ALU.add))
                nc.vector.tensor_tensor(gate_sb[:, c, :], gate_sb[:, c, :], u_sb[:, c, :], ALU.mult).then_inc(y_set, 1)

            weigh(0)
            weigh(1)
            for i in range(DC * NH):
                c, h = divmod(i, NH)
                dve.wait_ge(da_set, i + 1)
                dve.wait_ge(dbu_set, i + 1)
                nc.vector.tensor_tensor_scan(flat(d_bu, i % 2), flat(d_a, i % 2), flat(d_bu, i % 2), 0.0,
                                             ALU.mult, ALU.add).then_inc(h_set, 1)
                if h == NH - 1 and c > 0:
                    output(c - 1)
                    if c + 1 < DC:
                        weigh(c + 1)
                dve.wait_ge(h_set, i + 1)
                nc.vector.tensor_tensor(by_state(d_bu, i % 2), by_state(d_bu, i % 2),
                                        c_all[:, h * HN:(h + 1) * HN, :], ALU.mult).then_inc(hc_set, 1)
            output(DC - 1)

        @block.tensor
        def _(pe):
            for i in range(DC * NH):
                c, h = divmod(i, NH)
                pe.wait_ge(hc_set, i + 1)
                if h == 0 and c >= 2:
                    pe.wait_ge(y_set, c - 1)
                for n in range(HN):
                    end = nc.tensor.matmul(y_ps[:, c % 2, :], ident[:, :], by_state(d_bu, i % 2)[:, n, :],
                                           start=h == 0 and n == 0, stop=h == NH - 1 and n == HN - 1)
                end.then_inc(y_full, 1)


def mamba_output(nc, x_sb, y_sb, w_out):
    DC, R = y_sb.shape[1:]
    H = w_out.shape[2]
    RT = R // P
    with Scope(nc, "mo") as sc:
        raw = sc.sb("raw", [P, DC, H])
        w_hi, w_lo = sc.sb("w_hi", [P, DC, H], F32R), sc.sb("w_lo", [P, DC, H], F32R)
        y_hi, y_lo = sc.sb("y_hi", [P, DC, R], F32R), sc.sb("y_lo", [P, DC, R], F32R)
        ps = sc.ps("ps", [P, RT, 512])
        w_in, hi_set, lo_set, done = (sc.sem(n) for n in ("w_in", "hi_set", "lo_set", "done"))
        block = sc.block()

        @block.sync
        def _(sp):
            sp.dma_start(raw[:, :, :], w_out).then_inc(w_in, 16)

        @block.scalar
        def _(act):
            for c in range(DC):
                nc.scalar.activation(y_hi[:, c, :], y_sb[:, c, :], ACT.Copy).then_inc(hi_set, 1)
                if c == 0:
                    act.wait_ge(w_in, 16)
                nc.scalar.activation(w_hi[:, c, :], raw[:, c, :], ACT.Copy).then_inc(hi_set, 1)

        @block.vector
        def _(dve):
            for c in range(DC):
                dve.wait_ge(hi_set, 2 * c + 2)
                nc.vector.tensor_tensor(y_lo[:, c, :], y_sb[:, c, :], y_hi[:, c, :].bitcast(F32), ALU.subtract)
                nc.vector.tensor_tensor(w_lo[:, c, :], raw[:, c, :], w_hi[:, c, :].bitcast(F32),
                                        ALU.subtract).then_inc(lo_set, 1)
            for r in range(RT):
                dve.wait_ge(done, r + 1)
                nc.vector.tensor_tensor(x_sb[:, r, :], ps[:, r, :], x_sb[:, r, :], ALU.add)

        @block.tensor
        def _(pe):
            for c in range(DC):
                pe.wait_ge(lo_set, c + 1)
                for r in range(RT):
                    rs = slice(r * P, (r + 1) * P)
                    end = product(nc, ps[:, r, :], (y_hi[:, c, rs], y_lo[:, c, rs]), (w_hi[:, c, :], w_lo[:, c, :]),
                                  c == 0, c == DC - 1)
                    if c == DC - 1:
                        end.then_inc(done, 1)


def mamba(nc, x_sb, ident, B, w_in, conv_w, conv_b, w_x, w_dt, b_dt, a_log, d_skip, w_out):
    RT = x_sb.shape[1]
    H = x_sb.shape[2]
    R = RT * P
    DC = w_in.shape[0]
    NS = a_log.shape[2]
    with Scope(nc, "mamba") as sc:
        u_sb, gate_sb = sc.sb("u", [P, DC, R]), sc.sb("gate", [P, DC, R])
        with Scope(nc, "mamba_a") as sc1:
            ssm_sb = sc1.sb("ssm", [P, RT, w_x.shape[2]])
            with Scope(nc, "mamba_x") as sc2:
                xt_hi, xt_lo = sc2.sb("xt_hi", [P, H // P, R], F32R), sc2.sb("xt_lo", [P, H // P, R], F32R)
                layernorm_transposed(nc, "ln1", x_sb, xt_hi, xt_lo, ident)
                mamba_project(nc, xt_hi, xt_lo, w_in, conv_w, conv_b, w_x, u_sb, gate_sb, ssm_sb, B)
            b_all, c_all = sc1.sb("b_all", [P, NS, R]), sc1.sb("c_all", [P, NS, R])
            dt_sb = sc1.sb("dt", [P, DC, R])
            with Scope(nc, "mamba_w") as sc2:
                work = sc2.sb("work", [P, DC, R])
                mamba_parameters(nc, ssm_sb, w_dt, b_dt, ident, b_all, c_all, dt_sb, work)
            d_a = sc1.sb("d_a", [P, 2, NS // 2, B, R // B])
            d_bu = sc1.sb("d_bu", [P, 2, NS // 2, B, R // B])
            mamba_scan(nc, u_sb, gate_sb, b_all, c_all, dt_sb, d_a, d_bu, a_log, d_skip, ident)
        mamba_output(nc, x_sb, gate_sb, w_out)


def ternary_linear(nc, x_sb, xt_hi, xt_lo, w, bias, ones):
    KC, H = w.shape[1:]
    R = xt_hi.shape[2]
    RT = R // P
    with Scope(nc, "tl") as sc:
        raw, neg = sc.sb("raw", [P, KC, H]), sc.sb("neg", [P, KC, H])
        tern, tern_r = sc.sb("tern", [P, KC, H]), sc.sb("tern_r", [P, KC, H], F32R)
        bias_sb = sc.sb("bias", [P, H])
        part = sc.sb("part", [P, 2])
        tot = sc.sb("tot", [P, 2])
        few = sc.sb("few", [P, 1])
        scale = sc.sb("scale", [P, 1])
        tot_ps = sc.ps("tot_ps", [P, 512])
        ps = sc.ps("ps", [P, RT, 512])
        w_in, own, part_set, tot_full, tern_set, done = (
            sc.sem(n) for n in ("w_in", "own", "part_set", "tot_full", "tern_set", "done"))
        block = sc.block()

        @block.sync
        def _(sp):
            sp.dma_start(raw[:, :, :], w).then_inc(w_in, 16)
            sp.dma_start(bias_sb[:, :], bias.rearrange("(a n) -> a n", a=1).broadcast_to([P, H])).then_inc(w_in, 16)

        @block.vector
        def _(dve):
            step = Chain(dve, own)
            dve.wait_ge(w_in, 32)
            step(nc.vector.tensor_scalar(neg[:, :, :], raw[:, :, :], -0.5, None, ALU.is_lt))
            step(nc.vector.scalar_tensor_tensor(out=tern[:, :, :], in0=raw[:, :, :], scalar=0.5, in1=neg[:, :, :],
                                                op0=ALU.is_gt, op1=ALU.subtract))
            nc.vector.tensor_copy(tern_r[:, :, :], tern[:, :, :]).then_inc(tern_set, 1)
            step(nc.vector.tensor_tensor(neg[:, :, :], tern[:, :, :], tern[:, :, :], ALU.mult))
            step(nc.vector.tensor_reduce(part[:, 0:1], neg[:, :, :].rearrange("p k n -> p (k n)"), AX_X, ALU.add))
            step(nc.vector.tensor_tensor(neg[:, :, :], tern[:, :, :], raw[:, :, :], ALU.mult))
            nc.vector.tensor_reduce(part[:, 1:2], neg[:, :, :].rearrange("p k n -> p (k n)"), AX_X,
                                    ALU.add).then_inc(part_set, 1)
            dve.wait_ge(tot_full, 1)
            step(nc.vector.tensor_copy(tot[:, :], tot_ps[:, 0:2]))
            step(nc.vector.tensor_scalar(few[:, :], tot[:, 0:1], 0.0, None, ALU.is_equal))
            step(nc.vector.tensor_scalar(tot[:, 0:1], tot[:, 0:1], 1.0, None, ALU.max))
            step(nc.vector.reciprocal(scale[:, :], tot[:, 0:1]))
            step(nc.vector.scalar_tensor_tensor(out=scale[:, :], in0=scale[:, :], scalar=tot[:, 1:2], in1=few[:, :],
                                                op0=ALU.mult, op1=ALU.add))
            for r in range(RT):
                step(nc.vector.tensor_tensor(x_sb[:, r, :], x_sb[:, r, :], bias_sb[:, :], ALU.add))
            for r in range(RT):
                dve.wait_ge(done, r + 1)
                nc.vector.scalar_tensor_tensor(out=x_sb[:, r, :], in0=ps[:, r, :], scalar=scale[:, 0:1],
                                               in1=x_sb[:, r, :], op0=ALU.mult, op1=ALU.add)

        @block.tensor
        def _(pe):
            pe.wait_ge(tern_set, 1)
            for r in range(RT):
                rs = slice(r * P, (r + 1) * P)
                for k in range(KC):
                    nc.tensor.matmul(ps[:, r, :], xt_hi[:, k, rs], tern_r[:, k, :], start=k == 0, stop=False)
                    end = nc.tensor.matmul(ps[:, r, :], xt_lo[:, k, rs], tern_r[:, k, :], start=False, stop=k == KC - 1)
                end.then_inc(done, 1)
            pe.wait_ge(part_set, 1)
            nc.tensor.matmul(tot_ps[:, 0:2], ones[:, :], part[:, :], start=True, stop=True).then_inc(tot_full, 1)


def context_attention(nc, x_sb, xt_hi, xt_lo, ctx, ident, c_dram):
    B, S, H = ctx.shape
    KC = xt_hi.shape[1]
    R = xt_hi.shape[2]
    L = R // B
    SE = S + S % 2
    NC = -(-S // P)
    TILES = even_tiles(SE)
    NT = len(TILES)
    NB = -(-NC // 8)
    GROUPS = [(c, min(c + 2, NC)) for c in range(0, NC, 2)]
    if S % P and GROUPS[-1][1] - GROUPS[-1][0] > 1:
        GROUPS[-1:] = [(NC - 2, NC - 1), (NC - 1, NC)]
    NG = len(GROUPS)
    LO_DVE = 3
    EARLY = -(-(TILES[1][0] + TILES[1][1]) // P)

    def rows(c):
        return min(P, S - c * P)

    def group_of(c):
        return [g for g, (a, z) in enumerate(GROUPS) if a <= c < z][0]

    PARTS = [slice(0, 2), slice(2, 3), slice(3, KC)]
    SCORES, late = [], list(range(EARLY, NC))
    for t in range(NT):
        for part in range(len(PARTS)):
            SCORES.append(("s", t, part))
            if late:
                SCORES.append(("t", late.pop(0), None))

    NS = 3

    def slot(c):
        return 1 if c == NC - 1 and c % NS == 0 else c % NS

    def ago(c):
        return min(d for d in range(1, NS + 1) if d == NS or slot((c - d) % NC) == slot(c))

    def drive(eng, step):
        step(0, -1, True, True)
        with eng.Fori(0, (B - 2) // 2) as h:
            step(h, 0, True, True)
            step(h, 1, True, True)
        step((B - 2) // 2, 0, True, False)
        step((B - 2) // 2, 1, False, False)

    with Scope(nc, "ca") as sc:
        nat = sc.sb("nat", [P, 2, NC, H])
        n_hi, n_lo = sc.sb("n_hi", [P, NC, H], F32R), sc.sb("n_lo", [P, NC, H], F32R)
        t_hi, t_lo = sc.sb("t_hi", [P, KC, SE], F32R), sc.sb("t_lo", [P, KC, SE], F32R)
        q_hi, q_lo = sc.sb("q_hi", [P, 2, KC, L], F32R), sc.sb("q_lo", [P, 2, KC, L], F32R)
        prob = sc.sb("prob", [L, SE])
        tmax, nmax = sc.sb("tmax", [L, NT]), sc.sb("nmax", [L, 1])
        den, rden = sc.sb("den", [L, 2]), sc.sb("rden", [L, 2])
        pt_hi, pt_lo = sc.sb("pt_hi", [P, NC, L], F32R), sc.sb("pt_lo", [P, NC, L], F32R)
        c_sb = sc.sb("c_sb", [L, H])
        t_ps = sc.ps("t_ps", [P, NS, 512])
        s_ps = sc.ps("s_ps", [L, 2, 512])
        pt_ps = sc.ps("pt_ps", [P, NB, 512])
        c_ps = sc.ps("c_ps", [L, 512])
        nat_in = [[sc.sem(f"nat_in{i}_{g}") for g in range(NG)] for i in range(2)]
        passed, passed_pe, passed_sp = sc.sem("passed"), sc.sem("passed_pe"), sc.sem("passed_sp")
        c_out = sc.sem("c_out")
        q_set, n_hi_set, lo_dve, lo_pool, t_full, t_hi_set, t_free = (
            sc.sem(n) for n in ("q_set", "n_hi_set", "lo_dve", "lo_pool", "t_full", "t_hi_set", "t_free"))
        s_full, s_free, nmax_set, exp_set, pt_full, pt_hi_set, pt_free = (
            sc.sem(n) for n in ("s_full", "s_free", "nmax_set", "exp_set", "pt_full", "pt_hi_set", "pt_free"))
        pv_done, rden_set, c_set, pad_set, x_in = (sc.sem(n) for n in ("pv_done", "rden_set", "c_set", "pad_set", "x_in"))
        block = sc.block()

        def loaded(eng, h, i, g):
            eng.wait_ge(nat_in[i % 2][g], (h + i // 2 + 1) * 16)

        def split_done(eng, h, i, g):
            if g < LO_DVE:
                eng.wait_ge(lo_dve, (2 * h + i) * LO_DVE + g + 1)
            else:
                eng.wait_ge(lo_pool, (2 * h + i) * (NG - LO_DVE) + g - LO_DVE + 1)

        @block.sync
        def _(sp):
            def load(h, i, g):
                a, z = GROUPS[g]
                r = rows(a)
                sp.dma_start(nat[0:r, i % 2, a:z, :],
                             ctx[2 * h + i, a * P:a * P + (z - a) * r].rearrange("(c p) h -> p c h", p=r)
                             ).then_inc(nat_in[i % 2][g], 16)

            for i in range(2):
                for g in range(NG):
                    load(0, i, g)
            with sp.Fori(0, (B - 2) // 2) as h:
                for i in range(2):
                    for g, (a, z) in enumerate(GROUPS):
                        sp.wait_ge(t_full, (2 * h + i) * NC + z)
                        apart(sp, passed_sp)
                        split_done(sp, h, i, g)
                        load(h, i + 2, g)

        @block.gpsimd
        def _(pool):
            def step(h, i, has1, has2):
                i += 1
                if not has1:
                    return
                for g, (a, z) in enumerate(GROUPS):
                    r = rows(a)
                    loaded(pool, h, i, g)
                    pool.wait_ge(pv_done, (2 * h + i) * NG + g + 1)
                    apart(pool, passed)
                    nc.gpsimd.tensor_scalar(n_hi[0:r, a:z, :], nat[0:r, i % 2, a:z, :], 1.0, 1.0,
                                            ALU.mult, ALU.mult).then_inc(n_hi_set, 1)
                for g, (a, z) in enumerate(GROUPS):
                    if g >= LO_DVE:
                        r = rows(a)
                        pool.wait_ge(n_hi_set, (2 * h + i) * NG + g + 1)
                        nc.gpsimd.tensor_tensor(n_lo[0:r, a:z, :], nat[0:r, i % 2, a:z, :],
                                                n_hi[0:r, a:z, :].bitcast(F32), ALU.subtract).then_inc(lo_pool, 1)

            drive(pool, step)

        @block.tensor
        def _(pe):
            pe.sem_inc(pv_done, NG)

            def transpose(h, i, c):
                r = rows(c)
                n = (2 * h + i) * NC + c
                loaded(pe, h, i, group_of(c))
                pe.wait_ge(t_free, n + 1 + NS - ago(c))
                for k in range(KC):
                    end = nc.tensor.transpose(t_ps[:, slot(c), k * P:k * P + r],
                                              nat[0:r, i % 2, c, k * P:(k + 1) * P], ident[0:r, 0:r])
                end.then_inc(t_full, 1)

            def score_part(h, i, t, part):
                n = 2 * h + i
                c, w = TILES[t]
                if part == 0:
                    if t == 0:
                        pe.wait_ge(q_set, n * 2 + 2)
                    pe.wait_ge(t_free, n * NC + min(NC, -(-(c + w) // P)) + NS)
                    pe.wait_ge(s_free, n * NT + t + 1)
                for k in range(KC)[PARTS[part]]:
                    end = product(nc, s_ps[:, t % 2, 0:w], (q_hi[:, i % 2, k, :], q_lo[:, i % 2, k, :]),
                                  (t_hi[:, k, c:c + w], t_lo[:, k, c:c + w]), k == 0, k == KC - 1)
                if part == len(PARTS) - 1:
                    end.then_inc(s_full, 1)

            def pv(h, i, c):
                n = 2 * h + i
                r = rows(c)
                g = group_of(c)
                if c == 0:
                    pe.wait_ge(c_set, n + 1)
                if c % 8 == 0:
                    pe.wait_ge(pt_free, n * NB + c // 8 + 1 + NB)
                if c == GROUPS[g][0]:
                    split_done(pe, h, i, g)
                end = product(nc, c_ps[:, :], (pt_hi[0:r, c, :], pt_lo[0:r, c, :]),
                              (n_hi[0:r, c, :], n_lo[0:r, c, :]), c == 0, c == NC - 1)
                if c == GROUPS[g][1] - 1:
                    end.then_inc(pv_done, 1)

            def step(h, i, has1, has2):
                if i == -1:
                    for c in range(EARLY):
                        transpose(h, 0, c)
                if has1:
                    for kind, at, part in SCORES:
                        if kind == "s":
                            score_part(h, i + 1, at, part)
                        else:
                            transpose(h, i + 1, at)
                early = list(range(EARLY)) if has2 else []
                for c in range(NC):
                    if i >= 0:
                        pv(h, i, c)
                    if early and c % 2 == 1:
                        transpose(h, i + 2, early.pop(0))
                for c in early:
                    transpose(h, i + 2, c)
                if has1:
                    n = 2 * h + i + 1
                    pe.wait_ge(exp_set, n + 1)
                    for c in range(NC):
                        if c % 8 == 0:
                            pe.wait_ge(pt_free, n * NB + c // 8 + 1)
                            apart(pe, passed_pe)
                        r = rows(c)
                        end = nc.tensor.transpose(pt_ps[0:r, c // 8, (c % 8) * L:(c % 8 + 1) * L],
                                                  prob[:, c * P:c * P + r], ident[0:L, 0:L])
                        if c % 8 == 7 or c == NC - 1:
                            end.then_inc(pt_full, 1)

            drive(pe, step)

        def pt_parts():
            for g in range(NB):
                a, z = 8 * g, min(8 * g + 8, NC)
                if z == NC and rows(NC - 1) < P:
                    yield g, a, z - 1, P, False
                    yield g, z - 1, z, rows(z - 1), True
                else:
                    yield g, a, z, P, True

        def bank(g, a, z, r):
            return pt_ps[0:r, g, (a % 8) * L:(a % 8 + z - a) * L].rearrange("p (c l) -> p c l", l=L)

        def transposed(c, r):
            return t_ps[:, slot(c), :].rearrange("p (k n) -> p k n", k=KC)[:, :, 0:r]

        @block.scalar
        def _(act):
            def high(h, i, c):
                r = rows(c)
                act.wait_ge(t_full, (2 * h + i) * NC + c + 1)
                nc.scalar.activation(t_hi[:, :, c * P:c * P + r], transposed(c, r), ACT.Copy).then_inc(t_hi_set, 1)

            def query(h, i):
                b = 2 * h + i
                nc.scalar.activation(q_hi[:, i % 2], xt_hi[:, :, bass.ds(b * L, L)].bitcast(F32), ACT.Copy).then_inc(q_set, 1)
                nc.scalar.activation(q_lo[:, i % 2], xt_lo[:, :, bass.ds(b * L, L)].bitcast(F32), ACT.Copy).then_inc(q_set, 1)

            def step(h, i, has1, has2):
                if i == -1:
                    query(h, 0)
                    for c in range(EARLY):
                        high(h, 0, c)
                if has1:
                    for c in range(EARLY, NC):
                        high(h, i + 1, c)
                    n = 2 * h + i + 1
                    act.wait_ge(nmax_set, n + 1)
                    nc.scalar.activation(prob[:, 0:S], prob[:, 0:S], ACT.Exp, bias=nmax[:, 0:1],
                                         accum_out=den[:, (i + 1) % 2:(i + 1) % 2 + 1]).then_inc(exp_set, 1)
                if has2:
                    query(h, i + 2)
                    for c in range(EARLY):
                        high(h, i + 2, c)
                if has1:
                    for g, a, z, r, last in pt_parts():
                        act.wait_ge(pt_full, (2 * h + i + 1) * NB + g + 1)
                        nc.scalar.activation(pt_hi[0:r, a:z, :], bank(g, a, z, r), ACT.Copy).then_inc(pt_hi_set, 1)
                if i >= 0:
                    act.wait_ge(c_set, 2 * h + i + 2)
                    act.dma_start(c_dram[2 * h + i], c_sb[:, :]).then_inc(c_out, 16)

            act.sem_inc(c_out, 16)
            drive(act, step)
            act.wait_ge(c_out, (B + 1) * 16)
            x_view = c_dram.rearrange("(r b) l h -> r (b l) h", r=R // P)
            for r in range(R // P):
                act.dma_start(nat[:, 0, r, :], x_view[r]).then_inc(x_in, 16)

        @block.vector
        def _(dve):
            parts = list(pt_parts())

            def low(h, i, c):
                r = rows(c)
                dve.wait_ge(t_hi_set, (2 * h + i) * NC + c + 1)
                nc.vector.tensor_tensor(t_lo[:, :, c * P:c * P + r], transposed(c, r),
                                        t_hi[:, :, c * P:c * P + r].bitcast(F32), ALU.subtract).then_inc(t_free, 1)

            def natural_low(h, i, g):
                a, z = GROUPS[g]
                r = rows(a)
                dve.wait_ge(n_hi_set, (2 * h + i) * NG + g + 1)
                nc.vector.tensor_tensor(n_lo[0:r, a:z, :], nat[0:r, i % 2, a:z, :],
                                        n_hi[0:r, a:z, :].bitcast(F32), ALU.subtract).then_inc(lo_dve, 1)

            def maximum(h, i, t):
                c, w = TILES[t]
                w = min(w, S - c)
                dve.wait_ge(s_full, (2 * h + i) * NT + t + 1)
                nc.vector.tensor_scalar(prob[:, c:c + w], s_ps[:, t % 2, 0:w], 1.0, None, ALU.mult, ALU.max,
                                        accum_out=tmax[:, t:t + 1]).then_inc(s_free, 1)

            def step(h, i, has1, has2):
                if i == -1:
                    for c in range(EARLY):
                        low(h, 0, c)
                if has1:
                    n = 2 * h + i + 1
                    for kind, at, part in SCORES:
                        if kind == "t":
                            low(h, i + 1, at)
                        elif part == len(PARTS) - 1:
                            maximum(h, i + 1, at)
                            if at == NT // 2 and i >= 0:
                                natural_low(h, i, LO_DVE - 1)
                    dve.wait_ge(s_free, n * NT + NT + 2)
                    nc.vector.tensor_reduce(nmax[:, :], tmax[:, :], AX_X, ALU.max, negate=True).then_inc(nmax_set, 1)
                elif i >= 0:
                    natural_low(h, i, LO_DVE - 1)
                if has2:
                    for c in range(EARLY):
                        low(h, i + 2, c)
                        if c in (3, 5):
                            natural_low(h, i + 1, (c - 3) // 2)
                elif has1:
                    natural_low(h, i + 1, 0)
                    natural_low(h, i + 1, 1)
                s = (i + 1) % 2
                if has1:
                    dve.wait_ge(exp_set, n + 1)
                    nc.vector.reciprocal(rden[:, s:s + 1], den[:, s:s + 1]).then_inc(rden_set, 1)
                if i >= 0:
                    b = 2 * h + i
                    dve.wait_ge(pv_done, b * NG + 2 * NG)
                    dve.wait_ge(rden_set, b + 1)
                    dve.wait_ge(c_out, b * 16 + 16)
                    nc.vector.tensor_scalar(c_sb[:, :], c_ps[:, :], rden[:, i % 2:i % 2 + 1], None,
                                            ALU.mult).then_inc(c_set, 1)
                if has1:
                    for at, (g, a, z, r, last) in enumerate(parts):
                        dve.wait_ge(pt_hi_set, n * len(parts) + at + (1 if last else 2))
                        ins = nc.vector.tensor_tensor(pt_lo[0:r, a:z, :], bank(g, a, z, r),
                                                      pt_hi[0:r, a:z, :].bitcast(F32), ALU.subtract)
                        if last:
                            ins.then_inc(pt_free, 1)

            dve.sem_inc(t_free, NS)
            dve.sem_inc(s_free, 2)
            dve.sem_inc(pt_free, NB)
            dve.sem_inc(c_set, 1)
            if SE > S:
                nc.vector.memset(t_hi[:, :, S:SE].bitcast(F32), 0.0).then_inc(pad_set, 1)
                nc.vector.memset(t_lo[:, :, S:SE].bitcast(F32), 0.0).then_inc(pad_set, 1)
            drive(dve, step)
            dve.wait_ge(x_in, R // P * 16)
            nc.vector.tensor_tensor(x_sb[:, :, :], x_sb[:, :, :], nat[:, 0, 0:R // P, :], ALU.add)


def self_attention(nc, x_sb, xt_hi, xt_lo, w_qkv, w_o, rotary, head_mask, causal, ident, B, NH):
    RT, H = x_sb.shape[1:]
    KC = H // P
    R = RT * P
    L = R // B
    BR = P // L
    HD = H // NH
    HC = P // HD
    SCALE = float(HD) ** -0.5
    with Scope(nc, "sa") as top:
        qz_hi, qz_lo = (top.sb(n, [P, RT, KC, BR, P], F32R) for n in ("qz_hi", "qz_lo"))
        kt_hi, kt_lo = (top.sb(n, [P, RT, KC, P], F32R) for n in ("kt_hi", "kt_lo"))
        v_hi, v_lo = (top.sb(n, [L, B, H], F32R) for n in ("v_hi", "v_lo"))
        o_sb = top.sb("o_sb", [L, B, H])
        hm, cm = top.sb("hm", [P, HC]), top.sb("cm", [P, L])

        with Scope(nc, "sa1") as sc:
            raw = sc.sb("raw", [P, 3, KC, H])
            w_hi, w_lo = sc.sb("w_hi", [P, 3, KC, H], F32R), sc.sb("w_lo", [P, 3, KC, H], F32R)
            rot = sc.sb("rot", [P, 3])
            a_sb = sc.sb("a_sb", [P, 2, H])
            r_sb = sc.sb("r_sb", [P, 2, H])
            p_ps = sc.ps("p_ps", [P, 2, 512])
            v_ps = sc.ps("v_ps", [L, 2, 512])
            t_ps = sc.ps("t_ps", [P, 2, 512])
            w_in = [sc.sem(f"w_in{i}") for i in range(3)]
            small_in, w_hi_set, w_lo_set, p_full, a_set, r_set, zero_set, t_full, t_hi_set, t_free = (
                sc.sem(n) for n in ("small_in", "w_hi_set", "w_lo_set", "p_full", "a_set", "r_set",
                                    "zero_set", "t_full", "t_hi_set", "t_free"))
            v_full, v_hi_set, v_free = (sc.sem(n) for n in ("v_full", "v_hi_set", "v_free"))
            block = sc.block()
            units = [(i, r) for r in range(RT) for i in range(2)]

            @block.sync
            def _(sp):
                for i in range(3):
                    sp.dma_start(raw[:, i], w_qkv[i]).then_inc(w_in[i], 16)
                sp.dma_start(rot[:, :], rotary).then_inc(small_in, 16)
                sp.dma_start(hm[:, :], head_mask).then_inc(small_in, 16)
                sp.dma_start(cm[:, :], causal).then_inc(small_in, 16)
                sp.wait_ge(small_in, 48)

            @block.gpsimd
            def _(pool):
                nc.gpsimd.memset(qz_hi[:, :, :, :, :].bitcast(F32), 0.0).then_inc(zero_set, 1)
                nc.gpsimd.memset(qz_lo[:, :, :, :, :].bitcast(F32), 0.0).then_inc(zero_set, 1)

            @block.tensor
            def _(pe):
                def transposes(n):
                    pe.wait_ge(r_set, 2 * n + 2)
                    if n >= 2:
                        pe.wait_ge(t_free, n - 1)
                    for k in range(KC):
                        end = nc.tensor.transpose(t_ps[:, n % 2, k * P:(k + 1) * P], r_sb[:, n % 2, k * P:(k + 1) * P],
                                                  ident[:, :])
                    end.then_inc(t_full, 1)

                for n, (i, r) in enumerate(units):
                    pe.wait_ge(w_lo_set, i + 1)
                    if n >= 2:
                        pe.wait_ge(r_set, 2 * n - 2)
                    for k in range(KC):
                        rs = slice(r * P, (r + 1) * P)
                        end = product(nc, p_ps[:, n % 2, :], (xt_hi[:, k, rs], xt_lo[:, k, rs]),
                                      (w_hi[:, i, k, :], w_lo[:, i, k, :]), k == 0, k == KC - 1)
                    end.then_inc(p_full, 1)
                    if n > 0:
                        transposes(n - 1)
                transposes(len(units) - 1)
                pe.wait_ge(w_lo_set, 3)
                for b in range(B):
                    if b >= 2:
                        pe.wait_ge(v_free, b - 1)
                    for k in range(KC):
                        rs = slice(b * L, (b + 1) * L)
                        end = product(nc, v_ps[:, b % 2, :], (xt_hi[:, k, rs], xt_lo[:, k, rs]),
                                      (w_hi[:, 2, k, :], w_lo[:, 2, k, :]), k == 0, k == KC - 1)
                    end.then_inc(v_full, 1)

            def turned(n, bank):
                i, r = units[n]
                if i:
                    return [(kt_hi[:, r], kt_lo[:, r], bank.rearrange("p (k c) -> p k c", k=KC))]
                v = bank.rearrange("p (k b l) -> p b k l", k=KC, b=BR)
                return [(qz_hi[:, r, :, b, b * L:(b + 1) * L], qz_lo[:, r, :, b, b * L:(b + 1) * L], v[:, b])
                        for b in range(BR)]

            @block.scalar
            def _(act):
                for i in range(3):
                    act.wait_ge(w_in[i], 16)
                    nc.scalar.activation(w_hi[:, i], raw[:, i], ACT.Copy).then_inc(w_hi_set, 1)
                act.wait_ge(small_in, 48)
                act.wait_ge(zero_set, 2)

                def high(n):
                    act.wait_ge(t_full, n + 1)
                    for hi, _, src in turned(n, t_ps[:, n % 2, :]):
                        end = nc.scalar.activation(hi, src, ACT.Copy)
                    end.then_inc(t_hi_set, 1)

                for n in range(len(units)):
                    act.wait_ge(p_full, n + 1)
                    if n >= 2:
                        act.wait_ge(r_set, 2 * n - 2)
                    nc.scalar.activation(a_sb[:, n % 2, :], p_ps[:, n % 2, :], ACT.Copy,
                                         scale=rot[:, 0:1]).then_inc(a_set, 1)
                    if n > 0:
                        high(n - 1)
                high(len(units) - 1)
                for b in range(B):
                    act.wait_ge(v_full, b + 1)
                    nc.scalar.activation(v_hi[:, b, :], v_ps[:, b % 2, :], ACT.Copy).then_inc(v_hi_set, 1)

            @block.vector
            def _(dve):
                for i in range(3):
                    dve.wait_ge(w_hi_set, i + 1)
                    nc.vector.tensor_tensor(w_lo[:, i], raw[:, i], w_hi[:, i].bitcast(F32),
                                            ALU.subtract).then_inc(w_lo_set, 1)
                dve.wait_ge(small_in, 48)

                def low_part(n):
                    dve.wait_ge(t_hi_set, n + 1)
                    for hi, lo, src in turned(n, t_ps[:, n % 2, :]):
                        end = nc.vector.tensor_tensor(lo, src, hi.bitcast(F32), ALU.subtract)
                    end.then_inc(t_free, 1)

                for n in range(len(units)):
                    src = p_ps[:, n % 2, :].rearrange("p (m e) -> p e m", e=2)
                    a = a_sb[:, n % 2, :].rearrange("p (m e) -> p e m", e=2)
                    out = r_sb[:, n % 2, :].rearrange("p (m e) -> p e m", e=2)
                    dve.wait_ge(a_set, n + 1)
                    if n >= 2:
                        dve.wait_ge(t_full, n - 1)
                    nc.vector.scalar_tensor_tensor(out=out[:, 0], in0=src[:, 1], scalar=rot[:, 2:3], in1=a[:, 0],
                                                   op0=ALU.mult, op1=ALU.add).then_inc(r_set, 1)
                    nc.vector.scalar_tensor_tensor(out=out[:, 1], in0=src[:, 0], scalar=rot[:, 1:2], in1=a[:, 1],
                                                   op0=ALU.mult, op1=ALU.add).then_inc(r_set, 1)
                    if n > 0:
                        low_part(n - 1)
                low_part(len(units) - 1)
                for b in range(B):
                    dve.wait_ge(v_hi_set, b + 1)
                    nc.vector.tensor_tensor(v_lo[:, b, :], v_ps[:, b % 2, :], v_hi[:, b, :].bitcast(F32),
                                            ALU.subtract).then_inc(v_free, 1)

        with Scope(nc, "sa2") as sc:
            kb_hi, kb_lo = (sc.sb(n, [P, 2, BR, HC, L], F32R) for n in ("kb_hi", "kb_lo"))
            s_sb = sc.sb("s_sb", [P, 2, HC, L])
            mx, sm, rs_ = sc.sb("mx", [P, 2, HC]), sc.sb("sm", [P, 2, HC]), sc.sb("rs", [P, 2, HC])
            pt_hi, pt_lo = (sc.sb(n, [L, 2, HC, P], F32R) for n in ("pt_hi", "pt_lo"))
            s_ps = sc.ps("s_ps", [P, 2, 512])
            t_ps = sc.ps("t_ps", [L, 4, 512])
            o_ps = sc.ps("o_ps", [L, BR, 512])
            kb_hi_set, kb_lo_set, s_full, s_read, own, d_set, e_set, r_set, p_set, t_full, t_hi_set, t_lo_set = (
                sc.sem(n) for n in ("kb_hi_set", "kb_lo_set", "s_full", "s_read", "own", "d_set", "e_set", "r_set",
                                    "p_set", "t_full", "t_hi_set", "t_lo_set"))
            o_full, o_free = sc.sem("o_full"), sc.sem("o_free")
            block = sc.block()
            units = [(r, c) for r in range(RT) for c in range(KC)]
            NU = len(units)
            HB = 512 // P
            NB = HC // HB

            def wide(t):
                return t.unsqueeze(2).broadcast_to([P, HC, L])

            def blocks(eng, out, kt, n, sem):
                r, c = units[n]
                for b in range(BR):
                    end = eng.tensor_tensor(out[:, n % 2, b], kt[:, r, c, b * L:(b + 1) * L].bitcast(F32).unsqueeze(1)
                                            .broadcast_to([P, HC, L]), wide(hm[:, :]), ALU.mult)
                end.then_inc(sem, 1)

            @block.gpsimd
            def _(pool):
                for n in range(NU + 1):
                    if n < NU:
                        if n >= 2:
                            pool.wait_ge(s_full, n - 1)
                        blocks(nc.gpsimd, kb_hi, kt_hi, n, kb_hi_set)
                    if n > 0:
                        m = n - 1
                        pool.wait_ge(r_set, m + 1)
                        nc.gpsimd.tensor_tensor(s_sb[:, m % 2], s_sb[:, m % 2], wide(rs_[:, m % 2, :]),
                                                ALU.mult).then_inc(p_set, 1)

            @block.tensor
            def _(pe):
                def scores(n):
                    r, c = units[n]
                    pe.wait_ge(kb_hi_set, n + 1)
                    pe.wait_ge(kb_lo_set, n + 1)
                    if n >= 2:
                        pe.wait_ge(s_read, n - 1)
                    for b in range(BR):
                        end = product(nc, s_ps[:, n % 2, :], (qz_hi[:, r, c, b, :], qz_lo[:, r, c, b, :]),
                                      (kb_hi[:, n % 2, b].rearrange("p h l -> p (h l)"),
                                       kb_lo[:, n % 2, b].rearrange("p h l -> p (h l)")), b == 0, b == BR - 1)
                    end.then_inc(s_full, 1)

                def attend(n):
                    r, c = units[n]
                    pe.wait_ge(p_set, n + 1)
                    for i in range(NB):
                        t = n * NB + i
                        if t >= 4:
                            pe.wait_ge(t_lo_set, t - 3)
                        for h in range(HB):
                            end = nc.tensor.transpose(t_ps[:, t % 4, h * P:(h + 1) * P],
                                                      s_sb[:, n % 2, i * HB + h, :], ident[:, :])
                        end.then_inc(t_full, 1)

                def values(n):
                    r, c = units[n]
                    pe.wait_ge(t_lo_set, (n + 1) * NB)
                    if c == 0 and r > 0:
                        pe.wait_ge(o_free, r)
                    for b in range(BR):
                        for h in range(HC):
                            o = c * P + h * HD
                            ls = slice(b * L, (b + 1) * L)
                            end = product(nc, o_ps[:, b, o:o + HD],
                                          (pt_hi[:, n % 2, h, ls], pt_lo[:, n % 2, h, ls]),
                                          (v_hi[:, r * BR + b, o:o + HD], v_lo[:, r * BR + b, o:o + HD]), True, True)
                    end.then_inc(o_full, 1)

                scores(0)
                for n in range(NU):
                    if n + 1 < NU:
                        scores(n + 1)
                    if n > 0:
                        values(n - 1)
                    attend(n)
                values(NU - 1)

            def high(act, n):
                for i in range(NB):
                    t = n * NB + i
                    act.wait_ge(t_full, t + 1)
                    if n >= 2 and i == 0:
                        act.wait_ge(o_full, n - 1)
                    hs = slice(i * HB, (i + 1) * HB)
                    nc.scalar.activation(pt_hi[:, n % 2, hs, :], t_ps[:, t % 4, :].rearrange("p (h c) -> p h c", h=HB),
                                         ACT.Copy).then_inc(t_hi_set, 1)

            @block.scalar
            def _(act):
                for n in range(NU):
                    act.wait_ge(d_set, n + 1)
                    nc.scalar.activation(s_sb[:, n % 2], s_sb[:, n % 2], ACT.Exp).then_inc(e_set, 1)
                    if n > 0:
                        high(act, n - 1)
                high(act, NU - 1)

            @block.vector
            def _(dve):
                step = Chain(dve, own)

                def softmax(n):
                    s = s_sb[:, n % 2]
                    dve.wait_ge(s_full, n + 1)
                    if n >= 2:
                        dve.wait_ge(t_full, (n - 1) * NB)
                    ins = nc.vector.scalar_tensor_tensor(
                        out=s, in0=s_ps[:, n % 2, :].rearrange("p (h l) -> p h l", h=HC), scalar=SCALE,
                        in1=cm[:, :].unsqueeze(1).broadcast_to([P, HC, L]), op0=ALU.mult, op1=ALU.add)
                    ins.then_inc(s_read, 1)
                    dve.wait_ge(s_read, n + 1)
                    step(nc.vector.tensor_reduce(mx[:, n % 2, :], s, AX_X, ALU.max))
                    nc.vector.tensor_tensor(s, s, wide(mx[:, n % 2, :]), ALU.subtract).then_inc(d_set, 1)

                def sums(n):
                    dve.wait_ge(e_set, n + 1)
                    step(nc.vector.tensor_reduce(sm[:, n % 2, :], s_sb[:, n % 2], AX_X, ALU.add))
                    nc.vector.reciprocal(rs_[:, n % 2, :], sm[:, n % 2, :]).then_inc(r_set, 1)

                def low(n):
                    r, c = units[n]
                    for i in range(NB):
                        t = n * NB + i
                        dve.wait_ge(t_hi_set, t + 1)
                        hs = slice(i * HB, (i + 1) * HB)
                        nc.vector.tensor_tensor(pt_lo[:, n % 2, hs, :], t_ps[:, t % 4, :].rearrange("p (h c) -> p h c", h=HB),
                                                pt_hi[:, n % 2, hs, :].bitcast(F32), ALU.subtract).then_inc(t_lo_set, 1)

                def output(r):
                    dve.wait_ge(o_full, (r + 1) * KC)
                    nc.vector.tensor_copy(o_sb[:, r * BR:(r + 1) * BR, :], o_ps[:, :, :]).then_inc(o_free, 1)

                blocks(nc.vector, kb_lo, kt_lo, 0, kb_lo_set)
                for n in range(NU):
                    if n + 1 < NU:
                        if n >= 1:
                            dve.wait_ge(s_full, n)
                        blocks(nc.vector, kb_lo, kt_lo, n + 1, kb_lo_set)
                    softmax(n)
                    if n > 0:
                        low(n - 1)
                    sums(n)
                    if n > KC and units[n][1] == 1:
                        output(units[n][0] - 1)
                low(NU - 1)
                output(RT - 1)

        with Scope(nc, "sa3") as sc:
            raw = sc.sb("raw", [P, KC, H])
            w_hi, w_lo = sc.sb("w_hi", [P, KC, H], F32R), sc.sb("w_lo", [P, KC, H], F32R)
            ot_hi, ot_lo = sc.sb("ot_hi", [P, KC, R], F32R), sc.sb("ot_lo", [P, KC, R], F32R)
            t_ps = sc.ps("t_ps", [P, RT, 512])
            ps = sc.ps("ps", [P, RT, 512])
            w_in, w_hi_set, t_full, hi_set, lo_set, done = (
                sc.sem(n) for n in ("w_in", "w_hi_set", "t_full", "hi_set", "lo_set", "done"))
            block = sc.block()

            @block.sync
            def _(sp):
                sp.dma_start(raw[:, :, :], w_o).then_inc(w_in, 16)

            @block.tensor
            def _(pe):
                for r in range(RT):
                    for k in range(KC):
                        for b in range(BR):
                            o = k * P + b * L
                            end = nc.tensor.transpose(t_ps[:, r, o:o + L], o_sb[:, r * BR + b, k * P:(k + 1) * P],
                                                      ident[0:L, 0:L])
                    end.then_inc(t_full, 1)
                for r in range(RT):
                    pe.wait_ge(lo_set, r + 2)
                    rs = slice(r * P, (r + 1) * P)
                    for k in range(KC):
                        end = product(nc, ps[:, r, :], (ot_hi[:, k, rs], ot_lo[:, k, rs]),
                                      (w_hi[:, k, :], w_lo[:, k, :]), k == 0, k == KC - 1)
                    end.then_inc(done, 1)

            @block.scalar
            def _(act):
                act.wait_ge(w_in, 16)
                nc.scalar.activation(w_hi[:, :, :], raw[:, :, :], ACT.Copy).then_inc(w_hi_set, 1)
                for r in range(RT):
                    act.wait_ge(t_full, r + 1)
                    nc.scalar.activation(ot_hi[:, :, r * P:(r + 1) * P], t_ps[:, r, :].rearrange("p (k c) -> p k c", k=KC),
                                         ACT.Copy).then_inc(hi_set, 1)

            @block.vector
            def _(dve):
                dve.wait_ge(w_hi_set, 1)
                nc.vector.tensor_tensor(w_lo[:, :, :], raw[:, :, :], w_hi[:, :, :].bitcast(F32),
                                        ALU.subtract).then_inc(lo_set, 1)
                for r in range(RT):
                    dve.wait_ge(hi_set, r + 1)
                    rs = slice(r * P, (r + 1) * P)
                    nc.vector.tensor_tensor(ot_lo[:, :, rs], t_ps[:, r, :].rearrange("p (k c) -> p k c", k=KC),
                                            ot_hi[:, :, rs].bitcast(F32), ALU.subtract).then_inc(lo_set, 1)
                for r in range(RT):
                    dve.wait_ge(done, r + 1)
                    nc.vector.tensor_tensor(x_sb[:, r, :], ps[:, r, :], x_sb[:, r, :], ALU.add)


def octonion_ffn(nc, x_sb, xt_hi, xt_lo, w_gate, w_up, w_down, sign_in, sign_down, ones):
    RT, H = x_sb.shape[1:]
    KC = w_gate.shape[1]
    O = w_gate.shape[3]
    F = 8 * O
    FC = w_down.shape[1]
    D8 = w_down.shape[3]
    R = RT * P

    def width(c):
        return min(P, F - c * P)

    with Scope(nc, "of") as top:
        tern = [top.sb(f"tern{i}", [P, KC, 8, O], F32R) for i in range(2)]
        tern_d = top.sb("tern_d", [P, FC, 8, D8], F32R)
        scale = top.sb("scale", [P, 3])
        with Scope(nc, "of1") as sc:
            raw = [sc.sb(f"raw{i}", [P, KC, 8, O]) for i in range(2)]
            raw_d = sc.sb("raw_d", [P, FC, 8, D8])
            tmp = sc.sb("tmp", [P, FC * 8 * D8])
            si, sd = sc.sb("si", [P, KC, 8]), sc.sb("sd", [P, FC, 8])
            part = sc.sb("part", [P, 3])
            half, nhalf = sc.sb("half", [P, 3]), sc.sb("nhalf", [P, 3])
            tot_ps = sc.ps("tot_ps", [P, 512])
            w_in = [sc.sem(f"w_in{i}") for i in range(3)]
            small_in, zero_set, part_set, tot_full, own = (
                sc.sem(n) for n in ("small_in", "zero_set", "part_set", "tot_full", "own"))
            block = sc.block()
            COUNT = float(O * D8 * 8)

            @block.sync
            def _(sp):
                sp.dma_start(si[:, :, :], sign_in).then_inc(small_in, 16)
                sp.dma_start(sd[:, :, :], sign_down).then_inc(small_in, 16)
                sp.dma_start(raw[0][:, :, :, :], w_gate).then_inc(w_in[0], 16)
                sp.dma_start(raw[1][:, :, :, :], w_up).then_inc(w_in[1], 16)
                sp.wait_ge(zero_set, 1)
                last = width(FC - 1)
                sp.dma_start(raw_d[:, 0:FC - 1], w_down[:, 0:FC - 1]).then_inc(w_in[2], 16)
                sp.dma_start(raw_d[0:last, FC - 1], w_down[0:last, FC - 1]).then_inc(w_in[2], 16)

            @block.gpsimd
            def _(pool):
                nc.gpsimd.memset(raw_d[:, FC - 1], 0.0).then_inc(zero_set, 1)

            @block.scalar
            def _(act):
                for i in range(3):
                    act.wait_ge(w_in[i], 16 if i < 2 else 32)
                    w = raw[i][:, :, :, :] if i < 2 else raw_d[:, :, :, :]
                    t = tern[i][:, :, :, :] if i < 2 else tern_d[:, :, :, :]
                    nc.scalar.activation(t, w, ACT.Abs, accum_out=part[:, i:i + 1]).then_inc(part_set, 1)

            @block.tensor
            def _(pe):
                pe.wait_ge(part_set, 3)
                nc.tensor.matmul(tot_ps[:, 0:3], ones[:, :], part[:, :], start=True, stop=True).then_inc(tot_full, 1)

            @block.vector
            def _(dve):
                step = Chain(dve, own)
                dve.wait_ge(tot_full, 1)
                step(nc.vector.tensor_scalar(scale[:, :], tot_ps[:, 0:3], 1.0 / (8.0 * COUNT), None, ALU.mult))
                step(nc.vector.tensor_scalar(half[:, :], scale[:, :], 0.5, None, ALU.mult))
                step(nc.vector.tensor_scalar(nhalf[:, :], scale[:, :], -0.5, None, ALU.mult))
                dve.wait_ge(small_in, 32)
                for i in range(3):
                    w, t, s = (raw[i], tern[i], si) if i < 2 else (raw_d, tern_d, sd)
                    K, M = (KC, O) if i < 2 else (FC, D8)
                    w = w[:, :, :, :].rearrange("p k j o -> p (k j o)")
                    m = tmp[:, 0:K * 8 * M]
                    step(nc.vector.tensor_scalar(m, w, nhalf[:, i:i + 1], None, ALU.is_lt))
                    step(nc.vector.scalar_tensor_tensor(out=w, in0=w, scalar=half[:, i:i + 1], in1=m,
                                                        op0=ALU.is_gt, op1=ALU.subtract))
                    step(nc.vector.tensor_tensor(t[:, :, :, :].rearrange("p k j o -> p (k j) o"),
                                                 w.rearrange("p (a o) -> p a o", o=M),
                                                 s[:, :, :].rearrange("p k j -> p (k j)").unsqueeze(2)
                                                 .broadcast_to([P, K * 8, M]), ALU.mult))

        with Scope(nc, "of2") as sc:
            g_sb, h_sb = sc.sb("g_sb", [P, 2, R]), sc.sb("h_sb", [P, 2, R])
            h_hi, h_lo = sc.sb("h_hi", [P, 2, R], F32R), sc.sb("h_lo", [P, 2, R], F32R)
            gu_ps = sc.ps("gu_ps", [P, 4, 512])
            ps = sc.ps("ps", [P, RT, 512])
            gu_full, g_set, u_read, h_hi_set, h_lo_set, used, done = (
                sc.sem(n) for n in ("gu_full", "g_set", "u_read", "h_hi_set", "h_lo_set", "used", "done"))
            block = sc.block()

            @block.tensor
            def _(pe):
                def down(c):
                    w = width(c)
                    pe.wait_ge(h_lo_set, c + 1)
                    for r in range(RT):
                        rs = slice(r * P, (r + 1) * P)
                        t = tern_d[0:w, c].rearrange("p j o -> p (j o)")
                        nc.tensor.matmul(ps[:, r, :], h_hi[0:w, c % 2, rs], t, start=c == 0, stop=False)
                        end = nc.tensor.matmul(ps[:, r, :], h_lo[0:w, c % 2, rs], t, start=False, stop=c == FC - 1)
                        if c == FC - 1:
                            end.then_inc(done, 1)
                    if c < FC - 1:
                        end.then_inc(used, 1)

                for c in range(FC):
                    w = width(c)
                    for i in range(2):
                        if c >= 2:
                            pe.wait_ge((g_set, u_read)[i], c - 1)
                        flat = tern[i][:, :, :, :].rearrange("p k j o -> p k (j o)")
                        for k in range(KC):
                            o = gu_ps[0:w, 2 * (c % 2) + i, :]
                            t = flat[:, k, c * P:c * P + w]
                            nc.tensor.matmul(o, t, xt_hi[:, k, :], start=k == 0, stop=False)
                            end = nc.tensor.matmul(o, t, xt_lo[:, k, :], start=False, stop=k == KC - 1)
                        end.then_inc(gu_full, 1)
                    if c > 0:
                        down(c - 1)
                down(FC - 1)

            @block.scalar
            def _(act):
                def high(c):
                    w = width(c)
                    act.wait_ge(u_read, c + 1)
                    if c >= 2:
                        act.wait_ge(used, c - 1)
                    nc.scalar.activation(h_hi[0:w, c % 2, :], h_sb[0:w, c % 2, :], ACT.Copy).then_inc(h_hi_set, 1)

                for c in range(FC):
                    w = width(c)
                    act.wait_ge(gu_full, 2 * c + 1)
                    if c >= 2:
                        act.wait_ge(u_read, c - 1)
                    nc.scalar.activation(g_sb[0:w, c % 2, :], gu_ps[0:w, 2 * (c % 2), :], ACT.Silu,
                                         scale=scale[0:w, 0:1]).then_inc(g_set, 1)
                    if c > 0:
                        high(c - 1)
                high(FC - 1)

            @block.vector
            def _(dve):
                def low(c):
                    w = width(c)
                    dve.wait_ge(h_hi_set, c + 1)
                    nc.vector.tensor_tensor(h_lo[0:w, c % 2, :], h_sb[0:w, c % 2, :], h_hi[0:w, c % 2, :].bitcast(F32),
                                            ALU.subtract).then_inc(h_lo_set, 1)

                for c in range(FC):
                    w = width(c)
                    dve.wait_ge(g_set, c + 1)
                    dve.wait_ge(gu_full, 2 * c + 2)
                    if c >= 2:
                        dve.wait_ge(h_lo_set, c - 1)
                    nc.vector.scalar_tensor_tensor(out=h_sb[0:w, c % 2, :], in0=gu_ps[0:w, 2 * (c % 2) + 1, :],
                                                   scalar=scale[0:w, 1:2], in1=g_sb[0:w, c % 2, :],
                                                   op0=ALU.mult, op1=ALU.mult).then_inc(u_read, 1)
                    if c > 0:
                        low(c - 1)
                low(FC - 1)
                for r in range(RT):
                    dve.wait_ge(done, r + 1)
                    nc.vector.scalar_tensor_tensor(out=x_sb[:, r, :], in0=ps[:, r, :], scalar=scale[:, 2:3],
                                                   in1=x_sb[:, r, :], op0=ALU.mult, op1=ALU.add)


def attention_constants(L, HD):
    step = np.arange(P) % L
    angle = step.astype(np.float32)
    return {
        "rotary": np.stack([np.cos(angle), np.sin(angle), -np.sin(angle)], 1),
        "head_mask": (np.arange(P)[:, None] // HD == np.arange(P // HD)).astype(np.float32),
        "causal": np.where(np.arange(L) <= step[:, None], np.float32(0), np.float32(-1e30)),
    }


def octonion_terms():
    s = np.zeros((8, 8, 8), np.float32)
    s[0, 0, 0] = 1
    for i in range(1, 8):
        s[0, i, i] = s[i, 0, i] = 1
        s[i, i, 0] = -1
    for a, b, c in [(1, 2, 3), (1, 4, 5), (1, 7, 6), (2, 4, 6), (2, 5, 7), (3, 4, 7), (3, 6, 5)]:
        for x, y, z in ((a, b, c), (b, c, a), (c, a, b)):
            s[x, y, z], s[y, x, z] = 1, -1
    return np.abs(s).argmax(0), s.sum(0)


def perceiver(nc, x, ctx, ctx_t, identity, xa, ma, fl, sa, of, out):
    B = ctx.shape[0]
    _, RT, H = x.shape
    R = RT * P
    NKV = xa["wk"].shape[0]
    GL = xa["wq"].shape[3] * (R // B) // P
    q_dram = nc.dram_tensor("q_scratch", (B, NKV, P, GL), F32, kind="Internal").ap()
    o_dram = nc.dram_tensor("o_scratch", (B, NKV, P, GL), F32, kind="Internal").ap()
    c_dram = nc.dram_tensor("c_scratch", (B, R // B, H), F32, kind="Internal").ap()
    with Scope(nc, "all") as sc:
        x_sb, ident, ones = sc.sb("x", [P, RT, H]), sc.sb("ident", [P, P]), sc.sb("ones", [P, P])
        x_in, x_out = sc.sem("x_in"), sc.sem("x_out")
        with nc.Block() as block:
            @block.gpsimd
            def _(pool):
                nc.gpsimd.memset(ones[:, :], 1.0)

            @block.sync
            def _(sp):
                sp.dma_start(x_sb[:, :, :], x).then_inc(x_in, 16)
                sp.dma_start(ident[:, :], identity).then_inc(x_in, 16)
                sp.wait_ge(x_in, 32)

        def normalised(name, stage):
            with Scope(nc, name) as s:
                xt_hi, xt_lo = s.sb("xt_hi", [P, H // P, R], F32R), s.sb("xt_lo", [P, H // P, R], F32R)
                layernorm_transposed(nc, f"{name}_ln", x_sb, xt_hi, xt_lo, ident)
                stage(xt_hi, xt_lo)

        normalised("n0", lambda hi, lo: queries(nc, hi, lo, xa["wq"], xa["bq"], q_dram))
        cross_attention(nc, ctx_t, xa["wk"], xa["wv"], xa["bk"], xa["bv"], ident, q_dram, o_dram)
        attention_output(nc, x_sb, o_dram, xa["wo"], xa["bo"])
        mamba(nc, x_sb, ident, B, **ma)
        normalised("n2", lambda hi, lo: ternary_linear(nc, x_sb, hi, lo, fl["w"], fl["bias"], ones))
        normalised("n3", lambda hi, lo: context_attention(nc, x_sb, hi, lo, ctx, ident, c_dram))
        normalised("n4", lambda hi, lo: self_attention(nc, x_sb, hi, lo, sa["w_qkv"], sa["w_o"], sa["rotary"],
                                                       sa["head_mask"], sa["causal"], ident, B, 32))
        normalised("n5", lambda hi, lo: octonion_ffn(nc, x_sb, hi, lo, of["w_gate"], of["w_up"], of["w_down"],
                                                     of["sign_in"], of["sign_down"], ones))
        with nc.Block() as block:
            @block.sync
            def _(sp):
                sp.dma_start(out, x_sb[:, :, :]).then_inc(x_out, 16)
                sp.wait_ge(x_out, 16)


def kernel(**inputs):
    import numpy as np
    import concourse.bacc as bacc
    from concourse.bass_utils import run_bass_kernel_spmd

    def lay(a):
        return np.ascontiguousarray(a)

    def rows(w, shape=None):
        w = np.asarray(w)
        return lay(w.reshape(-1, P, *w.shape[1:]).swapaxes(0, 1))

    i = {k: np.asarray(v) for k, v in inputs.items()}
    B, L, H = i["x"].shape
    S = i["ctx_4096"].shape[1]
    NKV, D, NH = 8, 128, 32
    G = NH // NKV
    KD = NKV * D
    wkv = i["L0_xattn_Wkv"]
    pick, sign = octonion_terms()
    O, D8 = i["L1_ffn_w_gate"].shape[1:]
    F = 8 * O
    FC = -(-F // P)

    def octonion(w):
        return w[pick].transpose(0, 3, 1, 2).reshape(-1, 8, w.shape[1])

    def padded(w):
        out = np.zeros((FC * P, *w.shape[1:]), w.dtype)
        out[:F] = w
        return out

    groups = {
        "xa": {
            "wq": lay(i["L0_xattn_Wq"].reshape(H // P, P, NKV, G * D).transpose(2, 1, 0, 3)),
            "bq": lay(i["L0_xattn_bq"].reshape(NH, D).T),
            "wk": lay(wkv[:, :KD].reshape(H // P, P, NKV, D).transpose(2, 1, 0, 3)),
            "wv": lay(wkv[:, KD:].reshape(H // P, P, NKV // 2, 2 * D).transpose(2, 1, 0, 3)),
            "bk": lay(i["L0_xattn_bkv"][:KD].reshape(NKV, D).T),
            "bv": lay(i["L0_xattn_bkv"][KD:].reshape(NKV, D).T),
            "wo": lay(i["L0_xattn_Wo"].reshape(NKV, G, D, H).transpose(0, 2, 1, 3)),
            "bo": lay(i["L0_xattn_bo"]),
        },
        "ma": {
            "w_in": lay(i["L0_attn_W_in"].T.reshape(H // P, P, 2, -1, P).transpose(3, 1, 2, 0, 4)),
            "conv_w": rows(i["L0_attn_conv_w"]),
            "conv_b": rows(i["L0_attn_conv_b"]),
            "w_x": rows(i["L0_attn_W_x"].T),
            "w_dt": lay(i["L0_attn_W_dt"].T),
            "b_dt": rows(i["L0_attn_b_dt"]),
            "a_log": rows(i["L0_attn_A_log"]),
            "d_skip": rows(i["L0_attn_D"]),
            "w_out": rows(i["L0_attn_W_out"].T),
        },
        "fl": {"w": rows(i["L0_ffn_weight"].T), "bias": lay(i["L0_ffn_bias"])},
        "sa": {
            "w_qkv": np.stack([rows(i[f"L1_attn_w{n}"].T) for n in "qkv"]),
            "w_o": rows(i["L1_attn_wo"].T),
            **attention_constants(L, H // NH),
        },
        "of": {
            "w_gate": rows(octonion(i["L1_ffn_w_gate"])),
            "w_up": rows(octonion(i["L1_ffn_w_up"])),
            "w_down": rows(padded(octonion(i["L1_ffn_w_down"]))),
            "sign_in": rows(np.repeat(sign, D8, 0)),
            "sign_down": rows(padded(np.repeat(sign, O, 0))),
        },
    }
    alone = {
        "x": rows(i["x"].reshape(B * L, H)),
        "ctx": lay(i["ctx_4096"]),
        "ctx_t": lay(i["ctx_4096"].transpose(0, 2, 1).reshape(B, H // P, P, S).swapaxes(1, 2)),
        "identity": np.eye(P, dtype=np.float32),
    }

    nc = bacc.Bacc("TRN2", target_bir_lowering=False, num_devices=1)
    arrays = {}

    def given(name, a):
        arrays[f"in_{name}"] = a
        return nc.dram_tensor(f"in_{name}", a.shape, mybir.dt.from_np(a.dtype), kind="ExternalInput").ap()

    args = {n: given(n, a) for n, a in alone.items()}
    args |= {g: {n: given(f"{g}_{n}", a) for n, a in m.items()} for g, m in groups.items()}
    out = nc.dram_tensor("out", alone["x"].shape, F32, kind="ExternalOutput").ap()
    perceiver(nc, out=out, **args)
    r = run_bass_kernel_spmd(nc, [arrays], core_ids=[0])
    return np.asarray(r.results[0]["out"]).swapaxes(0, 1).reshape(B, L, H)
```

```python
from contextlib import ExitStack

import numpy as np
import concourse.bass as bass
from concourse import mybir
from concourse.alu_op_type import AluOpType as ALU

F32 = mybir.dt.float32
F32R = mybir.dt.float32r
ACT = mybir.ActivationFunctionType
AX_X = mybir.AxisListType.X
P = 128


class Scope:

    def __init__(self, nc, name):
        self.nc, self.name, self.stack, self.sems = nc, name, ExitStack(), []

    def __enter__(self):
        self.stack.__enter__()
        return self

    def __exit__(self, *a):
        self.stack.__exit__(*a)
        if self.sems:
            self.nc.clear_and_free_semaphores(self.sems)
            self.nc.all_engine_barrier()

    def sb(self, name, shape, dt=F32):
        return self.stack.enter_context(self.nc.sbuf_tensor(f"{self.name}_{name}", shape, dt))

    def ps(self, name, shape):
        return self.stack.enter_context(self.nc.psum_tensor(f"{self.name}_{name}", shape, F32))

    def sem(self, name):
        self.sems.append(self.nc.alloc_semaphore(f"{self.name}_{name}"))
        return self.sems[-1]

    def block(self):
        return self.stack.enter_context(self.nc.Block())


def apart(eng, passed):
    eng.sem_inc(passed, 1)


def product(nc, out, left, right, first, last):
    nc.tensor.matmul(out, left[0], right[0], start=first, stop=False)
    nc.tensor.matmul(out, left[0], right[1], start=False, stop=False)
    return nc.tensor.matmul(out, left[1], right[0], start=False, stop=last)


def even_tiles(n, most=512):
    count = -(-n // most)
    step = -(-n // (2 * count)) * 2
    return [(c, min(step, n - c)) for c in range(0, n, step)]


def cross_attention(nc, ctx_t, wk, wv, bk, bv, ident, q_dram, o_dram):
    B, _, KC, S = ctx_t.shape
    NKV = wk.shape[0]
    D = wk.shape[3]
    NQ = q_dram.shape[3]
    NU = NQ // P
    SE = S + S % 2
    NC = -(-S // P)
    NG = -(-NC // 2)
    TILES = even_tiles(SE)
    NT = len(TILES)
    SCALE = float(D) ** -0.5
    NPT = 2
    LO_DVE = 1

    def rows(c):
        return min(P, S - c * P)

    KV_TILES = NKV * NT + NKV // 2 * NG
    S_TILES = NKV * NU * NT
    PAIRS = NKV * NG

    def kv_tile(j):
        return j * NT + (j + 1) // 2 * NG

    def projections(b, j, last):
        tiles = []
        if j % 2 == 0:
            tiles += [("v", j, g, kv_tile(j) + NT + g) for g in range(NG)]
        if not (last and j == NKV - 1):
            tiles += [("k", j + 1, t, kv_tile(j + 1) + t) for t in range(NT)]
        return tiles

    def kv_done(b, tiles):
        return b * KV_TILES + tiles + KV_TILES

    def drive(eng, first, group, tail):
        first()
        with eng.Fori(0, B - 1) as b:
            for j in range(1, NKV + 1):
                group(b, j, False)
        for j in range(1, NKV):
            group(B - 1, j, True)
        tail(B - 1)

    with Scope(nc, "xa") as sc:
        raw = sc.sb("ctx_raw", [P, KC, SE])
        ctx_hi, ctx_lo = sc.sb("ctx_hi", [P, KC, SE], F32R), sc.sb("ctx_lo", [P, KC, SE], F32R)
        wk_raw = sc.sb("wk_raw", [P, 2, KC, D])
        wk_hi, wk_lo = sc.sb("wk_hi", [P, 2, KC, D], F32R), sc.sb("wk_lo", [P, 2, KC, D], F32R)
        wv_raw = sc.sb("wv_raw", [P, KC, 2 * D])
        wv_hi, wv_lo = sc.sb("wv_hi", [P, KC, 2 * D], F32R), sc.sb("wv_lo", [P, KC, 2 * D], F32R)
        q_raw = sc.sb("q_raw", [P, 2, NQ])
        q_hi, q_lo = sc.sb("q_hi", [P, 2, NQ], F32R), sc.sb("q_lo", [P, 2, NQ], F32R)
        k_hi, k_lo = sc.sb("k_hi", [P, SE], F32R), sc.sb("k_lo", [P, SE], F32R)
        v_hi, v_lo = sc.sb("v_hi", [P, NC, 2 * D], F32R), sc.sb("v_lo", [P, NC, 2 * D], F32R)
        prob = sc.sb("prob", [P, 2, NU, SE])
        pt_hi, pt_lo = sc.sb("pt_hi", [P, NPT, 2, NQ], F32R), sc.sb("pt_lo", [P, NPT, 2, NQ], F32R)
        tmax = sc.sb("tmax", [P, NU, NT])
        nmax = sc.sb("nmax", [P, NU])
        den = sc.sb("den", [P, NU])
        rden = sc.sb("rden", [P, NU])
        o_sb = sc.sb("o_sb", [P, 2, NQ])
        bk_sb, bv_sb = sc.sb("bk_sb", [P, NKV]), sc.sb("bv_sb", [P, NKV])
        kv_ps = sc.ps("kv_ps", [P, 2, 512])
        s_ps = sc.ps("s_ps", [P, 2, 512])
        t_ps = sc.ps("t_ps", [P, 2, 512])
        o_ps = sc.ps("o_ps", [P, 2, 512])

        bias_in = sc.sem("bias_in")
        ctx_in = [sc.sem(f"ctx_in{t}") for t in range(NT)]
        wk_in = [sc.sem(f"wk_in{i}") for i in range(2)]
        wv_in = sc.sem("wv_in")
        q_in = [sc.sem(f"q_in{i}") for i in range(2)]
        pad_set = sc.sem("pad_set")
        passed = sc.sem("passed")
        ctx_hi_set = sc.sem("ctx_hi_set")
        ctx_lo_dve, ctx_lo_pool = sc.sem("ctx_lo_dve"), sc.sem("ctx_lo_pool")
        w_hi_set = sc.sem("w_hi_set")
        wk_split, wv_split, q_split = sc.sem("wk_split"), sc.sem("wv_split"), sc.sem("q_split")
        kv_full, kv_hi, kv_free = sc.sem("kv_full"), sc.sem("kv_hi"), sc.sem("kv_free")
        s_full, s_free = sc.sem("s_full"), sc.sem("s_free")
        nmax_set, exp_done, rden_set, prob_set = (
            sc.sem("nmax_set"), sc.sem("exp_done"), sc.sem("rden_set"), sc.sem("prob_set"))
        t_full, t_hi, t_free = sc.sem("t_full"), sc.sem("t_hi"), sc.sem("t_free")
        pt_free = sc.sem("pt_free")
        o_full, o_free = sc.sem("o_full"), sc.sem("o_free")
        o_out = [sc.sem(f"o_out{i}") for i in range(2)]
        block = sc.block()

        @block.sync
        def _(sp):
            def load_ctx(b):
                for t, (c, w) in enumerate(TILES):
                    w = min(w, S - c)
                    sp.dma_start(raw[:, :, c:c + w], ctx_t[b][:, :, c:c + w]).then_inc(ctx_in[t], 16)

            def group(b, j, last):
                n = b * NKV + j
                g = j % NKV
                sp.wait_ge(wk_split, n + 1)
                sp.dma_start(wk_raw[:, j % 2], wk[g]).then_inc(wk_in[j % 2], 16)
                sp.wait_ge(q_split, n + 1)
                sp.dma_start(q_raw[:, j % 2], q_dram[b + j // NKV, g]).then_inc(q_in[j % 2], 16)
                if j % 2 == 0:
                    sp.wait_ge(wv_split, b * (NKV // 2) + j // 2 + 1)
                    sp.dma_start(wv_raw[:, :, :], wv[g // 2]).then_inc(wv_in, 16)
                if j == 2 and not last:
                    sp.wait_ge(ctx_lo_dve, b * LO_DVE + LO_DVE)
                    sp.wait_ge(ctx_lo_pool, b * (NT - LO_DVE) + NT - LO_DVE)
                    load_ctx(b + 1)

            def first():
                group(0, 0, False)
                load_ctx(0)
                sp.dma_start(bk_sb[:, :], bk).then_inc(bias_in, 16)
                sp.dma_start(bv_sb[:, :], bv).then_inc(bias_in, 16)

            drive(sp, first, group, lambda b: None)

        @block.gpsimd
        def _(pool):
            def halves(hi, lo, src, count):
                apart(pool, passed)
                nc.gpsimd.tensor_scalar(hi, src, 1.0, 1.0, ALU.mult, ALU.mult).then_inc(w_hi_set, 1)
                pool.wait_ge(w_hi_set, count)
                return nc.gpsimd.tensor_tensor(lo, src, hi.bitcast(F32), ALU.subtract)

            def split_ctx(b, n):
                for t, (c, w) in enumerate(TILES):
                    pool.wait_ge(ctx_in[t], (n + 1) * 16)
                    if b is not None:
                        pool.wait_ge(kv_full, kv_done(b, kv_tile(NKV - 1) + t + 1))
                        apart(pool, passed)
                    nc.gpsimd.tensor_scalar(ctx_hi[:, :, c:c + w], raw[:, :, c:c + w], 1.0, 1.0,
                                            ALU.mult, ALU.mult).then_inc(ctx_hi_set, 1)
                for t, (c, w) in enumerate(TILES):
                    if t >= LO_DVE:
                        pool.wait_ge(ctx_hi_set, n * NT + t + 1)
                        nc.gpsimd.tensor_tensor(ctx_lo[:, :, c:c + w], raw[:, :, c:c + w],
                                                ctx_hi[:, :, c:c + w].bitcast(F32),
                                                ALU.subtract).then_inc(ctx_lo_pool, 1)

            def weights(b, j):
                k = b * (2 * NKV + NKV // 2) + 2 * j + (j + 1) // 2
                pool.wait_ge(wk_in[j % 2], (b * (NKV // 2) + j // 2 + 1) * 16)
                pool.wait_ge(kv_full, kv_done(b, kv_tile(j - 2) + NT))
                halves(wk_hi[:, j % 2], wk_lo[:, j % 2], wk_raw[:, j % 2], k + 1).then_inc(wk_split, 1)
                pool.wait_ge(q_in[j % 2], (b * (NKV // 2) + j // 2 + 1) * 16)
                pool.wait_ge(s_full, b * S_TILES + (j - 1) * NU * NT + S_TILES)
                halves(q_hi[:, j % 2], q_lo[:, j % 2], q_raw[:, j % 2], k + 2).then_inc(q_split, 1)
                if j % 2 == 0:
                    pool.wait_ge(wv_in, (b * (NKV // 2) + j // 2 + 1) * 16)
                    pool.wait_ge(kv_full, kv_done(b, kv_tile(j - 2) + NT + NG))
                    halves(wv_hi[:, :, :], wv_lo[:, :, :], wv_raw[:, :, :], k + 3).then_inc(wv_split, 1)

            def first():
                pool.sem_inc(wk_split, 2)
                pool.sem_inc(q_split, 2)
                pool.sem_inc(wv_split, 1)
                nc.gpsimd.memset(raw[:, :, SE - 1:SE], 0.0).then_inc(pad_set, 1)
                pool.wait_ge(pad_set, 1)
                weights(0, 0)
                split_ctx(None, 0)

            def group(b, j, last):
                weights(b, j)
                if j == NKV:
                    split_ctx(b, b + 1)

            drive(pool, first, group, lambda b: None)

        @block.tensor
        def _(pe):
            pe.sem_inc(kv_full, KV_TILES)
            pe.sem_inc(s_full, S_TILES)
            pe.sem_inc(pt_free, NPT)

            def key_tile(b, j, t, n):
                c, w = TILES[t]
                if t == 0:
                    pe.wait_ge(wk_split, b * NKV + j + 3)
                if j % NKV == 0:
                    at = b + j // NKV
                    pe.wait_ge(ctx_hi_set, at * NT + t + 1)
                    if t < LO_DVE:
                        pe.wait_ge(ctx_lo_dve, at * LO_DVE + t + 1)
                    else:
                        pe.wait_ge(ctx_lo_pool, at * (NT - LO_DVE) + t + 1 - LO_DVE)
                pe.wait_ge(kv_free, b * KV_TILES + n + 1)
                for kc in range(KC):
                    end = product(nc, kv_ps[:, n % 2, 0:w],
                                  (wk_hi[:, j % 2, kc], wk_lo[:, j % 2, kc]),
                                  (ctx_hi[:, kc, c:c + w], ctx_lo[:, kc, c:c + w]), kc == 0, kc == KC - 1)
                end.then_inc(kv_full, 1)

            def value_tile(b, j, g, n):
                if g == 0:
                    pe.wait_ge(wv_split, b * (NKV // 2) + j // 2 + 2)
                pe.wait_ge(kv_free, b * KV_TILES + n + 1)
                for c in range(2 * g, min(2 * g + 2, NC)):
                    for kc in range(KC):
                        s = slice(c * P, c * P + rows(c))
                        o = (c % 2) * 2 * D
                        end = product(nc, kv_ps[0:rows(c), n % 2, o:o + 2 * D],
                                      (ctx_hi[:, kc, s], ctx_lo[:, kc, s]),
                                      (wv_hi[:, kc, :], wv_lo[:, kc, :]), kc == 0, kc == KC - 1)
                end.then_inc(kv_full, 1)

            def project(b, j, last):
                for kind, at, t, n in projections(b, j, last):
                    (key_tile if kind == "k" else value_tile)(b, at, t, n)

            def score_tile(b, j, i):
                u, t = divmod(i, NT)
                c, w = TILES[t]
                n = j * NU * NT + i
                if i == 0:
                    pe.wait_ge(q_split, b * NKV + j + 3)
                if u == 0:
                    pe.wait_ge(kv_free, b * KV_TILES + kv_tile(j) + t + 3)
                pe.wait_ge(s_free, b * S_TILES + n + 1)
                us = slice(u * P, (u + 1) * P)
                product(nc, s_ps[:, n % 2, 0:w], (q_hi[:, j % 2, us], q_lo[:, j % 2, us]),
                        (k_hi[:, c:c + w], k_lo[:, c:c + w]), True, True).then_inc(s_full, 1)

            def transposes(b, j, g):
                n = j * NG + g
                if g == 0:
                    pe.wait_ge(prob_set, b * (NKV * NU) + j * NU + NU)
                pe.wait_ge(t_free, b * PAIRS + n + 1)
                for c in range(2 * g, min(2 * g + 2, NC)):
                    r = rows(c)
                    for u in range(NU):
                        o = (c % 2) * NQ + u * P
                        end = nc.tensor.transpose(t_ps[0:r, n % 2, o:o + P],
                                                  prob[:, j % 2, u, c * P:c * P + r], ident[:, :])
                end.then_inc(t_full, 1)

            def pv(b, j, g):
                n = j * NG + g
                if g == 0:
                    pe.wait_ge(o_free, b * NKV + j + 1)
                pe.wait_ge(t_free, b * PAIRS + n + 3)
                for c in range(2 * g, min(2 * g + 2, NC)):
                    r = rows(c)
                    d = slice((j % 2) * D, (j % 2 + 1) * D)
                    end = product(nc, o_ps[:, j % 2, 0:NQ], (v_hi[0:r, c, d], v_lo[0:r, c, d]),
                                  (pt_hi[0:r, n % NPT, c % 2], pt_lo[0:r, n % NPT, c % 2]), c == 0, c == NC - 1)
                end.then_inc(pt_free, 1)

            def first():
                for t in range(NT):
                    key_tile(0, 0, t, t)
                for i in range(NU * NT):
                    score_tile(0, 0, i)
                project(0, 0, False)

            def group(b, j, last):
                for i in range(max(NU * NT, NG)):
                    if i < NU * NT:
                        score_tile(b, j, i)
                    if 2 <= i < NG + 2:
                        pv(b, j - 1, i - 2)
                    if i < NG:
                        transposes(b, j - 1, i)
                for g in range(max(NU * NT, NG) - 2, NG):
                    pv(b, j - 1, g)
                project(b, j, last)

            def tail(b):
                for i in range(NG + 1):
                    if i < NG:
                        transposes(b, NKV - 1, i)
                    if i > 0:
                        pv(b, NKV - 1, i - 1)

            drive(pe, first, group, tail)

        @block.scalar
        def _(act):
            def key_tile(b, j, t, n):
                c, w = TILES[t]
                act.wait_ge(kv_full, kv_done(b, n + 1))
                nc.scalar.activation(k_hi[:, c:c + w], kv_ps[:, n % 2, 0:w], ACT.Identity,
                                     bias=bk_sb[:, j % NKV:j % NKV + 1]).then_inc(kv_hi, 1)

            def value_tile(b, j, g, n):
                act.wait_ge(kv_full, kv_done(b, n + 1))
                m = min(2, NC - 2 * g)
                r = rows(2 * g)
                nc.scalar.activation(v_hi[0:r, 2 * g:2 * g + m, :],
                                     kv_ps[0:r, n % 2, 0:m * 2 * D].rearrange("p (c d) -> p c d", c=m),
                                     ACT.Copy).then_inc(kv_hi, 1)

            def exponentials(b, j, u):
                act.wait_ge(nmax_set, b * (NKV * NU) + j * NU + u + 1)
                nc.scalar.activation(prob[:, j % 2, u, 0:S], prob[:, j % 2, u, 0:S], ACT.Exp, bias=nmax[:, u:u + 1],
                                     accum_out=den[:, u:u + 1]).then_inc(exp_done, 1)

            def softmax_and_project(b, j, last):
                exponentials(b, j, 0)
                tiles = projections(b, j, last)
                for i, (kind, at, t, n) in enumerate(tiles):
                    (key_tile if kind == "k" else value_tile)(b, at, t, n)
                    if 0 <= i < NU - 1:
                        exponentials(b, j, i + 1)
                if not tiles:
                    for u in range(1, NU):
                        exponentials(b, j, u)

            def attend(b, j):
                for g in range(NG):
                    n = j * NG + g
                    m = min(2, NC - 2 * g)
                    r = rows(2 * g)
                    act.wait_ge(t_full, b * PAIRS + n + 1)
                    act.wait_ge(pt_free, b * PAIRS + n + 1)
                    nc.scalar.activation(pt_hi[0:r, n % NPT, 0:m, :],
                                         t_ps[0:r, n % 2, 0:m * NQ].rearrange("p (c d) -> p c d", c=m),
                                         ACT.Copy).then_inc(t_hi, 1)
                act.wait_ge(pt_free, b * PAIRS + (j + 1) * NG + NPT)
                act.wait_ge(o_out[j % 2], (b * (NKV // 2) + j // 2 + 1) * 16)
                nc.scalar.activation(o_sb[:, j % 2], o_ps[:, j % 2, 0:NQ], ACT.Identity,
                                     bias=bv_sb[:, j:j + 1]).then_inc(o_free, 1)
                act.wait_ge(o_free, b * NKV + j + 3)
                act.dma_start(o_dram[b, j], o_sb[:, j % 2]).then_inc(o_out[j % 2], 16)

            def first():
                act.sem_inc(o_free, 2)
                act.sem_inc(o_out[0], 16)
                act.sem_inc(o_out[1], 16)
                act.wait_ge(bias_in, 32)
                for t in range(NT):
                    key_tile(0, 0, t, t)
                softmax_and_project(0, 0, False)

            def group(b, j, last):
                attend(b, j - 1)
                softmax_and_project(b, j, last)

            drive(act, first, group, lambda b: attend(b, NKV - 1))
            for i in range(2):
                act.wait_ge(o_out[i], (B * NKV // 2 + 1) * 16)

        @block.vector
        def _(dve):
            def split_ctx(b, t, kc):
                c, w = TILES[t]
                dve.wait_ge(ctx_hi_set, b * NT + t + 1)
                end = nc.vector.tensor_tensor(ctx_lo[:, kc, c:c + w], raw[:, kc, c:c + w],
                                              ctx_hi[:, kc, c:c + w].bitcast(F32), ALU.subtract)
                if kc == KC - 1:
                    end.then_inc(ctx_lo_dve, 1)

            def key_tile(b, j, t, n):
                c, w = TILES[t]
                dve.wait_ge(kv_hi, b * KV_TILES + n + 1)
                nc.vector.scalar_tensor_tensor(
                    out=k_lo[:, c:c + w], in0=kv_ps[:, n % 2, 0:w], scalar=bk_sb[:, j % NKV:j % NKV + 1],
                    in1=k_hi[:, c:c + w].bitcast(F32), op0=ALU.add, op1=ALU.subtract).then_inc(kv_free, 1)

            def value_tile(b, j, g, n):
                m = min(2, NC - 2 * g)
                r = rows(2 * g)
                dve.wait_ge(kv_hi, b * KV_TILES + n + 1)
                nc.vector.tensor_tensor(v_lo[0:r, 2 * g:2 * g + m, :],
                                        kv_ps[0:r, n % 2, 0:m * 2 * D].rearrange("p (c d) -> p c d", c=m),
                                        v_hi[0:r, 2 * g:2 * g + m, :].bitcast(F32),
                                        ALU.subtract).then_inc(kv_free, 1)

            def score_tile(b, j, i):
                u, t = divmod(i, NT)
                c, w = TILES[t]
                w = min(w, S - c)
                n = j * NU * NT + i
                dve.wait_ge(s_full, b * S_TILES + n + 1 + S_TILES)
                nc.vector.tensor_scalar(prob[:, j % 2, u, c:c + w], s_ps[:, n % 2, 0:w], SCALE, None,
                                        ALU.mult, ALU.max,
                                        accum_out=tmax[:, u, t:t + 1]).then_inc(s_free, 1)
                if t == NT - 1:
                    dve.wait_ge(s_free, b * S_TILES + (j * NU + u + 1) * NT + 2)
                    nc.vector.tensor_reduce(nmax[:, u:u + 1], tmax[:, u, :], AX_X, ALU.max,
                                            negate=True).then_inc(nmax_set, 1)

            def normalise(b, j, u):
                n = b * (NKV * NU) + j * NU + u + 1
                dve.wait_ge(exp_done, n)
                nc.vector.reciprocal(rden[:, u:u + 1], den[:, u:u + 1]).then_inc(rden_set, 1)
                dve.wait_ge(rden_set, n)
                nc.vector.tensor_scalar(prob[:, j % 2, u, 0:S], prob[:, j % 2, u, 0:S], rden[:, u:u + 1], None,
                                        ALU.mult).then_inc(prob_set, 1)

            def low_transposed(b, j, g):
                n = j * NG + g
                m = min(2, NC - 2 * g)
                r = rows(2 * g)
                dve.wait_ge(t_hi, b * PAIRS + n + 1)
                nc.vector.tensor_tensor(pt_lo[0:r, n % NPT, 0:m, :],
                                        t_ps[0:r, n % 2, 0:m * NQ].rearrange("p (c d) -> p c d", c=m),
                                        pt_hi[0:r, n % NPT, 0:m, :].bitcast(F32),
                                        ALU.subtract).then_inc(t_free, 1)

            def softmax_and_project(b, j, last):
                normalise(b, j, 0)
                tiles = projections(b, j, last)
                for i, (kind, at, t, n) in enumerate(tiles):
                    (key_tile if kind == "k" else value_tile)(b, at, t, n)
                    if 1 <= i < NU:
                        normalise(b, j, i)
                if not tiles:
                    for u in range(1, NU):
                        normalise(b, j, u)

            def first():
                dve.sem_inc(kv_free, 2)
                dve.sem_inc(s_free, 2)
                dve.sem_inc(t_free, 2)
                for t in range(LO_DVE):
                    for kc in range(KC):
                        split_ctx(0, t, kc)
                dve.wait_ge(bias_in, 32)
                for t in range(NT):
                    key_tile(0, 0, t, t)
                for i in range(NU * NT):
                    score_tile(0, 0, i)
                softmax_and_project(0, 0, False)

            def group(b, j, last):
                ctx_steps = [(t, kc) for t in range(LO_DVE) for kc in range(KC)]
                for i in range(max(NU * NT, NG)):
                    if i < NU * NT:
                        score_tile(b, j, i)
                    if i < NG:
                        low_transposed(b, j - 1, i)
                    if j == NKV - 1 and not last and i % 2 == 1 and ctx_steps:
                        split_ctx(b + 1, *ctx_steps.pop(0))
                if j == NKV - 1 and not last:
                    for t, kc in ctx_steps:
                        split_ctx(b + 1, t, kc)
                softmax_and_project(b, j, last)

            def tail(b):
                for g in range(NG):
                    low_transposed(b, NKV - 1, g)

            drive(dve, first, group, tail)


class Chain:

    def __init__(self, eng, sem, start=0):
        self.eng, self.sem, self.count = eng, sem, start

    def __call__(self, ins):
        self.count += 1
        ins.then_inc(self.sem, 1)
        self.eng.wait_ge(self.sem, self.count)


def layernorm_transposed(nc, name, x_sb, xt_hi, xt_lo, ident, eps=1e-5):
    _, RT, H = x_sb.shape
    KC = H // P
    with Scope(nc, name) as sc:
        xn = sc.sb("xn", [P, RT, H])
        stats = sc.sb("stats", [P, RT, 6])
        mv = sc.sb("mv", [P, RT, 2])
        std = sc.sb("std", [P, RT])
        rstd = sc.sb("rstd", [P, RT])
        eps_sb = sc.sb("eps", [P, 1])
        t_ps = sc.ps("t_ps", [P, RT, 512])
        own, var_set, std_set, xn_set, t_full, hi_set = (
            sc.sem(n) for n in ("own", "var_set", "std_set", "xn_set", "t_full", "hi_set"))
        block = sc.block()

        @block.vector
        def _(dve):
            step = Chain(dve, own)
            nc.vector.memset(eps_sb[:, :], eps).then_inc(own, 1)
            step.count = 1
            for r in range(RT):
                step(nc.vector.bn_stats(stats[:, r, :], x_sb[:, r, :]))
                nc.vector.bn_aggr(mv[:, r, :], stats[:, r, :]).then_inc(var_set, 1)
            for r in range(RT):
                dve.wait_ge(std_set, r + 1)
                step(nc.vector.reciprocal(rstd[:, r:r + 1], std[:, r:r + 1]))
                nc.vector.tensor_scalar(xn[:, r, :], x_sb[:, r, :], mv[:, r, 0:1], rstd[:, r:r + 1],
                                        ALU.subtract, ALU.mult).then_inc(xn_set, 1)
            for r in range(RT):
                dve.wait_ge(hi_set, r + 1)
                out = xt_lo[:, :, r * P:(r + 1) * P]
                nc.vector.tensor_tensor(out, t_ps[:, r, :].rearrange("p (k c) -> p k c", k=KC),
                                        xt_hi[:, :, r * P:(r + 1) * P].bitcast(F32), ALU.subtract)

        @block.scalar
        def _(act):
            for r in range(RT):
                act.wait_ge(var_set, r + 1)
                nc.scalar.activation(std[:, r:r + 1], mv[:, r, 1:2], ACT.Sqrt, bias=eps_sb[:, 0:1]).then_inc(std_set, 1)
            for r in range(RT):
                act.wait_ge(t_full, r + 1)
                nc.scalar.activation(xt_hi[:, :, r * P:(r + 1) * P],
                                     t_ps[:, r, :].rearrange("p (k c) -> p k c", k=KC),
                                     ACT.Copy).then_inc(hi_set, 1)

        @block.tensor
        def _(pe):
            for r in range(RT):
                pe.wait_ge(xn_set, r + 1)
                for k in range(KC):
                    end = nc.tensor.transpose(t_ps[:, r, k * P:(k + 1) * P], xn[:, r, k * P:(k + 1) * P], ident[:, :])
                end.then_inc(t_full, 1)


def queries(nc, xt_hi, xt_lo, wq, bq, q_dram):
    NKV, _, KC, GD = wq.shape
    D = P
    G = GD // D
    B = q_dram.shape[0]
    R = xt_hi.shape[2]
    with Scope(nc, "q") as sc:
        raw = sc.sb("raw", [P, 2, KC, GD])
        w_hi, w_lo = sc.sb("w_hi", [P, 2, KC, GD], F32R), sc.sb("w_lo", [P, 2, KC, GD], F32R)
        bq_sb = sc.sb("bq_sb", [P, NKV * G])
        q_sb = sc.sb("q_sb", [P, 2, B, G, R // B])
        q_ps = sc.ps("q_ps", [P, 4, 512])
        bias_in = sc.sem("bias_in")
        w_in = [sc.sem(f"w_in{i}") for i in range(2)]
        w_hi_set, w_lo_set = sc.sem("w_hi_set"), sc.sem("w_lo_set")
        q_full, q_set = sc.sem("q_full"), sc.sem("q_set")
        q_out = [sc.sem(f"q_out{i}") for i in range(2)]
        block = sc.block()

        @block.sync
        def _(sp):
            sp.dma_start(bq_sb[:, :], bq).then_inc(bias_in, 16)
            with sp.Fori(0, NKV // 2) as h:
                j0 = 2 * h
                for i in range(2):
                    sp.wait_ge(w_lo_set, j0 + i + 1)
                    sp.dma_start(raw[:, i], wq[j0 + i]).then_inc(w_in[i], 16)

        def evacuate(act, j0, i):
            act.wait_ge(q_out[i], (j0 + 2) * 8)
            for g in range(G):
                n = (j0 + i) * G + g
                act.wait_ge(q_full, n + 1 + 2 * G)
                nc.scalar.activation(q_sb[:, i, :, g, :], q_ps[:, g, :].rearrange("p (b l) -> p b l", b=B),
                                     ACT.Identity, bias=bq_sb[:, bass.ds(n, 1)]).then_inc(q_set, 1)
            act.wait_ge(q_set, (j0 + i + 1) * G + G)
            act.dma_start(q_dram[:, j0 + i].rearrange("b d n -> d b n"),
                          q_sb[:, i].rearrange("p b g l -> p b (g l)")).then_inc(q_out[i], 16)

        @block.scalar
        def _(act):
            act.sem_inc(q_out[0], 16)
            act.sem_inc(q_out[1], 16)
            act.wait_ge(bias_in, 16)
            def weights(j0, i):
                act.wait_ge(w_in[i], (j0 + 2) * 8)
                act.wait_ge(q_full, (j0 + i + 1) * G)
                nc.scalar.activation(w_hi[:, i], raw[:, i], ACT.Copy).then_inc(w_hi_set, 1)

            weights(0, 0)
            weights(0, 1)
            with act.Fori(0, NKV // 2 - 1) as h:
                for i in range(2):
                    evacuate(act, 2 * h, i)
                    weights(2 * h + 2, i)
            for i in range(2):
                evacuate(act, NKV - 2, i)
            for i in range(2):
                act.wait_ge(q_out[i], (NKV // 2 + 1) * 16)

        @block.vector
        def _(dve):
            dve.sem_inc(w_lo_set, 2)
            with dve.Fori(0, NKV // 2) as h:
                j0 = 2 * h
                for i in range(2):
                    dve.wait_ge(w_hi_set, j0 + i + 1)
                    nc.vector.tensor_tensor(w_lo[:, i], raw[:, i], w_hi[:, i].bitcast(F32),
                                            ALU.subtract).then_inc(w_lo_set, 1)

        @block.tensor
        def _(pe):
            pe.sem_inc(q_full, 2 * G)
            pe.sem_inc(q_set, G)
            with pe.Fori(0, NKV // 2) as h:
                j0 = 2 * h
                for i in range(2):
                    pe.wait_ge(w_lo_set, j0 + i + 3)
                    for g in range(G):
                        pe.wait_ge(q_set, (j0 + i) * G + g + 1)
                        for k in range(KC):
                            end = product(nc, q_ps[:, g, :],
                                          (w_hi[:, i, k, g * D:(g + 1) * D], w_lo[:, i, k, g * D:(g + 1) * D]),
                                          (xt_hi[:, k, :], xt_lo[:, k, :]), k == 0, k == KC - 1)
                        end.then_inc(q_full, 1)


def attention_output(nc, x_sb, o_dram, wo, bo):
    B, NKV, D, GL = o_dram.shape
    G, H = wo.shape[2:]
    L = GL // G
    RT = B * L // P
    with Scope(nc, "wo") as sc:
        o_raw, w_raw = sc.sb("o_raw", [P, 2, B, GL]), sc.sb("w_raw", [P, 2, G, H])
        o_hi, o_lo = sc.sb("o_hi", [P, 2, G, B * L], F32R), sc.sb("o_lo", [P, 2, G, B * L], F32R)
        w_hi, w_lo = sc.sb("w_hi", [P, 2, G, H], F32R), sc.sb("w_lo", [P, 2, G, H], F32R)
        bo_sb = sc.sb("bo_sb", [P, H])
        ps = sc.ps("ps", [P, RT, 512])
        bias_in = sc.sem("bias_in")
        a_in = [sc.sem(f"a_in{i}") for i in range(2)]
        hi_set, lo_set, used, done, x_set = (sc.sem(n) for n in ("hi_set", "lo_set", "used", "done", "x_set"))
        block = sc.block()

        def spread(i):
            return o_raw[:, i].rearrange("p b (g l) -> p g b l", g=G)

        def heads(t, i):
            return t[:, i].rearrange("p g (b l) -> p g b l", b=B)

        @block.sync
        def _(sp):
            sp.dma_start(bo_sb[:, :], bo.rearrange("(a n) -> a n", a=1).broadcast_to([P, H])).then_inc(bias_in, 16)
            with sp.Fori(0, NKV // 2) as h:
                j0 = 2 * h
                for i in range(2):
                    sp.wait_ge(lo_set, (j0 + i) * 2 + 2)
                    sp.dma_start(o_raw[:, i], o_dram[:, j0 + i].rearrange("b d n -> d b n")).then_inc(a_in[i], 16)
                    sp.dma_start(w_raw[:, i], wo[j0 + i]).then_inc(a_in[i], 16)

        @block.scalar
        def _(act):
            with act.Fori(0, NKV // 2) as h:
                j0 = 2 * h
                for i in range(2):
                    act.wait_ge(a_in[i], (j0 + 2) * 16)
                    act.wait_ge(used, j0 + i + 1)
                    for g in range(G):
                        nc.scalar.activation(heads(o_hi, i)[:, g], spread(i)[:, g], ACT.Copy)
                    nc.scalar.activation(w_hi[:, i], w_raw[:, i], ACT.Copy).then_inc(hi_set, 1)

        @block.vector
        def _(dve):
            dve.sem_inc(lo_set, 4)
            with dve.Fori(0, NKV // 2) as h:
                j0 = 2 * h
                for i in range(2):
                    dve.wait_ge(hi_set, j0 + i + 1)
                    for g in range(G):
                        end = nc.vector.tensor_tensor(heads(o_lo, i)[:, g], spread(i)[:, g],
                                                      heads(o_hi, i)[:, g].bitcast(F32), ALU.subtract)
                    end.then_inc(lo_set, 1)
                    nc.vector.tensor_tensor(w_lo[:, i], w_raw[:, i], w_hi[:, i].bitcast(F32),
                                            ALU.subtract).then_inc(lo_set, 1)
            dve.wait_ge(bias_in, 16)
            for r in range(RT):
                nc.vector.tensor_tensor(x_sb[:, r, :], x_sb[:, r, :], bo_sb[:, :], ALU.add).then_inc(x_set, 1)
            for r in range(RT):
                dve.wait_ge(done, r + 1)
                dve.wait_ge(x_set, r + 1)
                nc.vector.tensor_tensor(x_sb[:, r, :], ps[:, r, :], x_sb[:, r, :], ALU.add)

        @block.tensor
        def _(pe):
            pe.sem_inc(used, 2)

            def pair(j0, first, last):
                for i in range(2):
                    pe.wait_ge(lo_set, (j0 + i) * 2 + 6)
                    for g in range(G):
                        for r in range(RT):
                            rs = slice(r * P, (r + 1) * P)
                            end_of_all = last and i == 1 and g == G - 1
                            end = product(nc, ps[:, r, :], (o_hi[:, i, g, rs], o_lo[:, i, g, rs]),
                                          (w_hi[:, i, g, :], w_lo[:, i, g, :]),
                                          first and i == 0 and g == 0, end_of_all)
                            if end_of_all:
                                end.then_inc(done, 1)
                            elif g == G - 1 and r == RT - 1:
                                end.then_inc(used, 1)

            pair(0, True, False)
            with pe.Fori(1, NKV // 2 - 1) as h:
                pair(2 * h, False, False)
            pair(NKV - 2, False, True)


def mamba_project(nc, xt_hi, xt_lo, w_in, conv_w, conv_b, w_x, u_sb, gate_sb, ssm_sb, B):
    DC, _, _, KC, _ = w_in.shape
    K = conv_w.shape[2]
    N = w_x.shape[2]
    R = xt_hi.shape[2]
    RT = R // P
    L = R // B
    with Scope(nc, "mp") as sc:
        raw = sc.sb("raw", [P, 2, 2, KC, P])
        w_hi, w_lo = sc.sb("w_hi", [P, 2, 2, KC, P], F32R), sc.sb("w_lo", [P, 2, 2, KC, P], F32R)
        cw, cb = sc.sb("cw", [P, DC, K]), sc.sb("cb", [P, DC])
        wx_raw = sc.sb("wx_raw", [P, DC, N])
        wx_hi, wx_lo = sc.sb("wx_hi", [P, DC, N], F32R), sc.sb("wx_lo", [P, DC, N], F32R)
        xpad = sc.sb("xpad", [P, 2, B, L + K - 1])
        xc = sc.sb("xc", [P, 2, B, L])
        u_hi, u_lo = sc.sb("u_hi", [P, 2, R], F32R), sc.sb("u_lo", [P, 2, R], F32R)
        xg_ps = sc.ps("xg_ps", [P, 4, 512])
        ssm_ps = sc.ps("ssm_ps", [P, RT, 512])
        small_in = sc.sem("small_in")
        w_in_s = [sc.sem(f"w_in{i}") for i in range(2)]
        pad_set, wx_hi_set, wx_set, w_hi_set, w_lo_set = (
            sc.sem(n) for n in ("pad_set", "wx_hi_set", "wx_set", "w_hi_set", "w_lo_set"))
        xg_full, x_read, gate_read, conv, xc_set, u_set, u_hi_set, u_lo_set, ssm_full = (
            sc.sem(n) for n in ("xg_full", "x_read", "gate_read", "conv", "xc_set", "u_set", "u_hi_set", "u_lo_set",
                                "ssm_full"))
        block = sc.block()

        @block.sync
        def _(sp):
            sp.dma_start(cw[:, :, :], conv_w).then_inc(small_in, 16)
            sp.dma_start(cb[:, :], conv_b).then_inc(small_in, 16)
            sp.dma_start(wx_raw[:, :, :], w_x).then_inc(small_in, 16)
            for c in range(DC):
                if c >= 2:
                    sp.wait_ge(w_lo_set, c - 1)
                sp.dma_start(raw[:, c % 2], w_in[c]).then_inc(w_in_s[c % 2], 16)

        @block.gpsimd
        def _(pool):
            nc.gpsimd.memset(xpad[:, :, :, 0:K - 1], 0.0).then_inc(pad_set, 1)
            pool.wait_ge(small_in, 48)
            nc.gpsimd.tensor_scalar(wx_hi[:, :, :], wx_raw[:, :, :], 1.0, 1.0, ALU.mult, ALU.mult).then_inc(wx_hi_set, 1)
            pool.wait_ge(wx_hi_set, 1)
            nc.gpsimd.tensor_tensor(wx_lo[:, :, :], wx_raw[:, :, :], wx_hi[:, :, :].bitcast(F32),
                                    ALU.subtract).then_inc(wx_set, 1)

        @block.tensor
        def _(pe):
            def ssm(c):
                pe.wait_ge(u_lo_set, c + 1)
                if c == 0:
                    pe.wait_ge(wx_set, 1)
                for r in range(RT):
                    rs = slice(r * P, (r + 1) * P)
                    end = product(nc, ssm_ps[:, r, 0:N], (u_hi[:, c % 2, rs], u_lo[:, c % 2, rs]),
                                  (wx_hi[:, c, :], wx_lo[:, c, :]), c == 0, c == DC - 1)
                end.then_inc(ssm_full, 1)

            for c in range(DC):
                pe.wait_ge(w_lo_set, c + 1)
                for part in range(2):
                    if c >= 2:
                        pe.wait_ge((x_read, gate_read)[part], c - 1)
                    for k in range(KC):
                        end = product(nc, xg_ps[:, 2 * (c % 2) + part, :],
                                      (w_hi[:, c % 2, part, k], w_lo[:, c % 2, part, k]),
                                      (xt_hi[:, k, :], xt_lo[:, k, :]), k == 0, k == KC - 1)
                    end.then_inc(xg_full, 1)
                if c > 1:
                    ssm(c - 2)
            ssm(DC - 2)
            ssm(DC - 1)

        @block.scalar
        def _(act):
            def weights(c):
                act.wait_ge(w_in_s[c % 2], (c // 2 + 1) * 16)
                if c >= 2:
                    act.wait_ge(xg_full, 2 * (c - 1))
                nc.scalar.activation(w_hi[:, c % 2], raw[:, c % 2], ACT.Copy).then_inc(w_hi_set, 1)

            def silu(c):
                act.wait_ge(xc_set, c + 1)
                nc.scalar.activation(u_sb[:, c, :], xc[:, c % 2].rearrange("p b l -> p (b l)"),
                                     ACT.Silu).then_inc(u_set, 1)
                if c >= 2:
                    act.wait_ge(ssm_full, c - 1)
                act.wait_ge(u_set, c + 1)
                nc.scalar.activation(u_hi[:, c % 2], u_sb[:, c, :], ACT.Copy).then_inc(u_hi_set, 1)

            act.wait_ge(pad_set, 1)
            weights(0)
            for c in range(DC):
                if c + 1 < DC:
                    weights(c + 1)
                act.wait_ge(xg_full, 2 * c + 1)
                if c >= 2:
                    act.wait_ge(xc_set, c - 1)
                nc.scalar.activation(xpad[:, c % 2, :, K - 1:], xg_ps[:, 2 * (c % 2), :].rearrange("p (b l) -> p b l", b=B),
                                     ACT.Copy).then_inc(x_read, 1)
                act.wait_ge(xg_full, 2 * c + 2)
                nc.scalar.activation(gate_sb[:, c, :], xg_ps[:, 2 * (c % 2) + 1, :], ACT.Silu).then_inc(gate_read, 1)
                if c > 0:
                    silu(c - 1)
            silu(DC - 1)

        @block.vector
        def _(dve):
            step = Chain(dve, conv)

            def u_low(c):
                dve.wait_ge(u_hi_set, c + 1)
                nc.vector.tensor_tensor(u_lo[:, c % 2], u_sb[:, c, :], u_hi[:, c % 2].bitcast(F32),
                                        ALU.subtract).then_inc(u_lo_set, 1)

            dve.wait_ge(small_in, 48)
            for c in range(DC + 1):
                if c < DC:
                    dve.wait_ge(w_hi_set, c + 1)
                    nc.vector.tensor_tensor(w_lo[:, c % 2], raw[:, c % 2], w_hi[:, c % 2].bitcast(F32),
                                            ALU.subtract).then_inc(w_lo_set, 1)
                if c > 1:
                    u_low(c - 2)
                if c > 0:
                    a = c - 1
                    s = a % 2
                    dve.wait_ge(x_read, a + 1)
                    if a >= 2:
                        dve.wait_ge(u_set, a - 1)
                    step(nc.vector.tensor_scalar(xc[:, s], xpad[:, s, :, 0:L], cw[:, a, 0:1], cb[:, a:a + 1],
                                                 ALU.mult, ALU.add))
                    for j in range(1, K):
                        ins = nc.vector.scalar_tensor_tensor(out=xc[:, s], in0=xpad[:, s, :, j:j + L],
                                                             scalar=cw[:, a, j:j + 1], in1=xc[:, s],
                                                             op0=ALU.mult, op1=ALU.add)
                        if j < K - 1:
                            step(ins)
                        else:
                            ins.then_inc(xc_set, 1)
            u_low(DC - 1)
            dve.wait_ge(ssm_full, DC)
            for r in range(RT):
                nc.vector.tensor_copy(ssm_sb[:, r, :], ssm_ps[:, r, 0:N])


def mamba_parameters(nc, ssm_sb, w_dt, b_dt, ident, b_all, c_all, dt_sb, work, eps=1e-6):
    _, RT, N = ssm_sb.shape
    NS, DC, R = b_all.shape[1], dt_sb.shape[1], dt_sb.shape[2]
    RANK = N - 2 * NS
    assert NS == 2 * DC
    with Scope(nc, "mr") as sc:
        sq = sc.sb("sq", [P, RT, N])
        ms = sc.sb("ms", [P, RT, 3])
        eps_sb = sc.sb("eps", [P, 1])
        nrm = sc.sb("nrm", [P, RT, N])
        n_hi, n_lo = sc.sb("n_hi", [N, R], F32R), sc.sb("n_lo", [N, R], F32R)
        sel = sc.sb("sel", [N, 2 * NS, P], F32R)
        wd_raw = sc.sb("wd_raw", [RANK, DC * P])
        wd_hi, wd_lo = sc.sb("wd_hi", [RANK, DC * P], F32R), sc.sb("wd_lo", [RANK, DC * P], F32R)
        bd = sc.sb("bd", [P, DC])
        t_ps = sc.ps("t_ps", [P, 512])
        bc_ps = sc.ps("bc_ps", [P, 4, 512])
        d_ps = sc.ps("d_ps", [P, 2, 512])
        small_in, own, ms_set, std_set, nrm_set, t_full, n_hi_set, n_lo_set, wd_hi_set, wd_set, sel_set = (
            sc.sem(n) for n in ("small_in", "own", "ms_set", "std_set", "nrm_set", "t_full", "n_hi_set", "n_lo_set",
                                "wd_hi_set", "wd_set", "sel_set"))
        bc_full, bc_even, bc_odd, d_full, d_abs, d_read, e_set, ln_set = (
            sc.sem(n) for n in ("bc_full", "bc_even", "bc_odd", "d_full", "d_abs", "d_read", "e_set", "ln_set"))
        block = sc.block()
        segments = [(0, RANK), (RANK, NS), (RANK + NS, NS)]

        @block.sync
        def _(sp):
            sp.dma_start(wd_raw[:, :], w_dt).then_inc(small_in, 16)
            sp.dma_start(bd[:, :], b_dt).then_inc(small_in, 16)

        @block.gpsimd
        def _(pool):
            pool.wait_ge(small_in, 32)
            nc.gpsimd.tensor_scalar(wd_hi[:, :], wd_raw[:, :], 1.0, 1.0, ALU.mult, ALU.mult).then_inc(wd_hi_set, 1)
            pool.wait_ge(wd_hi_set, 1)
            nc.gpsimd.tensor_tensor(wd_lo[:, :], wd_raw[:, :], wd_hi[:, :].bitcast(F32), ALU.subtract).then_inc(wd_set, 1)
            for h in range(2):
                hs = slice(h * NS, (h + 1) * NS)
                nc.gpsimd.tensor_copy(sel[:, hs, :], ident[0:N, RANK + h * NS:RANK + (h + 1) * NS].unsqueeze(2)
                                      .broadcast_to([N, NS, P])).then_inc(sel_set, 1)

        @block.vector
        def _(dve):
            step = Chain(dve, own)
            step(nc.vector.memset(eps_sb[:, :], eps))
            step(nc.vector.tensor_tensor(sq[:, :, :], ssm_sb[:, :, :], ssm_sb[:, :, :], ALU.mult))
            for i, (a, n) in enumerate(segments):
                step(nc.vector.tensor_reduce(ms[:, :, i:i + 1], sq[:, :, a:a + n], AX_X, ALU.add))
                nc.vector.tensor_scalar(ms[:, :, i], ms[:, :, i], 1.0 / n, None, ALU.mult).then_inc(ms_set, 1)
            dve.wait_ge(std_set, 1)
            step(nc.vector.reciprocal(ms[:, :, :], ms[:, :, :]))
            for i, (a, n) in enumerate(segments):
                nc.vector.tensor_tensor(nrm[:, :, a:a + n], ssm_sb[:, :, a:a + n],
                                        ms[:, :, i:i + 1].broadcast_to([P, RT, n]), ALU.mult).then_inc(nrm_set, 1)
            dve.wait_ge(n_hi_set, 1)
            nc.vector.tensor_tensor(n_lo[:, :], t_ps[0:N, :], n_hi[:, :].bitcast(F32), ALU.subtract).then_inc(n_lo_set, 1)
            for c in range(DC):
                dve.wait_ge(d_abs, c + 1)
                nc.vector.tensor_scalar(work[:, c, :], d_ps[:, c % 2, :], bd[:, c:c + 1], 0.0,
                                        ALU.add, ALU.max).then_inc(d_read, 1)

            def softplus(c):
                dve.wait_ge(ln_set, c + 1)
                nc.vector.tensor_tensor(dt_sb[:, c, :], dt_sb[:, c, :], work[:, c, :], ALU.add)

            for i in range(1, 2 * NS, 2):
                dve.wait_ge(bc_full, i + 1)
                nc.vector.tensor_copy((b_all, c_all)[i // NS][:, i % NS, :], bc_ps[:, i % 4, :]).then_inc(bc_odd, 1)
                c = i // 2 - DC
                if 0 <= c - 1 < DC:
                    softplus(c - 1)
            softplus(DC - 1)

        @block.tensor
        def _(pe):
            pe.wait_ge(nrm_set, 3)
            for r in range(RT):
                end = nc.tensor.transpose(t_ps[0:N, r * P:(r + 1) * P], nrm[:, r, :], ident[:, :])
            end.then_inc(t_full, 1)
            pe.wait_ge(n_lo_set, 1)
            pe.wait_ge(wd_set, 1)
            for c in range(DC):
                if c >= 2:
                    pe.wait_ge(d_read, c - 1)
                cs = slice(c * P, (c + 1) * P)
                product(nc, d_ps[:, c % 2, :], (wd_hi[:, cs], wd_lo[:, cs]), (n_hi[0:RANK, :], n_lo[0:RANK, :]),
                        True, True).then_inc(d_full, 1)
            for i in range(2 * NS):
                if i % NS == 0:
                    pe.wait_ge(sel_set, i // NS + 1)
                if i >= 4:
                    pe.wait_ge((bc_even, bc_odd)[i % 2], i // 2 - 1)
                nc.tensor.matmul(bc_ps[:, i % 4, :], sel[:, i, :], n_hi[:, :], start=True, stop=False)
                nc.tensor.matmul(bc_ps[:, i % 4, :], sel[:, i, :], n_lo[:, :], start=False, stop=True).then_inc(bc_full, 1)

        @block.scalar
        def _(act):
            act.wait_ge(ms_set, 3)
            nc.scalar.activation(ms[:, :, :], ms[:, :, :], ACT.Sqrt, bias=eps_sb[:, 0:1]).then_inc(std_set, 1)
            act.wait_ge(t_full, 1)
            nc.scalar.activation(n_hi[:, :], t_ps[0:N, :], ACT.Copy).then_inc(n_hi_set, 1)
            act.wait_ge(small_in, 32)
            for c in range(DC):
                act.wait_ge(d_full, c + 1)
                nc.scalar.activation(dt_sb[:, c, :], d_ps[:, c % 2, :], ACT.Abs, bias=bd[:, c:c + 1]).then_inc(d_abs, 1)
            act.wait_ge(d_abs, DC)
            for i in range(0, 2 * NS, 2):
                act.wait_ge(bc_full, i + 1)
                nc.scalar.activation((b_all, c_all)[i // NS][:, i % NS, :], bc_ps[:, i % 4, :], ACT.Copy).then_inc(bc_even, 1)
                c = i // 2 % DC
                if i // 2 < DC:
                    nc.scalar.activation(dt_sb[:, c, :], dt_sb[:, c, :], ACT.Exp, scale=-1.0).then_inc(e_set, 1)
                elif i // 2 < 2 * DC:
                    act.wait_ge(e_set, c + 1)
                    nc.scalar.activation(dt_sb[:, c, :], dt_sb[:, c, :], ACT.Ln, bias=1.0).then_inc(ln_set, 1)


def mamba_scan(nc, u_sb, gate_sb, b_all, c_all, dt_sb, d_a, d_bu, a_log, d_skip, w_out, wo_raw, ident):
    DC, R = dt_sb.shape[1:]
    NS = b_all.shape[1]
    HN = d_a.shape[2]
    NH = NS // HN
    DA, DB = d_a.shape[1], d_bu.shape[1]
    B, L = d_a.shape[3:]
    with Scope(nc, "ms") as sc:
        a_sb, dk = sc.sb("a_sb", [P, DC, NS]), sc.sb("dk", [P, DC])
        dtu = sc.sb("dtu", [P, 2, R])
        y_ps = sc.ps("y_ps", [P, 2, 512])
        small_in, next_in, own, a_exp, a_set, dtu_set, da_set, dbu_set, h_set, hc_set, y_full, y_set = (
            sc.sem(n) for n in ("small_in", "next_in", "own", "a_exp", "a_set", "dtu_set", "da_set", "dbu_set", "h_set", "hc_set",
                                "y_full", "y_set"))
        block = sc.block()

        def flat(t, s):
            return t[:, s].rearrange("p n b l -> p (n b l)")

        def by_state(t, s):
            return t[:, s].rearrange("p n b l -> p n (b l)")

        @block.sync
        def _(sp):
            sp.dma_start(a_sb[:, :, :], a_log).then_inc(small_in, 16)
            sp.dma_start(dk[:, :], d_skip).then_inc(small_in, 16)
            sp.dma_start(wo_raw[:, :, :], w_out).then_inc(next_in, 16)
            sp.wait_ge(next_in, 16)

        @block.scalar
        def _(act):
            act.wait_ge(small_in, 32)
            nc.scalar.activation(a_sb[:, :, :], a_sb[:, :, :], ACT.Exp).then_inc(a_exp, 1)
            act.wait_ge(a_set, 1)
            for i in range(DC * NH):
                c, h = divmod(i, NH)
                if i >= DA:
                    act.wait_ge(h_set, i - DA + 1)
                for n in range(HN):
                    end = nc.scalar.activation(d_a[:, i % DA, n, :, 1:L],
                                               dt_sb[:, c, :].rearrange("p (b l) -> p b l", b=B)[:, :, 1:L],
                                               ACT.Exp, scale=a_sb[:, c, h * HN + n:h * HN + n + 1])
                end.then_inc(da_set, 1)

        @block.gpsimd
        def _(pool):
            for i in range(DC * NH):
                c, h = divmod(i, NH)
                pool.wait_ge(dtu_set, c + 1)
                if i >= DB:
                    pool.wait_ge(y_full, i - DB + 1)
                nc.gpsimd.tensor_tensor(by_state(d_bu, i % DB), b_all[:, h * HN:(h + 1) * HN, :],
                                        dtu[:, c % 2, :].unsqueeze(1).broadcast_to([P, HN, R]),
                                        ALU.mult).then_inc(dbu_set, 1)

        @block.vector
        def _(dve):
            step = Chain(dve, own)
            nc.vector.memset(d_a[:, :, :, :, 0:1], 0.0).then_inc(own, 1)
            step.count = 1
            dve.wait_ge(a_exp, 1)
            nc.vector.tensor_scalar(a_sb[:, :, :], a_sb[:, :, :], -1.0, None, ALU.mult).then_inc(a_set, 1)

            def weigh(c):
                if c >= 2:
                    dve.wait_ge(dbu_set, NH * (c - 1))
                nc.vector.tensor_tensor(dtu[:, c % 2, :], dt_sb[:, c, :], u_sb[:, c, :], ALU.mult).then_inc(dtu_set, 1)

            def output(c):
                dve.wait_ge(y_full, NH * (c + 1))
                step(nc.vector.scalar_tensor_tensor(out=u_sb[:, c, :], in0=u_sb[:, c, :], scalar=dk[:, c:c + 1],
                                                    in1=y_ps[:, c % 2, :], op0=ALU.mult, op1=ALU.add))
                nc.vector.tensor_tensor(gate_sb[:, c, :], gate_sb[:, c, :], u_sb[:, c, :], ALU.mult).then_inc(y_set, 1)

            weigh(0)
            weigh(1)
            for i in range(DC * NH + 1):
                if i < DC * NH:
                    c, h = divmod(i, NH)
                    dve.wait_ge(da_set, i + 1)
                    dve.wait_ge(dbu_set, i + 1)
                    nc.vector.tensor_tensor_scan(flat(d_bu, i % DB), flat(d_a, i % DA), flat(d_bu, i % DB), 0.0,
                                                 ALU.mult, ALU.add).then_inc(h_set, 1)
                    if h == NH // 2 and c > 0:
                        output(c - 1)
                        if c + 1 < DC:
                            weigh(c + 1)
                if i > 0:
                    h = (i - 1) % NH
                    dve.wait_ge(h_set, i)
                    nc.vector.tensor_tensor(by_state(d_bu, (i - 1) % DB), by_state(d_bu, (i - 1) % DB),
                                            c_all[:, h * HN:(h + 1) * HN, :], ALU.mult).then_inc(hc_set, 1)
            output(DC - 1)

        @block.tensor
        def _(pe):
            for i in range(DC * NH):
                c, h = divmod(i, NH)
                pe.wait_ge(hc_set, i + 1)
                if h == 0 and c >= 2:
                    pe.wait_ge(y_set, c - 1)
                for n in range(HN):
                    end = nc.tensor.matmul(y_ps[:, c % 2, :], ident[:, :], by_state(d_bu, i % DB)[:, n, :],
                                           start=h == 0 and n == 0, stop=h == NH - 1 and n == HN - 1)
                end.then_inc(y_full, 1)


def mamba_output(nc, x_sb, y_sb, raw):
    DC, R = y_sb.shape[1:]
    H = raw.shape[2]
    RT = R // P
    with Scope(nc, "mo") as sc:
        w_hi, w_lo = sc.sb("w_hi", [P, DC, H], F32R), sc.sb("w_lo", [P, DC, H], F32R)
        y_hi, y_lo = sc.sb("y_hi", [P, DC, R], F32R), sc.sb("y_lo", [P, DC, R], F32R)
        ps = sc.ps("ps", [P, RT, 512])
        hi_set, lo_set, done = (sc.sem(n) for n in ("hi_set", "lo_set", "done"))
        block = sc.block()

        @block.scalar
        def _(act):
            for c in range(DC):
                nc.scalar.activation(y_hi[:, c, :], y_sb[:, c, :], ACT.Copy).then_inc(hi_set, 1)
                nc.scalar.activation(w_hi[:, c, :], raw[:, c, :], ACT.Copy).then_inc(hi_set, 1)

        @block.vector
        def _(dve):
            for c in range(DC):
                dve.wait_ge(hi_set, 2 * c + 2)
                nc.vector.tensor_tensor(y_lo[:, c, :], y_sb[:, c, :], y_hi[:, c, :].bitcast(F32), ALU.subtract)
                nc.vector.tensor_tensor(w_lo[:, c, :], raw[:, c, :], w_hi[:, c, :].bitcast(F32),
                                        ALU.subtract).then_inc(lo_set, 1)
            for r in range(RT):
                dve.wait_ge(done, r + 1)
                nc.vector.tensor_tensor(x_sb[:, r, :], ps[:, r, :], x_sb[:, r, :], ALU.add)

        @block.tensor
        def _(pe):
            for c in range(DC):
                pe.wait_ge(lo_set, c + 1)
                for r in range(RT):
                    rs = slice(r * P, (r + 1) * P)
                    end = product(nc, ps[:, r, :], (y_hi[:, c, rs], y_lo[:, c, rs]), (w_hi[:, c, :], w_lo[:, c, :]),
                                  c == 0, c == DC - 1)
                    if c == DC - 1:
                        end.then_inc(done, 1)


def mamba(nc, x_sb, ident, B, w_in, conv_w, conv_b, w_x, w_dt, b_dt, a_log, d_skip, w_out):
    RT = x_sb.shape[1]
    H = x_sb.shape[2]
    R = RT * P
    DC = w_in.shape[0]
    NS = a_log.shape[2]
    with Scope(nc, "mamba") as sc:
        u_sb, gate_sb = sc.sb("u", [P, DC, R]), sc.sb("gate", [P, DC, R])
        wo_raw = sc.sb("wo_raw", [P, DC, H])
        with Scope(nc, "mamba_a") as sc1:
            ssm_sb = sc1.sb("ssm", [P, RT, w_x.shape[2]])
            with Scope(nc, "mamba_x") as sc2:
                xt_hi, xt_lo = sc2.sb("xt_hi", [P, H // P, R], F32R), sc2.sb("xt_lo", [P, H // P, R], F32R)
                layernorm_transposed(nc, "ln1", x_sb, xt_hi, xt_lo, ident)
                mamba_project(nc, xt_hi, xt_lo, w_in, conv_w, conv_b, w_x, u_sb, gate_sb, ssm_sb, B)
            b_all, c_all = sc1.sb("b_all", [P, NS, R]), sc1.sb("c_all", [P, NS, R])
            dt_sb = sc1.sb("dt", [P, DC, R])
            with Scope(nc, "mamba_w") as sc2:
                work = sc2.sb("work", [P, DC, R])
                mamba_parameters(nc, ssm_sb, w_dt, b_dt, ident, b_all, c_all, dt_sb, work)
            d_a = sc1.sb("d_a", [P, 3, NS // 4, B, R // B])
            d_bu = sc1.sb("d_bu", [P, 4, NS // 4, B, R // B])
            mamba_scan(nc, u_sb, gate_sb, b_all, c_all, dt_sb, d_a, d_bu, a_log, d_skip, w_out, wo_raw,
                       ident)
        mamba_output(nc, x_sb, gate_sb, wo_raw)


def ternary_linear(nc, x_sb, xt_hi, xt_lo, w, bias, ones):
    KC, H = w.shape[1:]
    R = xt_hi.shape[2]
    RT = R // P
    with Scope(nc, "tl") as sc:
        raw, neg = sc.sb("raw", [P, KC, H]), sc.sb("neg", [P, KC, H])
        tern, tern_r = sc.sb("tern", [P, KC, H]), sc.sb("tern_r", [P, KC, H], F32R)
        bias_sb = sc.sb("bias", [P, H])
        part = sc.sb("part", [P, 2])
        tot = sc.sb("tot", [P, 2])
        few = sc.sb("few", [P, 1])
        scale = sc.sb("scale", [P, 1])
        tot_ps = sc.ps("tot_ps", [P, 512])
        ps = sc.ps("ps", [P, RT, 512])
        w_in, own, part_set, tot_full, tern_set, done = (
            sc.sem(n) for n in ("w_in", "own", "part_set", "tot_full", "tern_set", "done"))
        block = sc.block()

        @block.sync
        def _(sp):
            sp.dma_start(raw[:, :, :], w).then_inc(w_in, 16)
            sp.dma_start(bias_sb[:, :], bias.rearrange("(a n) -> a n", a=1).broadcast_to([P, H])).then_inc(w_in, 16)

        @block.vector
        def _(dve):
            step = Chain(dve, own)
            dve.wait_ge(w_in, 32)
            step(nc.vector.tensor_scalar(neg[:, :, :], raw[:, :, :], -0.5, None, ALU.is_lt))
            step(nc.vector.scalar_tensor_tensor(out=tern[:, :, :], in0=raw[:, :, :], scalar=0.5, in1=neg[:, :, :],
                                                op0=ALU.is_gt, op1=ALU.subtract))
            nc.vector.tensor_copy(tern_r[:, :, :], tern[:, :, :]).then_inc(tern_set, 1)
            step(nc.vector.tensor_tensor(neg[:, :, :], tern[:, :, :], tern[:, :, :], ALU.mult))
            step(nc.vector.tensor_reduce(part[:, 0:1], neg[:, :, :].rearrange("p k n -> p (k n)"), AX_X, ALU.add))
            step(nc.vector.tensor_tensor(neg[:, :, :], tern[:, :, :], raw[:, :, :], ALU.mult))
            nc.vector.tensor_reduce(part[:, 1:2], neg[:, :, :].rearrange("p k n -> p (k n)"), AX_X,
                                    ALU.add).then_inc(part_set, 1)
            dve.wait_ge(tot_full, 1)
            step(nc.vector.tensor_copy(tot[:, :], tot_ps[:, 0:2]))
            step(nc.vector.tensor_scalar(few[:, :], tot[:, 0:1], 0.0, None, ALU.is_equal))
            step(nc.vector.tensor_scalar(tot[:, 0:1], tot[:, 0:1], 1.0, None, ALU.max))
            step(nc.vector.reciprocal(scale[:, :], tot[:, 0:1]))
            step(nc.vector.scalar_tensor_tensor(out=scale[:, :], in0=scale[:, :], scalar=tot[:, 1:2], in1=few[:, :],
                                                op0=ALU.mult, op1=ALU.add))
            for r in range(RT):
                step(nc.vector.tensor_tensor(x_sb[:, r, :], x_sb[:, r, :], bias_sb[:, :], ALU.add))
            for r in range(RT):
                dve.wait_ge(done, r + 1)
                nc.vector.scalar_tensor_tensor(out=x_sb[:, r, :], in0=ps[:, r, :], scalar=scale[:, 0:1],
                                               in1=x_sb[:, r, :], op0=ALU.mult, op1=ALU.add)

        @block.tensor
        def _(pe):
            pe.wait_ge(tern_set, 1)
            for r in range(RT):
                rs = slice(r * P, (r + 1) * P)
                for k in range(KC):
                    nc.tensor.matmul(ps[:, r, :], xt_hi[:, k, rs], tern_r[:, k, :], start=k == 0, stop=False)
                    end = nc.tensor.matmul(ps[:, r, :], xt_lo[:, k, rs], tern_r[:, k, :], start=False, stop=k == KC - 1)
                end.then_inc(done, 1)
            pe.wait_ge(part_set, 1)
            nc.tensor.matmul(tot_ps[:, 0:2], ones[:, :], part[:, :], start=True, stop=True).then_inc(tot_full, 1)


def context_attention(nc, x_sb, xt_hi, xt_lo, ctx, ident, c_dram):
    B, S, H = ctx.shape
    KC = xt_hi.shape[1]
    R = xt_hi.shape[2]
    L = R // B
    SE = S + S % 2
    NC = -(-S // P)
    TILES = even_tiles(SE)
    NT = len(TILES)
    NB = -(-NC // 8)
    GROUPS = [(c, min(c + 2, NC)) for c in range(0, NC, 2)]
    if S % P and GROUPS[-1][1] - GROUPS[-1][0] > 1:
        GROUPS[-1:] = [(NC - 2, NC - 1), (NC - 1, NC)]
    NG = len(GROUPS)
    LO_DVE = 3
    EARLY = -(-(TILES[1][0] + TILES[1][1]) // P)

    def rows(c):
        return min(P, S - c * P)

    def group_of(c):
        return [g for g, (a, z) in enumerate(GROUPS) if a <= c < z][0]

    PARTS = [slice(0, 2), slice(2, 3), slice(3, KC)]
    SCORES, late = [], list(range(EARLY, NC))
    for t in range(NT):
        for part in range(len(PARTS)):
            SCORES.append(("s", t, part))
            if late:
                SCORES.append(("t", late.pop(0), None))

    NS = 3

    def slot(c):
        return 1 if c == NC - 1 and c % NS == 0 else c % NS

    def ago(c):
        return min(d for d in range(1, NS + 1) if d == NS or slot((c - d) % NC) == slot(c))

    def drive(eng, step):
        step(0, -1, True, True)
        with eng.Fori(0, (B - 2) // 2) as h:
            step(h, 0, True, True)
            step(h, 1, True, True)
        step((B - 2) // 2, 0, True, False)
        step((B - 2) // 2, 1, False, False)

    with Scope(nc, "ca") as sc:
        nat = sc.sb("nat", [P, 2, NC, H])
        n_hi, n_lo = sc.sb("n_hi", [P, NC, H], F32R), sc.sb("n_lo", [P, NC, H], F32R)
        t_hi, t_lo = sc.sb("t_hi", [P, KC, SE], F32R), sc.sb("t_lo", [P, KC, SE], F32R)
        q_hi, q_lo = sc.sb("q_hi", [P, 2, KC, L], F32R), sc.sb("q_lo", [P, 2, KC, L], F32R)
        prob = sc.sb("prob", [L, SE])
        tmax, nmax = sc.sb("tmax", [L, NT]), sc.sb("nmax", [L, 1])
        den, rden = sc.sb("den", [L, 2]), sc.sb("rden", [L, 2])
        pt_hi, pt_lo = sc.sb("pt_hi", [P, NC, L], F32R), sc.sb("pt_lo", [P, NC, L], F32R)
        c_sb = sc.sb("c_sb", [L, H])
        t_ps = sc.ps("t_ps", [P, NS, 512])
        s_ps = sc.ps("s_ps", [L, 2, 512])
        pt_ps = sc.ps("pt_ps", [P, NB, 512])
        c_ps = sc.ps("c_ps", [L, 512])
        nat_in = [[sc.sem(f"nat_in{i}_{g}") for g in range(NG)] for i in range(2)]
        passed, passed_pe, passed_sp = sc.sem("passed"), sc.sem("passed_pe"), sc.sem("passed_sp")
        c_out = sc.sem("c_out")
        q_set, n_hi_set, lo_dve, lo_pool, t_full, t_hi_set, t_free = (
            sc.sem(n) for n in ("q_set", "n_hi_set", "lo_dve", "lo_pool", "t_full", "t_hi_set", "t_free"))
        s_full, s_free, nmax_set, exp_set, pt_full, pt_hi_set, pt_free = (
            sc.sem(n) for n in ("s_full", "s_free", "nmax_set", "exp_set", "pt_full", "pt_hi_set", "pt_free"))
        pv_done, rden_set, c_set, pad_set, x_in = (sc.sem(n) for n in ("pv_done", "rden_set", "c_set", "pad_set", "x_in"))
        block = sc.block()

        def loaded(eng, h, i, g):
            eng.wait_ge(nat_in[i % 2][g], (h + i // 2 + 1) * 16)

        def split_done(eng, h, i, g):
            if g < LO_DVE:
                eng.wait_ge(lo_dve, (2 * h + i) * LO_DVE + g + 1)
            else:
                eng.wait_ge(lo_pool, (2 * h + i) * (NG - LO_DVE) + g - LO_DVE + 1)

        @block.sync
        def _(sp):
            def load(h, i, g):
                a, z = GROUPS[g]
                r = rows(a)
                sp.dma_start(nat[0:r, i % 2, a:z, :],
                             ctx[2 * h + i, a * P:a * P + (z - a) * r].rearrange("(c p) h -> p c h", p=r)
                             ).then_inc(nat_in[i % 2][g], 16)

            for i in range(2):
                for g in range(NG):
                    load(0, i, g)
            with sp.Fori(0, (B - 2) // 2) as h:
                for i in range(2):
                    for g, (a, z) in enumerate(GROUPS):
                        sp.wait_ge(t_full, (2 * h + i) * NC + z)
                        apart(sp, passed_sp)
                        split_done(sp, h, i, g)
                        load(h, i + 2, g)

        @block.gpsimd
        def _(pool):
            def step(h, i, has1, has2):
                i += 1
                if not has1:
                    return
                for g, (a, z) in enumerate(GROUPS):
                    r = rows(a)
                    loaded(pool, h, i, g)
                    pool.wait_ge(pv_done, (2 * h + i) * NG + g + 1)
                    apart(pool, passed)
                    nc.gpsimd.tensor_scalar(n_hi[0:r, a:z, :], nat[0:r, i % 2, a:z, :], 1.0, 1.0,
                                            ALU.mult, ALU.mult).then_inc(n_hi_set, 1)
                for g, (a, z) in enumerate(GROUPS):
                    if g >= LO_DVE:
                        r = rows(a)
                        pool.wait_ge(n_hi_set, (2 * h + i) * NG + g + 1)
                        nc.gpsimd.tensor_tensor(n_lo[0:r, a:z, :], nat[0:r, i % 2, a:z, :],
                                                n_hi[0:r, a:z, :].bitcast(F32), ALU.subtract).then_inc(lo_pool, 1)

            drive(pool, step)

        @block.tensor
        def _(pe):
            pe.sem_inc(pv_done, NG)

            def transpose(h, i, c):
                r = rows(c)
                n = (2 * h + i) * NC + c
                loaded(pe, h, i, group_of(c))
                pe.wait_ge(t_free, n + 1 + NS - ago(c))
                for k in range(KC):
                    end = nc.tensor.transpose(t_ps[:, slot(c), k * P:k * P + r],
                                              nat[0:r, i % 2, c, k * P:(k + 1) * P], ident[0:r, 0:r])
                end.then_inc(t_full, 1)

            def score_part(h, i, t, part):
                n = 2 * h + i
                c, w = TILES[t]
                if part == 0:
                    if t == 0:
                        pe.wait_ge(q_set, n * 2 + 2)
                    pe.wait_ge(t_free, n * NC + min(NC, -(-(c + w) // P)) + NS)
                    pe.wait_ge(s_free, n * NT + t + 1)
                for k in range(KC)[PARTS[part]]:
                    end = product(nc, s_ps[:, t % 2, 0:w], (q_hi[:, i % 2, k, :], q_lo[:, i % 2, k, :]),
                                  (t_hi[:, k, c:c + w], t_lo[:, k, c:c + w]), k == 0, k == KC - 1)
                if part == len(PARTS) - 1:
                    end.then_inc(s_full, 1)

            def pv(h, i, c):
                n = 2 * h + i
                r = rows(c)
                g = group_of(c)
                if c == 0:
                    pe.wait_ge(c_set, n + 1)
                if c % 8 == 0:
                    pe.wait_ge(pt_free, n * NB + c // 8 + 1 + NB)
                if c == GROUPS[g][0]:
                    split_done(pe, h, i, g)
                end = product(nc, c_ps[:, :], (pt_hi[0:r, c, :], pt_lo[0:r, c, :]),
                              (n_hi[0:r, c, :], n_lo[0:r, c, :]), c == 0, c == NC - 1)
                if c == GROUPS[g][1] - 1:
                    end.then_inc(pv_done, 1)

            def step(h, i, has1, has2):
                if i == -1:
                    for c in range(EARLY):
                        transpose(h, 0, c)
                if has1:
                    for kind, at, part in SCORES:
                        if kind == "s":
                            score_part(h, i + 1, at, part)
                        else:
                            transpose(h, i + 1, at)
                early = list(range(EARLY)) if has2 else []
                for c in range(NC):
                    if i >= 0:
                        pv(h, i, c)
                    if early and c % 2 == 1:
                        transpose(h, i + 2, early.pop(0))
                for c in early:
                    transpose(h, i + 2, c)
                if has1:
                    n = 2 * h + i + 1
                    pe.wait_ge(exp_set, n + 1)
                    for c in range(NC):
                        if c % 8 == 0:
                            pe.wait_ge(pt_free, n * NB + c // 8 + 1)
                            apart(pe, passed_pe)
                        r = rows(c)
                        end = nc.tensor.transpose(pt_ps[0:r, c // 8, (c % 8) * L:(c % 8 + 1) * L],
                                                  prob[:, c * P:c * P + r], ident[0:L, 0:L])
                        if c % 8 == 7 or c == NC - 1:
                            end.then_inc(pt_full, 1)

            drive(pe, step)

        def pt_parts():
            for g in range(NB):
                a, z = 8 * g, min(8 * g + 8, NC)
                if z == NC and rows(NC - 1) < P:
                    yield g, a, z - 1, P, False
                    yield g, z - 1, z, rows(z - 1), True
                else:
                    yield g, a, z, P, True

        def bank(g, a, z, r):
            return pt_ps[0:r, g, (a % 8) * L:(a % 8 + z - a) * L].rearrange("p (c l) -> p c l", l=L)

        def transposed(c, r):
            return t_ps[:, slot(c), :].rearrange("p (k n) -> p k n", k=KC)[:, :, 0:r]

        @block.scalar
        def _(act):
            def high(h, i, c):
                r = rows(c)
                act.wait_ge(t_full, (2 * h + i) * NC + c + 1)
                nc.scalar.activation(t_hi[:, :, c * P:c * P + r], transposed(c, r), ACT.Copy).then_inc(t_hi_set, 1)

            def query(h, i):
                b = 2 * h + i
                nc.scalar.activation(q_hi[:, i % 2], xt_hi[:, :, bass.ds(b * L, L)].bitcast(F32), ACT.Copy).then_inc(q_set, 1)
                nc.scalar.activation(q_lo[:, i % 2], xt_lo[:, :, bass.ds(b * L, L)].bitcast(F32), ACT.Copy).then_inc(q_set, 1)

            def step(h, i, has1, has2):
                if i == -1:
                    query(h, 0)
                    for c in range(EARLY):
                        high(h, 0, c)
                if has1:
                    for c in range(EARLY, NC):
                        high(h, i + 1, c)
                    n = 2 * h + i + 1
                    act.wait_ge(nmax_set, n + 1)
                    nc.scalar.activation(prob[:, 0:S], prob[:, 0:S], ACT.Exp, bias=nmax[:, 0:1],
                                         accum_out=den[:, (i + 1) % 2:(i + 1) % 2 + 1]).then_inc(exp_set, 1)
                if has2:
                    query(h, i + 2)
                    for c in range(EARLY):
                        high(h, i + 2, c)
                if has1:
                    for g, a, z, r, last in pt_parts():
                        act.wait_ge(pt_full, (2 * h + i + 1) * NB + g + 1)
                        nc.scalar.activation(pt_hi[0:r, a:z, :], bank(g, a, z, r), ACT.Copy).then_inc(pt_hi_set, 1)
                if i >= 0:
                    act.wait_ge(c_set, 2 * h + i + 2)
                    act.dma_start(c_dram[2 * h + i], c_sb[:, :]).then_inc(c_out, 16)

            act.sem_inc(c_out, 16)
            drive(act, step)
            act.wait_ge(c_out, (B + 1) * 16)
            x_view = c_dram.rearrange("(r b) l h -> r (b l) h", r=R // P)
            for r in range(R // P):
                act.dma_start(nat[:, 0, r, :], x_view[r]).then_inc(x_in, 16)

        @block.vector
        def _(dve):
            parts = list(pt_parts())

            def low(h, i, c):
                r = rows(c)
                dve.wait_ge(t_hi_set, (2 * h + i) * NC + c + 1)
                nc.vector.tensor_tensor(t_lo[:, :, c * P:c * P + r], transposed(c, r),
                                        t_hi[:, :, c * P:c * P + r].bitcast(F32), ALU.subtract).then_inc(t_free, 1)

            def natural_low(h, i, g):
                a, z = GROUPS[g]
                r = rows(a)
                dve.wait_ge(n_hi_set, (2 * h + i) * NG + g + 1)
                nc.vector.tensor_tensor(n_lo[0:r, a:z, :], nat[0:r, i % 2, a:z, :],
                                        n_hi[0:r, a:z, :].bitcast(F32), ALU.subtract).then_inc(lo_dve, 1)

            def maximum(h, i, t):
                c, w = TILES[t]
                w = min(w, S - c)
                dve.wait_ge(s_full, (2 * h + i) * NT + t + 1)
                nc.vector.tensor_scalar(prob[:, c:c + w], s_ps[:, t % 2, 0:w], 1.0, None, ALU.mult, ALU.max,
                                        accum_out=tmax[:, t:t + 1]).then_inc(s_free, 1)

            def step(h, i, has1, has2):
                if i == -1:
                    for c in range(EARLY):
                        low(h, 0, c)
                if has1:
                    n = 2 * h + i + 1
                    for kind, at, part in SCORES:
                        if kind == "t":
                            low(h, i + 1, at)
                        elif part == len(PARTS) - 1:
                            maximum(h, i + 1, at)
                            if at == NT // 2 and i >= 0:
                                natural_low(h, i, LO_DVE - 1)
                    dve.wait_ge(s_free, n * NT + NT + 2)
                    nc.vector.tensor_reduce(nmax[:, :], tmax[:, :], AX_X, ALU.max, negate=True).then_inc(nmax_set, 1)
                elif i >= 0:
                    natural_low(h, i, LO_DVE - 1)
                if has2:
                    for c in range(EARLY):
                        low(h, i + 2, c)
                        if c in (3, 5):
                            natural_low(h, i + 1, (c - 3) // 2)
                elif has1:
                    natural_low(h, i + 1, 0)
                    natural_low(h, i + 1, 1)
                s = (i + 1) % 2
                if has1:
                    dve.wait_ge(exp_set, n + 1)
                    nc.vector.reciprocal(rden[:, s:s + 1], den[:, s:s + 1]).then_inc(rden_set, 1)
                if i >= 0:
                    b = 2 * h + i
                    dve.wait_ge(pv_done, b * NG + 2 * NG)
                    dve.wait_ge(rden_set, b + 1)
                    dve.wait_ge(c_out, b * 16 + 16)
                    nc.vector.tensor_scalar(c_sb[:, :], c_ps[:, :], rden[:, i % 2:i % 2 + 1], None,
                                            ALU.mult).then_inc(c_set, 1)
                if has1:
                    for at, (g, a, z, r, last) in enumerate(parts):
                        dve.wait_ge(pt_hi_set, n * len(parts) + at + (1 if last else 2))
                        ins = nc.vector.tensor_tensor(pt_lo[0:r, a:z, :], bank(g, a, z, r),
                                                      pt_hi[0:r, a:z, :].bitcast(F32), ALU.subtract)
                        if last:
                            ins.then_inc(pt_free, 1)

            dve.sem_inc(t_free, NS)
            dve.sem_inc(s_free, 2)
            dve.sem_inc(pt_free, NB)
            dve.sem_inc(c_set, 1)
            if SE > S:
                nc.vector.memset(t_hi[:, :, S:SE].bitcast(F32), 0.0).then_inc(pad_set, 1)
                nc.vector.memset(t_lo[:, :, S:SE].bitcast(F32), 0.0).then_inc(pad_set, 1)
            drive(dve, step)
            dve.wait_ge(x_in, R // P * 16)
            nc.vector.tensor_tensor(x_sb[:, :, :], x_sb[:, :, :], nat[:, 0, 0:R // P, :], ALU.add)


class OctonionWeights:

    def __init__(self, nc, scope, given):
        self.nc, self.given = nc, given
        _, _, O = given["w_gate"].shape
        D8 = given["w_down"].shape[2]
        REST_CHUNKS = given["w_rest"].shape[1]
        KC = given["sign_in"].shape[1]
        self.O, self.D8, self.KC, self.MAIN = O, D8, KC, given["w_down"].shape[0]
        self.LEFT = O - self.MAIN
        self.PARTS = P // self.LEFT
        self.F = 8 * O
        self.FC = 8 + REST_CHUNKS
        self.WIDEST = max(self.F, REST_CHUNKS * 8 * D8)
        self.tern = [scope.sb(f"tern{i}", [P, KC * 8 * O], F32R) for i in range(2)]
        self.down, self.rest = scope.sb("down", [P, 8, D8]), scope.sb("rest", [P, REST_CHUNKS, 8, D8])
        self.sign_in, self.sign_down, self.sign_rest = (
            scope.sb("sign_in", [P, KC, 8]), scope.sb("sign_down", [P, 8, 8]), scope.sb("sign_rest", [P, REST_CHUNKS, 8]))
        self.part, self.tot = scope.sb("part", [P, 4]), scope.sb("tot", [P, 4])
        self.scale, self.half, self.nhalf = (scope.sb(n, [P, 3]) for n in ("scale", "half", "nhalf"))
        self.w_in = [scope.sem(f"w_in{i}") for i in range(4)]
        self.sign_in_set, self.zero_set, self.part_set, self.tot_full, self.own, self.tern_set, self.down_set = (
            scope.sem(n) for n in ("sign_in_set", "zero_set", "part_set", "tot_full", "own", "tern_set", "down_set"))

    def width(self, c):
        return self.MAIN if c < 8 else min(self.PARTS, 8 - (c - 8) * self.PARTS) * self.LEFT

    def main(self, i):
        return self.tern[i][:, 0:self.KC * 8 * self.MAIN].rearrange("p (c k o) -> p c k o", c=self.KC, k=8)

    def left(self, i):
        return self.tern[i][:, self.KC * 8 * self.MAIN:].rearrange("p (c k o) -> p c k o", c=self.KC, k=8)

    def columns(self, i, kc, c):
        if c < 8:
            return self.main(i)[:, kc, c, :]
        a = (c - 8) * self.PARTS * self.LEFT
        return self.left(i)[:, kc].rearrange("p k o -> p (k o)")[:, a:a + self.width(c)]

    def place(self, scope):
        self.raw = [scope.sb(f"raw{i}", [P, 8, self.O])[:, :, :] for i in range(2)]

    def zero(self, eng):
        eng.memset(self.rest[:, :, :, :], 0.0).then_inc(self.zero_set, 1)

    def load(self, sp):
        g = self.given
        sp.dma_start(self.sign_in[:, :, :], g["sign_in"]).then_inc(self.sign_in_set, 16)
        sp.dma_start(self.sign_down[:, :, :], g["sign_down"]).then_inc(self.sign_in_set, 16)
        sp.dma_start(self.sign_rest[:, :, :], g["sign_rest"]).then_inc(self.sign_in_set, 16)
        sp.dma_start(self.raw[0], g["w_gate"]).then_inc(self.w_in[0], 16)
        sp.dma_start(self.raw[1], g["w_up"]).then_inc(self.w_in[1], 16)
        sp.dma_start(self.down[:, :, :], g["w_down"]).then_inc(self.w_in[2], 16)
        sp.wait_ge(self.zero_set, 1)
        for c in range(8, self.FC):
            w = self.width(c)
            sp.dma_start(self.rest[0:w, c - 8], g["w_rest"][0:w, c - 8]).then_inc(self.w_in[3], 16)

    def magnitudes(self, act, spare):
        for i, w in enumerate((self.raw[0], self.raw[1], self.down[:, :, :], self.rest[:, :, :, :])):
            act.wait_ge(self.w_in[i], 16 if i < 3 else 16 * (self.FC - 8))
            w = w.rearrange("p k o -> p (k o)") if i < 3 else w.rearrange("p c k o -> p (c k o)")
            if i > 0:
                act.wait_ge(self.part_set, i)
            self.nc.scalar.activation(spare[:, 0:w.shape[1]], w, ACT.Abs,
                                      accum_out=self.part[:, i:i + 1]).then_inc(self.part_set, 1)

    def totals(self, pe, bank, ones):
        pe.wait_ge(self.part_set, 4)
        self.nc.tensor.matmul(bank[:, 0:4], ones[:, :], self.part[:, :], start=True, stop=True).then_inc(self.tot_full, 1)

    def ternary(self, dve, bank, spare):
        nc, step = self.nc, Chain(dve, self.own)
        dve.wait_ge(self.tot_full, 1)
        step(nc.vector.tensor_copy(self.tot[:, :], bank[:, 0:4]))
        step(nc.vector.tensor_scalar(self.scale[:, 0:2], self.tot[:, 0:2], 0.5 / (self.F * self.D8), None, ALU.mult))
        step(nc.vector.scalar_tensor_tensor(out=self.scale[:, 2:3], in0=self.tot[:, 3:4], scalar=0.125,
                                            in1=self.tot[:, 2:3], op0=ALU.mult, op1=ALU.add))
        step(nc.vector.tensor_scalar(self.scale[:, 2:3], self.scale[:, 2:3], 1.0 / (self.F * self.D8), None, ALU.mult))
        step(nc.vector.tensor_scalar(self.half[:, :], self.scale[:, :], 0.5, None, ALU.mult))
        step(nc.vector.tensor_scalar(self.nhalf[:, :], self.scale[:, :], -0.5, None, ALU.mult))
        for i, w in enumerate((self.raw[1], self.raw[0], self.down[:, :, :], self.rest[:, :, :, :])):
            w = w.rearrange("p k o -> p (k o)") if i < 3 else w.rearrange("p c k o -> p (c k o)")
            m = spare[:, 0:w.shape[1]]
            at = (1, 0, 2, 2)[i]
            step(nc.vector.tensor_scalar(m, w, self.nhalf[:, at:at + 1], None, ALU.is_lt))
            step(nc.vector.scalar_tensor_tensor(out=w, in0=w, scalar=self.half[:, at:at + 1], in1=m,
                                                op0=ALU.is_gt, op1=ALU.subtract))
            dve.sem_inc(self.tern_set, 1)

    def permuted(self, eng, out, src, sign, mask):
        n = out.shape[2]
        if mask == 0:
            return eng.tensor_tensor(out, src, sign.unsqueeze(2).broadcast_to([out.shape[0], 8, n]), ALU.mult)
        o, s = (t.rearrange("p (a b c) o -> p a b c o", a=2, b=2) for t in (out, src))
        g = sign.rearrange("p (a b c) -> p a b c", a=2, b=2)
        bits = [mask >> 2 & 1, mask >> 1 & 1, mask & 1]
        for v in range(8):
            v = [v >> 2 & 1, v >> 1 & 1, v & 1]
            if any(x and not b for x, b in zip(v, bits)):
                continue
            to = (slice(None), *(x if b else slice(None) for x, b in zip(v, bits)))
            frm = (slice(None), *(1 - x if b else slice(None) for x, b in zip(v, bits)))
            sg = g[to]
            end = eng.tensor_tensor(o[to], s[frm], sg.unsqueeze(len(sg.shape)).broadcast_to([*sg.shape, n]), ALU.mult)
        return end

    def spread(self, eng, i):
        for kc in range(self.KC):
            for out, a, z in ((self.main(i), 0, self.MAIN), (self.left(i), self.MAIN, self.O)):
                self.permuted(eng, out[:, kc], self.raw[i][:, :, a:z], self.sign_in[:, kc, :], 2 * kc)

    def spread_down(self, eng, out):
        for c in range(8):
            self.permuted(eng, out[:, c], self.down[:, :, :], self.sign_down[:, c, :], c).then_inc(self.down_set, 1)
        for c in range(8, self.FC):
            self.permuted(eng, out[:, c], self.rest[:, c - 8], self.sign_rest[:, c - 8, :], 0).then_inc(self.down_set, 1)


def self_attention(nc, x_sb, xt_hi, xt_lo, w_qkv, w_o, rotary, head_mask, causal, ident, ones, B, NH, weights):
    RT, H = x_sb.shape[1:]
    KC = H // P
    R = RT * P
    L = R // B
    BR = P // L
    HD = H // NH
    HC = P // HD
    HP = P // L
    SCALE = float(HD) ** -0.5
    with Scope(nc, "sa") as top:
        qz_hi, qz_lo = (t[:, 0:RT * KC * BR * P].rearrange("p (r k b c) -> p r k b c", r=RT, k=KC, b=BR)
                        for t in weights.tern)
        kt_hi, kt_lo = (top.sb(n, [P, RT, KC, P], F32R) for n in ("kt_hi", "kt_lo"))
        v_hi, v_lo = (top.sb(n, [P, B, H], F32R) for n in ("v_hi", "v_lo"))
        hm, cm = top.sb("hm", [P, HC]), top.sb("cm", [P, L])

        with Scope(nc, "sa1") as sc:
            raw = sc.sb("raw", [P, 2, KC, H])
            w_hi, w_lo = sc.sb("w_hi", [P, 3, KC, H], F32R), sc.sb("w_lo", [P, 3, KC, H], F32R)
            rot = sc.sb("rot", [P, 3])
            xd = sc.sb("xd", [P, 2, 2, KC, HP, L], F32R)
            a_sb = sc.sb("a_sb", [P, 2, H])
            r_sb = sc.sb("r_sb", [P, 2, H])
            p_ps = sc.ps("p_ps", [P, 2, 512])
            v_ps = sc.ps("v_ps", [P, 2, 512])
            t_ps = sc.ps("t_ps", [P, 2, 512])
            w_in = [sc.sem(f"w_in{i}") for i in range(3)]
            small_in, w_hi_set, w_lo_set, p_full, a_set, r_set, zero_set, t_full, t_hi_set, t_free = (
                sc.sem(n) for n in ("small_in", "w_hi_set", "w_lo_set", "p_full", "a_set", "r_set",
                                    "zero_set", "t_full", "t_hi_set", "t_free"))
            xd_set, v_full, v_hi_set, v_free = (sc.sem(n) for n in ("xd_set", "v_full", "v_hi_set", "v_free"))
            block = sc.block()
            units = [(i, r) for r in range(RT) for i in range(2)]

            def of_part(t, h):
                return t[h * L:(h + 1) * L].rearrange("p (m h d) -> p m h d", h=HP, d=HD)[:, :, h]

            @block.sync
            def _(sp):
                sp.dma_start(rot[:, :], rotary).then_inc(small_in, 16)
                sp.dma_start(hm[:, :], head_mask).then_inc(small_in, 16)
                sp.dma_start(cm[:, :], causal).then_inc(small_in, 16)
                for i in range(3):
                    if i >= 2:
                        sp.wait_ge(w_lo_set, i - 1)
                    sp.dma_start(raw[:, i % 2], w_qkv[i]).then_inc(w_in[i], 16)
                sp.wait_ge(small_in, 48)

            @block.gpsimd
            def _(pool):
                nc.gpsimd.memset(qz_hi[:, :, :, :, :].bitcast(F32), 0.0).then_inc(zero_set, 1)
                nc.gpsimd.memset(qz_lo[:, :, :, :, :].bitcast(F32), 0.0).then_inc(zero_set, 1)
                nc.gpsimd.memset(v_hi[:, :, :].bitcast(F32), 0.0).then_inc(zero_set, 1)
                nc.gpsimd.memset(v_lo[:, :, :].bitcast(F32), 0.0).then_inc(zero_set, 1)
                for b in range(B):
                    if b >= 2:
                        pool.wait_ge(v_full, b - 1)
                    for i, t in enumerate((xt_hi, xt_lo)):
                        nc.gpsimd.tensor_scalar(xd[:, b % 2, i], t[:, :, b * L:(b + 1) * L].bitcast(F32).unsqueeze(2)
                                                .broadcast_to([P, KC, HP, L]), 1.0, 1.0,
                                                ALU.mult, ALU.mult).then_inc(xd_set, 1)

            @block.tensor
            def _(pe):
                def transposes(n):
                    pe.wait_ge(r_set, 2 * n + 2)
                    if n >= 2:
                        pe.wait_ge(t_free, n - 1)
                    for k in range(KC):
                        end = nc.tensor.transpose(t_ps[:, n % 2, k * P:(k + 1) * P], r_sb[:, n % 2, k * P:(k + 1) * P],
                                                  ident[:, :])
                    end.then_inc(t_full, 1)

                for n, (i, r) in enumerate(units):
                    pe.wait_ge(w_lo_set, i + 1)
                    if n >= 2:
                        pe.wait_ge(r_set, 2 * n - 2)
                    for k in range(KC):
                        rs = slice(r * P, (r + 1) * P)
                        end = product(nc, p_ps[:, n % 2, :], (xt_hi[:, k, rs], xt_lo[:, k, rs]),
                                      (w_hi[:, i, k, :], w_lo[:, i, k, :]), k == 0, k == KC - 1)
                    end.then_inc(p_full, 1)
                    if n > 0:
                        transposes(n - 1)
                transposes(len(units) - 1)
                pe.wait_ge(w_lo_set, 3)
                for b in range(B):
                    if b >= 2:
                        pe.wait_ge(v_free, b - 1)
                    pe.wait_ge(xd_set, 2 * b + 2)
                    for k in range(KC):
                        rows = [xd[:, b % 2, i, k].rearrange("p h l -> p (h l)") for i in range(2)]
                        end = product(nc, v_ps[:, b % 2, :], rows,
                                      (w_hi[:, 2, k, :], w_lo[:, 2, k, :]), k == 0, k == KC - 1)
                    end.then_inc(v_full, 1)

            def turned(n, bank):
                i, r = units[n]
                if i:
                    return [(kt_hi[:, r], kt_lo[:, r], bank.rearrange("p (k c) -> p k c", k=KC))]
                v = bank.rearrange("p (k b l) -> p b k l", k=KC, b=BR)
                return [(qz_hi[:, r, :, b, b * L:(b + 1) * L], qz_lo[:, r, :, b, b * L:(b + 1) * L], v[:, b])
                        for b in range(BR)]

            @block.scalar
            def _(act):
                for i in range(3):
                    act.wait_ge(w_in[i], 16)
                    nc.scalar.activation(w_hi[:, i], raw[:, i % 2], ACT.Copy).then_inc(w_hi_set, 1)
                act.wait_ge(small_in, 48)
                act.wait_ge(zero_set, 2)

                def high(n):
                    act.wait_ge(t_full, n + 1)
                    for hi, _, src in turned(n, t_ps[:, n % 2, :]):
                        end = nc.scalar.activation(hi, src, ACT.Copy)
                    end.then_inc(t_hi_set, 1)

                for n in range(len(units)):
                    act.wait_ge(p_full, n + 1)
                    if n >= 2:
                        act.wait_ge(r_set, 2 * n - 2)
                    nc.scalar.activation(a_sb[:, n % 2, :], p_ps[:, n % 2, :], ACT.Copy,
                                         scale=rot[:, 0:1]).then_inc(a_set, 1)
                    if n > 0:
                        high(n - 1)
                high(len(units) - 1)
                act.wait_ge(zero_set, 4)
                for b in range(B):
                    act.wait_ge(v_full, b + 1)
                    for h in range(HP):
                        end = nc.scalar.activation(of_part(v_hi[:, b, :], h), of_part(v_ps[:, b % 2, :], h), ACT.Copy)
                    end.then_inc(v_hi_set, 1)

            @block.vector
            def _(dve):
                for i in range(3):
                    dve.wait_ge(w_hi_set, i + 1)
                    nc.vector.tensor_tensor(w_lo[:, i], raw[:, i % 2], w_hi[:, i].bitcast(F32),
                                            ALU.subtract).then_inc(w_lo_set, 1)
                dve.wait_ge(small_in, 48)

                def low_part(n):
                    dve.wait_ge(t_hi_set, n + 1)
                    for hi, lo, src in turned(n, t_ps[:, n % 2, :]):
                        end = nc.vector.tensor_tensor(lo, src, hi.bitcast(F32), ALU.subtract)
                    end.then_inc(t_free, 1)

                for n in range(len(units)):
                    src = p_ps[:, n % 2, :].rearrange("p (m e) -> p e m", e=2)
                    a = a_sb[:, n % 2, :].rearrange("p (m e) -> p e m", e=2)
                    out = r_sb[:, n % 2, :].rearrange("p (m e) -> p e m", e=2)
                    dve.wait_ge(a_set, n + 1)
                    if n >= 2:
                        dve.wait_ge(t_full, n - 1)
                    nc.vector.scalar_tensor_tensor(out=out[:, 0], in0=src[:, 1], scalar=rot[:, 2:3], in1=a[:, 0],
                                                   op0=ALU.mult, op1=ALU.add).then_inc(r_set, 1)
                    nc.vector.scalar_tensor_tensor(out=out[:, 1], in0=src[:, 0], scalar=rot[:, 1:2], in1=a[:, 1],
                                                   op0=ALU.mult, op1=ALU.add).then_inc(r_set, 1)
                    if n > 0:
                        low_part(n - 1)
                low_part(len(units) - 1)
                for b in range(B):
                    dve.wait_ge(v_hi_set, b + 1)
                    for h in range(HP):
                        end = nc.vector.tensor_tensor(of_part(v_lo[:, b, :], h), of_part(v_ps[:, b % 2, :], h),
                                                      of_part(v_hi[:, b, :], h).bitcast(F32), ALU.subtract)
                    end.then_inc(v_free, 1)

        o_sb = top.sb("o_sb", [L, B, H])
        weights.place(top)
        wo_hi, wo_lo = top.sb("wo_hi", [P, KC, H], F32R), top.sb("wo_lo", [P, KC, H], F32R)

        with Scope(nc, "sa2") as sc:
            kb_hi, kb_lo = (sc.sb(n, [P, 2, BR, HC, L], F32R) for n in ("kb_hi", "kb_lo"))
            NS = 3
            s_sb = sc.sb("s_sb", [P, NS, HC, L])
            mx, sm, rs_ = sc.sb("mx", [P, 2, HC]), sc.sb("sm", [P, 2, HC]), sc.sb("rs", [P, 2, HC])
            pt_hi, pt_lo = (sc.sb(n, [P, 2, HC // HP, P], F32R) for n in ("pt_hi", "pt_lo"))
            s_ps = sc.ps("s_ps", [P, 2, 512])
            t_ps = sc.ps("t_ps", [P, 2, 512])
            o_ps = sc.ps("o_ps", [L, 2, BR, 512])
            kb_hi_set, kb_lo_set, s_full, s_read, own, d_set, e_set, r_set, p_set, t_full, t_hi_set, t_lo_set = (
                sc.sem(n) for n in ("kb_hi_set", "kb_lo_set", "s_full", "s_read", "own", "d_set", "e_set", "r_set",
                                    "p_set", "t_full", "t_hi_set", "t_lo_set"))
            o_full, o_free = sc.sem("o_full"), sc.sem("o_free")
            wo_in, wo_hi_set, wo_lo_set = sc.sem("wo_in"), sc.sem("wo_hi_set"), sc.sem("wo_lo_set")
            wo_raw = sc.sb("wo_raw", [P, KC, H])
            block = sc.block()
            units = [(r, c) for r in range(RT) for c in range(KC)]
            NU = len(units)

            def wide(t):
                return t.unsqueeze(2).broadcast_to([P, HC, L])

            def blocks(eng, out, kt, n, sem):
                r, c = units[n]
                for b in range(BR):
                    end = eng.tensor_tensor(out[:, n % 2, b], kt[:, r, c, b * L:(b + 1) * L].bitcast(F32).unsqueeze(1)
                                            .broadcast_to([P, HC, L]), wide(hm[:, :]), ALU.mult)
                end.then_inc(sem, 1)

            @block.sync
            def _(sp):
                sp.dma_start(wo_raw[:, :, :], w_o).then_inc(wo_in, 16)
                weights.load(sp)

            @block.gpsimd
            def _(pool):
                blocks(nc.gpsimd, kb_hi, kt_hi, 0, kb_hi_set)
                weights.zero(nc.gpsimd)
                for n in range(NU + 1):
                    if n + 1 < NU:
                        if n >= 1:
                            pool.wait_ge(s_full, n)
                        blocks(nc.gpsimd, kb_hi, kt_hi, n + 1, kb_hi_set)
                    if n > 0:
                        m = n - 1
                        pool.wait_ge(r_set, m + 1)
                        nc.gpsimd.tensor_tensor(s_sb[:, m % NS], s_sb[:, m % NS], wide(rs_[:, m % 2, :]),
                                                ALU.mult).then_inc(p_set, 1)
                    if 2 <= n < 2 + KC:
                        k = n - 2
                        pool.wait_ge(wo_hi_set, 1)
                        nc.gpsimd.tensor_tensor(wo_lo[:, k, :], wo_raw[:, k, :], wo_hi[:, k, :].bitcast(F32),
                                                ALU.subtract).then_inc(wo_lo_set, 1)

            @block.tensor
            def _(pe):
                def scores(n):
                    r, c = units[n]
                    pe.wait_ge(kb_hi_set, n + 1)
                    pe.wait_ge(kb_lo_set, n + 1)
                    if n >= 2:
                        pe.wait_ge(s_read, n - 1)
                    for b in range(BR):
                        end = product(nc, s_ps[:, n % 2, :], (qz_hi[:, r, c, b, :], qz_lo[:, r, c, b, :]),
                                      (kb_hi[:, n % 2, b].rearrange("p h l -> p (h l)"),
                                       kb_lo[:, n % 2, b].rearrange("p h l -> p (h l)")), b == 0, b == BR - 1)
                    end.then_inc(s_full, 1)

                def attend(n):
                    r, c = units[n]
                    pe.wait_ge(p_set, n + 1)
                    if n >= 2:
                        pe.wait_ge(t_lo_set, n - 1)
                    for i in range(HC // HP):
                        end = nc.tensor.transpose(t_ps[:, n % 2, i * P:(i + 1) * P],
                                                  s_sb[:, n % NS, i * HP:(i + 1) * HP, :].rearrange("p h l -> p (h l)"),
                                                  ident[:, :])
                    end.then_inc(t_full, 1)

                def values(n):
                    r, c = units[n]
                    pe.wait_ge(t_lo_set, n + 1)
                    if c == 0 and r > 1:
                        pe.wait_ge(o_free, r - 1)
                    for b in range(BR):
                        for i in range(HC // HP):
                            cs = slice(c * P + i * HP * HD, c * P + (i + 1) * HP * HD)
                            ls = slice(b * L, (b + 1) * L)
                            end = product(nc, o_ps[:, r % 2, b, cs], (pt_hi[:, n % 2, i, ls], pt_lo[:, n % 2, i, ls]),
                                          (v_hi[:, r * BR + b, cs], v_lo[:, r * BR + b, cs]), True, True)
                    end.then_inc(o_full, 1)

                scores(0)
                for n in range(NU + 2):
                    if n + 1 < NU:
                        scores(n + 1)
                    if 1 <= n <= NU:
                        attend(n - 1)
                    if n >= 2:
                        values(n - 2)

            def high(act, n):
                act.wait_ge(t_full, n + 1)
                if n >= 2:
                    act.wait_ge(o_full, n - 1)
                nc.scalar.activation(pt_hi[:, n % 2].rearrange("p i c -> p (i c)"), t_ps[:, n % 2, :],
                                     ACT.Copy).then_inc(t_hi_set, 1)

            @block.scalar
            def _(act):
                act.wait_ge(wo_in, 16)
                nc.scalar.activation(wo_hi[:, :, :], wo_raw[:, :, :], ACT.Copy).then_inc(wo_hi_set, 1)
                for n in range(NU):
                    act.wait_ge(d_set, n + 1)
                    nc.scalar.activation(s_sb[:, n % NS], s_sb[:, n % NS], ACT.Exp).then_inc(e_set, 1)
                    if n > 0:
                        high(act, n - 1)
                high(act, NU - 1)
                act.wait_ge(wo_lo_set, KC)
                weights.magnitudes(act, wo_raw[:, :, :].rearrange("p k h -> p (k h)"))

            @block.vector
            def _(dve):
                step = Chain(dve, own)

                def softmax(n):
                    s = s_sb[:, n % NS]
                    dve.wait_ge(s_full, n + 1)
                    if n >= NS:
                        dve.wait_ge(t_full, n - NS + 1)
                    ins = nc.vector.scalar_tensor_tensor(
                        out=s, in0=s_ps[:, n % 2, :].rearrange("p (h l) -> p h l", h=HC), scalar=SCALE,
                        in1=cm[:, :].unsqueeze(1).broadcast_to([P, HC, L]), op0=ALU.mult, op1=ALU.add)
                    ins.then_inc(s_read, 1)
                    dve.wait_ge(s_read, n + 1)
                    step(nc.vector.tensor_reduce(mx[:, n % 2, :], s, AX_X, ALU.max))
                    nc.vector.tensor_tensor(s, s, wide(mx[:, n % 2, :]), ALU.subtract).then_inc(d_set, 1)

                def sums(n):
                    dve.wait_ge(e_set, n + 1)
                    step(nc.vector.tensor_reduce(sm[:, n % 2, :], s_sb[:, n % NS], AX_X, ALU.add))
                    nc.vector.reciprocal(rs_[:, n % 2, :], sm[:, n % 2, :]).then_inc(r_set, 1)

                def low(n):
                    dve.wait_ge(t_hi_set, n + 1)
                    nc.vector.tensor_tensor(pt_lo[:, n % 2].rearrange("p i c -> p (i c)"), t_ps[:, n % 2, :],
                                            pt_hi[:, n % 2].rearrange("p i c -> p (i c)").bitcast(F32),
                                            ALU.subtract).then_inc(t_lo_set, 1)

                def output(r):
                    dve.wait_ge(o_full, (r + 1) * KC)
                    nc.vector.tensor_copy(o_sb[:, r * BR:(r + 1) * BR, :], o_ps[:, r % 2]).then_inc(o_free, 1)

                blocks(nc.vector, kb_lo, kt_lo, 0, kb_lo_set)
                for n in range(NU + 2):
                    if n + 1 < NU:
                        if n >= 1:
                            dve.wait_ge(s_full, n)
                        blocks(nc.vector, kb_lo, kt_lo, n + 1, kb_lo_set)
                    if n < NU:
                        softmax(n)
                    if n > KC and n % KC == 2 % KC:
                        output(n // KC - 1)
                    if 1 <= n <= NU:
                        sums(n - 1)
                    if n >= 2:
                        low(n - 2)
                output(RT - 1)

        with Scope(nc, "sa3") as sc:
            ot_hi, ot_lo = sc.sb("ot_hi", [P, KC, R], F32R), sc.sb("ot_lo", [P, KC, R], F32R)
            t_ps = sc.ps("t_ps", [P, RT, 512])
            ps = sc.ps("ps", [P, RT, 512])
            spare = sc.sb("spare", [P, weights.WIDEST])
            t_full, hi_set, lo_set, done = (sc.sem(n) for n in ("t_full", "hi_set", "lo_set", "done"))
            block = sc.block()

            @block.gpsimd
            def _(pool):
                pool.wait_ge(weights.tern_set, 1)
                weights.spread(nc.gpsimd, 1)

            @block.tensor
            def _(pe):
                for r in range(RT):
                    for k in range(KC):
                        for b in range(BR):
                            o = k * P + b * L
                            end = nc.tensor.transpose(t_ps[:, r, o:o + L], o_sb[:, r * BR + b, k * P:(k + 1) * P],
                                                      ident[0:L, 0:L])
                    end.then_inc(t_full, 1)
                for r in range(RT):
                    pe.wait_ge(lo_set, r + 1)
                    if r == 0:
                        weights.totals(pe, t_ps[:, 0, :], ones)
                    rs = slice(r * P, (r + 1) * P)
                    for k in range(KC):
                        end = product(nc, ps[:, r, :], (ot_hi[:, k, rs], ot_lo[:, k, rs]),
                                      (wo_hi[:, k, :], wo_lo[:, k, :]), k == 0, k == KC - 1)
                    end.then_inc(done, 1)

            @block.scalar
            def _(act):
                for r in range(RT):
                    act.wait_ge(t_full, r + 1)
                    nc.scalar.activation(ot_hi[:, :, r * P:(r + 1) * P], t_ps[:, r, :].rearrange("p (k c) -> p k c", k=KC),
                                         ACT.Copy).then_inc(hi_set, 1)

            @block.vector
            def _(dve):
                for r in range(RT):
                    dve.wait_ge(hi_set, r + 1)
                    rs = slice(r * P, (r + 1) * P)
                    nc.vector.tensor_tensor(ot_lo[:, :, rs], t_ps[:, r, :].rearrange("p (k c) -> p k c", k=KC),
                                            ot_hi[:, :, rs].bitcast(F32), ALU.subtract).then_inc(lo_set, 1)
                dve.wait_ge(weights.sign_in_set, 48)
                weights.ternary(dve, t_ps[:, 0, :], spare)
                weights.spread(nc.vector, 0)
                for r in range(RT):
                    dve.wait_ge(done, r + 1)
                    nc.vector.tensor_tensor(x_sb[:, r, :], ps[:, r, :], x_sb[:, r, :], ALU.add)


def octonion_ffn(nc, x_sb, xt_hi, xt_lo, weights):
    RT, H = x_sb.shape[1:]
    KC, FC, width, scale = weights.KC, weights.FC, weights.width, weights.scale
    R = RT * P

    with Scope(nc, "fo") as sc:
        g_sb, h_sb = sc.sb("g_sb", [P, 2, R]), sc.sb("h_sb", [P, 2, R])
        h_hi, h_lo = sc.sb("h_hi", [P, 2, R], F32R), sc.sb("h_lo", [P, 2, R], F32R)
        tern_d = sc.sb("tern_d", [P, FC, 8, weights.D8], F32R)
        gu_ps = sc.ps("gu_ps", [P, 4, 512])
        ps = sc.ps("ps", [P, RT, 512])
        gu_full, g_set, u_read, h_hi_set, h_lo_set, used, done = (
            sc.sem(n) for n in ("gu_full", "g_set", "u_read", "h_hi_set", "h_lo_set", "used", "done"))
        block = sc.block()

        @block.gpsimd
        def _(pool):
            weights.spread_down(nc.gpsimd, tern_d)

        @block.tensor
        def _(pe):
            def down(c):
                w = width(c)
                pe.wait_ge(h_lo_set, c + 1)
                pe.wait_ge(weights.down_set, c + 1)
                for r in range(RT):
                    rs = slice(r * P, (r + 1) * P)
                    t = tern_d[0:w, c].rearrange("p k o -> p (k o)")
                    nc.tensor.matmul(ps[:, r, :], h_hi[0:w, c % 2, rs], t, start=c == 0, stop=False)
                    end = nc.tensor.matmul(ps[:, r, :], h_lo[0:w, c % 2, rs], t, start=False, stop=c == FC - 1)
                    if c == FC - 1:
                        end.then_inc(done, 1)
                if c < FC - 1:
                    end.then_inc(used, 1)

            for c in range(FC):
                w = width(c)
                for i in range(2):
                    if c >= 2:
                        pe.wait_ge((g_set, u_read)[i], c - 1)
                    for k in range(KC):
                        o = gu_ps[0:w, 2 * (c % 2) + i, :]
                        t = weights.columns(i, k, c)
                        nc.tensor.matmul(o, t, xt_hi[:, k, :], start=k == 0, stop=False)
                        end = nc.tensor.matmul(o, t, xt_lo[:, k, :], start=False, stop=k == KC - 1)
                    end.then_inc(gu_full, 1)
                if c > 0:
                    down(c - 1)
            down(FC - 1)

        @block.scalar
        def _(act):
            def high(c):
                w = width(c)
                act.wait_ge(u_read, c + 1)
                if c >= 2:
                    act.wait_ge(used, c - 1)
                nc.scalar.activation(h_hi[0:w, c % 2, :], h_sb[0:w, c % 2, :], ACT.Copy).then_inc(h_hi_set, 1)

            for c in range(FC):
                w = width(c)
                act.wait_ge(gu_full, 2 * c + 1)
                if c >= 2:
                    act.wait_ge(u_read, c - 1)
                nc.scalar.activation(g_sb[0:w, c % 2, :], gu_ps[0:w, 2 * (c % 2), :], ACT.Silu,
                                     scale=scale[0:w, 0:1]).then_inc(g_set, 1)
                if c > 0:
                    high(c - 1)
            high(FC - 1)

        @block.vector
        def _(dve):
            def low(c):
                w = width(c)
                dve.wait_ge(h_hi_set, c + 1)
                nc.vector.tensor_tensor(h_lo[0:w, c % 2, :], h_sb[0:w, c % 2, :], h_hi[0:w, c % 2, :].bitcast(F32),
                                        ALU.subtract).then_inc(h_lo_set, 1)

            for c in range(FC):
                w = width(c)
                dve.wait_ge(g_set, c + 1)
                dve.wait_ge(gu_full, 2 * c + 2)
                if c >= 2:
                    dve.wait_ge(h_lo_set, c - 1)
                nc.vector.scalar_tensor_tensor(out=h_sb[0:w, c % 2, :], in0=gu_ps[0:w, 2 * (c % 2) + 1, :],
                                               scalar=scale[0:w, 1:2], in1=g_sb[0:w, c % 2, :],
                                               op0=ALU.mult, op1=ALU.mult).then_inc(u_read, 1)
                if c > 0:
                    low(c - 1)
            low(FC - 1)
            for r in range(RT):
                dve.wait_ge(done, r + 1)
                nc.vector.scalar_tensor_tensor(out=x_sb[:, r, :], in0=ps[:, r, :], scalar=scale[:, 2:3],
                                               in1=x_sb[:, r, :], op0=ALU.mult, op1=ALU.add)


def attention_constants(L, HD):
    step = np.arange(P) % L
    angle = step.astype(np.float32)
    return {
        "rotary": np.stack([np.cos(angle), np.sin(angle), -np.sin(angle)], 1),
        "head_mask": (np.arange(P)[:, None] // HD == np.arange(P // HD)).astype(np.float32),
        "causal": np.where(np.arange(L) <= step[:, None], np.float32(0), np.float32(-1e30)),
    }


def octonion_signs():
    s = np.zeros((8, 8, 8), np.float32)
    s[0, 0, 0] = 1
    for i in range(1, 8):
        s[0, i, i] = s[i, 0, i] = 1
        s[i, i, 0] = -1
    for a, b, c in [(1, 2, 3), (1, 4, 5), (1, 7, 6), (2, 4, 6), (2, 5, 7), (3, 4, 7), (3, 6, 5)]:
        for x, y, z in ((a, b, c), (b, c, a), (c, a, b)):
            s[x, y, z], s[y, x, z] = 1, -1
    return s.sum(0)


def perceiver(nc, x, ctx, ctx_t, identity, xa, ma, fl, sa, of, out):
    B = ctx.shape[0]
    _, RT, H = x.shape
    R = RT * P
    NKV = xa["wk"].shape[0]
    GL = xa["wq"].shape[3] * (R // B) // P
    q_dram = nc.dram_tensor("q_scratch", (B, NKV, P, GL), F32, kind="Internal").ap()
    o_dram = nc.dram_tensor("o_scratch", (B, NKV, P, GL), F32, kind="Internal").ap()
    c_dram = nc.dram_tensor("c_scratch", (B, R // B, H), F32, kind="Internal").ap()
    with Scope(nc, "all") as sc:
        x_sb, ident, ones = sc.sb("x", [P, RT, H]), sc.sb("ident", [P, P]), sc.sb("ones", [P, P])
        x_in, x_out = sc.sem("x_in"), sc.sem("x_out")
        with nc.Block() as block:
            @block.gpsimd
            def _(pool):
                nc.gpsimd.memset(ones[:, :], 1.0)

            @block.sync
            def _(sp):
                sp.dma_start(x_sb[:, :, :], x).then_inc(x_in, 16)
                sp.dma_start(ident[:, :], identity).then_inc(x_in, 16)
                sp.wait_ge(x_in, 32)

        def normalised(name, stage):
            with Scope(nc, name) as s:
                xt_hi, xt_lo = s.sb("xt_hi", [P, H // P, R], F32R), s.sb("xt_lo", [P, H // P, R], F32R)
                layernorm_transposed(nc, f"{name}_ln", x_sb, xt_hi, xt_lo, ident)
                stage(xt_hi, xt_lo)

        normalised("n0", lambda hi, lo: queries(nc, hi, lo, xa["wq"], xa["bq"], q_dram))
        cross_attention(nc, ctx_t, xa["wk"], xa["wv"], xa["bk"], xa["bv"], ident, q_dram, o_dram)
        attention_output(nc, x_sb, o_dram, xa["wo"], xa["bo"])
        mamba(nc, x_sb, ident, B, **ma)
        normalised("n2", lambda hi, lo: ternary_linear(nc, x_sb, hi, lo, fl["w"], fl["bias"], ones))
        normalised("n3", lambda hi, lo: context_attention(nc, x_sb, hi, lo, ctx, ident, c_dram))
        with Scope(nc, "of") as s:
            weights = OctonionWeights(nc, s, of)
            normalised("n4", lambda hi, lo: self_attention(nc, x_sb, hi, lo, sa["w_qkv"], sa["w_o"], sa["rotary"],
                                                           sa["head_mask"], sa["causal"], ident, ones, B, 32, weights))
            normalised("n5", lambda hi, lo: octonion_ffn(nc, x_sb, hi, lo, weights))
        with nc.Block() as block:
            @block.sync
            def _(sp):
                sp.dma_start(out, x_sb[:, :, :]).then_inc(x_out, 16)
                sp.wait_ge(x_out, 16)


def kernel(**inputs):
    import numpy as np
    import concourse.bacc as bacc
    from concourse.bass_utils import run_bass_kernel_spmd

    def lay(a):
        return np.ascontiguousarray(a)

    def rows(w, shape=None):
        w = np.asarray(w)
        return lay(w.reshape(-1, P, *w.shape[1:]).swapaxes(0, 1))

    i = {k: np.asarray(v) for k, v in inputs.items()}
    B, L, H = i["x"].shape
    S = i["ctx_4096"].shape[1]
    NKV, D, NH = 8, 128, 32
    G = NH // NKV
    KD = NKV * D
    wkv = i["L0_xattn_Wkv"]
    sign = octonion_signs()
    O, D8 = i["L1_ffn_w_gate"].shape[1:]
    MAIN = min(O, P)
    LEFT = O - MAIN
    PARTS = P // LEFT
    REST_CHUNKS = -(-8 // PARTS)

    def halves(w):
        return lay(np.concatenate([w[np.arange(8) ^ p].transpose(2, 0, 1) for p in range(P // D8)]))

    def rest(t):
        out = np.zeros((REST_CHUNKS * PARTS, *t.shape[1:]), t.dtype)
        out[:8] = t
        out = out.reshape(REST_CHUNKS, PARTS * LEFT, *t.shape[2:]).swapaxes(0, 1)
        return lay(np.concatenate([out, np.zeros((P - len(out), *out.shape[1:]), t.dtype)]))

    pick = np.arange(8)[:, None] ^ np.arange(8)
    down = i["L1_ffn_w_down"].transpose(2, 0, 1)

    groups = {
        "xa": {
            "wq": lay(i["L0_xattn_Wq"].reshape(H // P, P, NKV, G * D).transpose(2, 1, 0, 3)),
            "bq": lay(i["L0_xattn_bq"].reshape(NH, D).T),
            "wk": lay(wkv[:, :KD].reshape(H // P, P, NKV, D).transpose(2, 1, 0, 3)),
            "wv": lay(wkv[:, KD:].reshape(H // P, P, NKV // 2, 2 * D).transpose(2, 1, 0, 3)),
            "bk": lay(i["L0_xattn_bkv"][:KD].reshape(NKV, D).T),
            "bv": lay(i["L0_xattn_bkv"][KD:].reshape(NKV, D).T),
            "wo": lay(i["L0_xattn_Wo"].reshape(NKV, G, D, H).transpose(0, 2, 1, 3)),
            "bo": lay(i["L0_xattn_bo"]),
        },
        "ma": {
            "w_in": lay(i["L0_attn_W_in"].T.reshape(H // P, P, 2, -1, P).transpose(3, 1, 2, 0, 4)),
            "conv_w": rows(i["L0_attn_conv_w"]),
            "conv_b": rows(i["L0_attn_conv_b"]),
            "w_x": rows(i["L0_attn_W_x"].T),
            "w_dt": lay(i["L0_attn_W_dt"].T),
            "b_dt": rows(i["L0_attn_b_dt"]),
            "a_log": rows(i["L0_attn_A_log"]),
            "d_skip": rows(i["L0_attn_D"]),
            "w_out": rows(i["L0_attn_W_out"].T),
        },
        "fl": {"w": rows(i["L0_ffn_weight"].T), "bias": lay(i["L0_ffn_bias"])},
        "sa": {
            "w_qkv": np.stack([rows(i[f"L1_attn_w{n}"].T) for n in "qkv"]),
            "w_o": rows(i["L1_attn_wo"].T),
            **attention_constants(L, H // NH),
        },
        "of": {
            "w_gate": halves(i["L1_ffn_w_gate"]),
            "w_up": halves(i["L1_ffn_w_up"]),
            "w_down": lay(down[:MAIN]),
            "w_rest": rest(down[MAIN:][:, pick].swapaxes(0, 1)),
            "sign_in": rows(np.repeat(sign, D8, 0)),
            "sign_down": lay(np.broadcast_to(sign, (P, 8, 8))),
            "sign_rest": rest(np.repeat(sign[:, None], LEFT, 1)),
        },
    }
    alone = {
        "x": rows(i["x"].reshape(B * L, H)),
        "ctx": lay(i["ctx_4096"]),
        "ctx_t": lay(i["ctx_4096"].transpose(0, 2, 1).reshape(B, H // P, P, S).swapaxes(1, 2)),
        "identity": np.eye(P, dtype=np.float32),
    }

    nc = bacc.Bacc("TRN2", target_bir_lowering=False, num_devices=1)
    arrays = {}

    def given(name, a):
        arrays[f"in_{name}"] = a
        return nc.dram_tensor(f"in_{name}", a.shape, mybir.dt.from_np(a.dtype), kind="ExternalInput").ap()

    args = {n: given(n, a) for n, a in alone.items()}
    args |= {g: {n: given(f"{g}_{n}", a) for n, a in m.items()} for g, m in groups.items()}
    out = nc.dram_tensor("out", alone["x"].shape, F32, kind="ExternalOutput").ap()
    perceiver(nc, out=out, **args)
    r = run_bass_kernel_spmd(nc, [arrays], core_ids=[0])
    return np.asarray(r.results[0]["out"]).swapaxes(0, 1).reshape(B, L, H)
```

```python
from contextlib import ExitStack

import numpy as np
import concourse.bass as bass
from concourse import mybir
from concourse.alu_op_type import AluOpType as ALU

F32 = mybir.dt.float32
F32R = mybir.dt.float32r
ACT = mybir.ActivationFunctionType
AX_X = mybir.AxisListType.X
P = 128


class Scope:

    def __init__(self, nc, name):
        self.nc, self.name, self.stack, self.sems = nc, name, ExitStack(), []

    def __enter__(self):
        self.stack.__enter__()
        return self

    def __exit__(self, *a):
        self.stack.__exit__(*a)
        if self.sems:
            self.nc.clear_and_free_semaphores(self.sems)
            self.nc.all_engine_barrier()

    def sb(self, name, shape, dt=F32):
        return self.stack.enter_context(self.nc.sbuf_tensor(f"{self.name}_{name}", shape, dt))

    def ps(self, name, shape):
        return self.stack.enter_context(self.nc.psum_tensor(f"{self.name}_{name}", shape, F32))

    def sem(self, name):
        self.sems.append(self.nc.alloc_semaphore(f"{self.name}_{name}"))
        return self.sems[-1]

    def block(self):
        return self.stack.enter_context(self.nc.Block())


def apart(eng, passed):
    eng.sem_inc(passed, 1)


def product(nc, out, left, right, first, last):
    nc.tensor.matmul(out, left[0], right[0], start=first, stop=False)
    nc.tensor.matmul(out, left[0], right[1], start=False, stop=False)
    return nc.tensor.matmul(out, left[1], right[0], start=False, stop=last)


def even_tiles(n, most=512):
    count = -(-n // most)
    step = -(-n // (2 * count)) * 2
    return [(c, min(step, n - c)) for c in range(0, n, step)]


class Context:
    LO_DVE = 1

    def __init__(self, nc, scope, ctx_t):
        self.nc, self.ctx_t = nc, ctx_t
        _, _, KC, self.S = ctx_t.shape
        self.SE = self.S + self.S % 2
        self.TILES = even_tiles(self.SE)
        self.raw = scope.sb("raw", [P, KC, self.SE])
        self.hi, self.lo = scope.sb("hi", [P, KC, self.SE], F32R), scope.sb("lo", [P, KC, self.SE], F32R)
        self.loaded = [scope.sem(f"loaded{t}") for t in range(len(self.TILES))]
        self.pad_set, self.hi_set, self.lo_dve, self.lo_pool = (
            scope.sem(n) for n in ("pad_set", "hi_set", "lo_dve", "lo_pool"))

    def load(self, sp, b):
        for t, (c, w) in enumerate(self.TILES):
            w = min(w, self.S - c)
            sp.dma_start(self.raw[:, :, c:c + w], self.ctx_t[b][:, :, c:c + w]).then_inc(self.loaded[t], 16)

    def split_first(self, pool):
        self.nc.gpsimd.memset(self.raw[:, :, self.SE - 1:self.SE], 0.0).then_inc(self.pad_set, 1)
        pool.wait_ge(self.pad_set, 1)
        for t, (c, w) in enumerate(self.TILES):
            pool.wait_ge(self.loaded[t], 16)
            src, hi = self.raw[:, :, c:c + w], self.hi[:, :, c:c + w]
            self.nc.gpsimd.tensor_scalar(hi, src, 1.0, 1.0, ALU.mult, ALU.mult).then_inc(self.hi_set, 1)
            pool.wait_ge(self.hi_set, t + 1)
            self.nc.gpsimd.tensor_tensor(self.lo[:, :, c:c + w], src, hi.bitcast(F32), ALU.subtract
                                         ).then_inc(self.lo_dve if t < self.LO_DVE else self.lo_pool, 1)


def cross_attention(nc, context, wk, wv, bk, bv, ident, q_dram, o_dram):
    B, _, KC, S = context.ctx_t.shape
    NKV = wk.shape[0]
    D = wk.shape[3]
    NQ = q_dram.shape[3]
    NU = NQ // P
    SE, TILES = context.SE, context.TILES
    NC = -(-S // P)
    NG = -(-NC // 2)
    NT = len(TILES)
    SCALE = float(D) ** -0.5
    NPT = 2
    LO_DVE = context.LO_DVE

    def rows(c):
        return min(P, S - c * P)

    KV_TILES = NKV * NT + NKV // 2 * NG
    S_TILES = NKV * NU * NT
    PAIRS = NKV * NG

    def kv_tile(j):
        return j * NT + (j + 1) // 2 * NG

    def projections(b, j, last):
        tiles = []
        if j % 2 == 0:
            tiles += [("v", j, g, kv_tile(j) + NT + g) for g in range(NG)]
        if not (last and j == NKV - 1):
            tiles += [("k", j + 1, t, kv_tile(j + 1) + t) for t in range(NT)]
        return tiles

    def kv_done(b, tiles):
        return b * KV_TILES + tiles + KV_TILES

    def drive(eng, first, group, tail):
        first()
        with eng.Fori(0, B - 1) as b:
            for j in range(1, NKV + 1):
                group(b, j, False)
        for j in range(1, NKV):
            group(B - 1, j, True)
        tail(B - 1)

    with Scope(nc, "xa") as sc:
        raw, ctx_hi, ctx_lo = context.raw, context.hi, context.lo
        wk_raw = sc.sb("wk_raw", [P, 2, KC, D])
        wk_hi, wk_lo = sc.sb("wk_hi", [P, 2, KC, D], F32R), sc.sb("wk_lo", [P, 2, KC, D], F32R)
        wv_raw = sc.sb("wv_raw", [P, KC, 2 * D])
        wv_hi, wv_lo = sc.sb("wv_hi", [P, KC, 2 * D], F32R), sc.sb("wv_lo", [P, KC, 2 * D], F32R)
        q_raw = sc.sb("q_raw", [P, 2, NQ])
        q_hi, q_lo = sc.sb("q_hi", [P, 2, NQ], F32R), sc.sb("q_lo", [P, 2, NQ], F32R)
        k_hi, k_lo = sc.sb("k_hi", [P, SE], F32R), sc.sb("k_lo", [P, SE], F32R)
        v_hi, v_lo = sc.sb("v_hi", [P, NC, 2 * D], F32R), sc.sb("v_lo", [P, NC, 2 * D], F32R)
        prob = sc.sb("prob", [P, 2, NU, SE])
        pt_hi, pt_lo = sc.sb("pt_hi", [P, NPT, 2, NQ], F32R), sc.sb("pt_lo", [P, NPT, 2, NQ], F32R)
        tmax = sc.sb("tmax", [P, NU, NT])
        nmax = sc.sb("nmax", [P, NU])
        den = sc.sb("den", [P, NU])
        rden = sc.sb("rden", [P, NU])
        o_sb = sc.sb("o_sb", [P, 2, NQ])
        bk_sb, bv_sb = sc.sb("bk_sb", [P, NKV]), sc.sb("bv_sb", [P, NKV])
        kv_ps = sc.ps("kv_ps", [P, 2, 512])
        s_ps = sc.ps("s_ps", [P, 2, 512])
        t_ps = sc.ps("t_ps", [P, 2, 512])
        o_ps = sc.ps("o_ps", [P, 2, 512])

        bias_in = sc.sem("bias_in")
        ctx_in, ctx_hi_set, ctx_lo_dve, ctx_lo_pool = context.loaded, context.hi_set, context.lo_dve, context.lo_pool
        wk_in = [sc.sem(f"wk_in{i}") for i in range(2)]
        wv_in = sc.sem("wv_in")
        q_in = [sc.sem(f"q_in{i}") for i in range(2)]
        passed, passed_sp = sc.sem("passed"), sc.sem("passed_sp")
        w_hi_set = sc.sem("w_hi_set")
        wk_split, wv_split, q_split = sc.sem("wk_split"), sc.sem("wv_split"), sc.sem("q_split")
        kv_full, kv_hi, kv_free = sc.sem("kv_full"), sc.sem("kv_hi"), sc.sem("kv_free")
        s_full, s_free = sc.sem("s_full"), sc.sem("s_free")
        nmax_set, exp_done, rden_set, prob_set = (
            sc.sem("nmax_set"), sc.sem("exp_done"), sc.sem("rden_set"), sc.sem("prob_set"))
        t_full, t_hi, t_free = sc.sem("t_full"), sc.sem("t_hi"), sc.sem("t_free")
        pt_free = sc.sem("pt_free")
        o_free = sc.sem("o_free")
        o_out = [sc.sem(f"o_out{i}") for i in range(2)]
        block = sc.block()

        @block.sync
        def _(sp):
            def weights(b, j):
                n = b * NKV + j
                g = j % NKV
                sp.wait_ge(wk_split, n + 1)
                sp.dma_start(wk_raw[:, j % 2], wk[g]).then_inc(wk_in[j % 2], 16)
                sp.wait_ge(q_split, n + 1)
                sp.dma_start(q_raw[:, j % 2], q_dram[b + j // NKV, g]).then_inc(q_in[j % 2], 16)
                if j % 2 == 0:
                    sp.wait_ge(wv_split, b * (NKV // 2) + j // 2 + 1)
                    sp.dma_start(wv_raw[:, :, :], wv[g // 2]).then_inc(wv_in, 16)

            def store(b, j):
                sp.wait_ge(o_free, b * NKV + j + 3)
                apart(sp, passed_sp)
                sp.dma_start(o_dram[b, j], o_sb[:, j % 2]).then_inc(o_out[j % 2], 16)

            def group(b, j, last):
                if not (last and j == NKV - 1):
                    weights(b, j + 1)
                if j == 2 and not last:
                    sp.wait_ge(ctx_lo_dve, b * LO_DVE + LO_DVE)
                    sp.wait_ge(ctx_lo_pool, b * (NT - LO_DVE) + NT - LO_DVE)
                    context.load(sp, b + 1)
                store(b, j - 1)

            def first():
                weights(0, 0)
                weights(0, 1)
                sp.dma_start(bk_sb[:, :], bk).then_inc(bias_in, 16)
                sp.dma_start(bv_sb[:, :], bv).then_inc(bias_in, 16)

            drive(sp, first, group, lambda b: store(b, NKV - 1))
            for i in range(2):
                sp.wait_ge(o_out[i], (B * NKV // 2 + 1) * 16)

        @block.gpsimd
        def _(pool):
            def halves(hi, lo, src, count):
                apart(pool, passed)
                nc.gpsimd.tensor_scalar(hi, src, 1.0, 1.0, ALU.mult, ALU.mult).then_inc(w_hi_set, 1)
                pool.wait_ge(w_hi_set, count)
                return nc.gpsimd.tensor_tensor(lo, src, hi.bitcast(F32), ALU.subtract)

            def split_ctx(b, n):
                for t, (c, w) in enumerate(TILES):
                    pool.wait_ge(ctx_in[t], (n + 1) * 16)
                    pool.wait_ge(kv_full, kv_done(b, kv_tile(NKV - 1) + t + 1))
                    apart(pool, passed)
                    nc.gpsimd.tensor_scalar(ctx_hi[:, :, c:c + w], raw[:, :, c:c + w], 1.0, 1.0,
                                            ALU.mult, ALU.mult).then_inc(ctx_hi_set, 1)
                for t, (c, w) in enumerate(TILES):
                    if t >= LO_DVE:
                        pool.wait_ge(ctx_hi_set, n * NT + t + 1)
                        nc.gpsimd.tensor_tensor(ctx_lo[:, :, c:c + w], raw[:, :, c:c + w],
                                                ctx_hi[:, :, c:c + w].bitcast(F32),
                                                ALU.subtract).then_inc(ctx_lo_pool, 1)

            def weights(b, j):
                k = b * (2 * NKV + NKV // 2) + 2 * j + (j + 1) // 2
                pool.wait_ge(wk_in[j % 2], (b * (NKV // 2) + j // 2 + 1) * 16)
                pool.wait_ge(kv_full, kv_done(b, kv_tile(j - 2) + NT))
                halves(wk_hi[:, j % 2], wk_lo[:, j % 2], wk_raw[:, j % 2], k + 1).then_inc(wk_split, 1)
                pool.wait_ge(q_in[j % 2], (b * (NKV // 2) + j // 2 + 1) * 16)
                pool.wait_ge(s_full, b * S_TILES + (j - 1) * NU * NT + S_TILES)
                halves(q_hi[:, j % 2], q_lo[:, j % 2], q_raw[:, j % 2], k + 2).then_inc(q_split, 1)
                if j % 2 == 0:
                    pool.wait_ge(wv_in, (b * (NKV // 2) + j // 2 + 1) * 16)
                    pool.wait_ge(kv_full, kv_done(b, kv_tile(j - 2) + NT + NG))
                    halves(wv_hi[:, :, :], wv_lo[:, :, :], wv_raw[:, :, :], k + 3).then_inc(wv_split, 1)

            def first():
                pool.sem_inc(wk_split, 2)
                pool.sem_inc(q_split, 2)
                pool.sem_inc(wv_split, 1)
                weights(0, 0)

            def group(b, j, last):
                weights(b, j)
                if j == NKV:
                    split_ctx(b, b + 1)

            drive(pool, first, group, lambda b: None)

        @block.tensor
        def _(pe):
            pe.sem_inc(kv_full, KV_TILES)
            pe.sem_inc(s_full, S_TILES)
            pe.sem_inc(pt_free, NPT)

            def key_tile(b, j, t, n):
                c, w = TILES[t]
                if t == 0:
                    pe.wait_ge(wk_split, b * NKV + j + 3)
                if j % NKV == 0:
                    at = b + j // NKV
                    pe.wait_ge(ctx_hi_set, at * NT + t + 1)
                    if t < LO_DVE:
                        pe.wait_ge(ctx_lo_dve, at * LO_DVE + t + 1)
                    else:
                        pe.wait_ge(ctx_lo_pool, at * (NT - LO_DVE) + t + 1 - LO_DVE)
                pe.wait_ge(kv_free, b * KV_TILES + n + 1)
                for kc in range(KC):
                    end = product(nc, kv_ps[:, n % 2, 0:w],
                                  (wk_hi[:, j % 2, kc], wk_lo[:, j % 2, kc]),
                                  (ctx_hi[:, kc, c:c + w], ctx_lo[:, kc, c:c + w]), kc == 0, kc == KC - 1)
                end.then_inc(kv_full, 1)

            def value_tile(b, j, g, n):
                if g == 0:
                    pe.wait_ge(wv_split, b * (NKV // 2) + j // 2 + 2)
                pe.wait_ge(kv_free, b * KV_TILES + n + 1)
                for c in range(2 * g, min(2 * g + 2, NC)):
                    for kc in range(KC):
                        s = slice(c * P, c * P + rows(c))
                        o = (c % 2) * 2 * D
                        end = product(nc, kv_ps[0:rows(c), n % 2, o:o + 2 * D],
                                      (ctx_hi[:, kc, s], ctx_lo[:, kc, s]),
                                      (wv_hi[:, kc, :], wv_lo[:, kc, :]), kc == 0, kc == KC - 1)
                end.then_inc(kv_full, 1)

            def project(b, j, last):
                for kind, at, t, n in projections(b, j, last):
                    (key_tile if kind == "k" else value_tile)(b, at, t, n)

            def score_tile(b, j, i):
                u, t = divmod(i, NT)
                c, w = TILES[t]
                n = j * NU * NT + i
                if i == 0:
                    pe.wait_ge(q_split, b * NKV + j + 3)
                if u == 0:
                    pe.wait_ge(kv_free, b * KV_TILES + kv_tile(j) + t + 3)
                pe.wait_ge(s_free, b * S_TILES + n + 1)
                us = slice(u * P, (u + 1) * P)
                product(nc, s_ps[:, n % 2, 0:w], (q_hi[:, j % 2, us], q_lo[:, j % 2, us]),
                        (k_hi[:, c:c + w], k_lo[:, c:c + w]), True, True).then_inc(s_full, 1)

            def transposes(b, j, g):
                n = j * NG + g
                if g == 0:
                    pe.wait_ge(prob_set, b * (NKV * NU) + j * NU + NU)
                pe.wait_ge(t_free, b * PAIRS + n + 1)
                for c in range(2 * g, min(2 * g + 2, NC)):
                    r = rows(c)
                    for u in range(NU):
                        o = (c % 2) * NQ + u * P
                        end = nc.tensor.transpose(t_ps[0:r, n % 2, o:o + P],
                                                  prob[:, j % 2, u, c * P:c * P + r], ident[:, :])
                end.then_inc(t_full, 1)

            def pv(b, j, g):
                n = j * NG + g
                if g == 0:
                    pe.wait_ge(o_free, b * NKV + j + 1)
                pe.wait_ge(t_free, b * PAIRS + n + 3)
                for c in range(2 * g, min(2 * g + 2, NC)):
                    r = rows(c)
                    d = slice((j % 2) * D, (j % 2 + 1) * D)
                    end = product(nc, o_ps[:, j % 2, 0:NQ], (v_hi[0:r, c, d], v_lo[0:r, c, d]),
                                  (pt_hi[0:r, n % NPT, c % 2], pt_lo[0:r, n % NPT, c % 2]), c == 0, c == NC - 1)
                end.then_inc(pt_free, 1)

            def first():
                for t in range(NT):
                    key_tile(0, 0, t, t)
                for i in range(NU * NT):
                    score_tile(0, 0, i)
                project(0, 0, False)

            def group(b, j, last):
                for i in range(max(NU * NT, NG)):
                    if i < NU * NT:
                        score_tile(b, j, i)
                    if 2 <= i < NG + 2:
                        pv(b, j - 1, i - 2)
                    if i < NG:
                        transposes(b, j - 1, i)
                for g in range(max(NU * NT, NG) - 2, NG):
                    pv(b, j - 1, g)
                project(b, j, last)

            def tail(b):
                for i in range(NG + 1):
                    if i < NG:
                        transposes(b, NKV - 1, i)
                    if i > 0:
                        pv(b, NKV - 1, i - 1)

            drive(pe, first, group, tail)

        @block.scalar
        def _(act):
            def key_tile(b, j, t, n):
                c, w = TILES[t]
                act.wait_ge(kv_full, kv_done(b, n + 1))
                nc.scalar.activation(k_hi[:, c:c + w], kv_ps[:, n % 2, 0:w], ACT.Identity,
                                     bias=bk_sb[:, j % NKV:j % NKV + 1]).then_inc(kv_hi, 1)

            def value_tile(b, j, g, n):
                act.wait_ge(kv_full, kv_done(b, n + 1))
                m = min(2, NC - 2 * g)
                r = rows(2 * g)
                nc.scalar.activation(v_hi[0:r, 2 * g:2 * g + m, :],
                                     kv_ps[0:r, n % 2, 0:m * 2 * D].rearrange("p (c d) -> p c d", c=m),
                                     ACT.Copy).then_inc(kv_hi, 1)

            def exponentials(b, j, u):
                act.wait_ge(nmax_set, b * (NKV * NU) + j * NU + u + 1)
                nc.scalar.activation(prob[:, j % 2, u, 0:S], prob[:, j % 2, u, 0:S], ACT.Exp, bias=nmax[:, u:u + 1],
                                     accum_out=den[:, u:u + 1]).then_inc(exp_done, 1)

            def softmax_and_project(b, j, last):
                exponentials(b, j, 0)
                tiles = projections(b, j, last)
                for i, (kind, at, t, n) in enumerate(tiles):
                    (key_tile if kind == "k" else value_tile)(b, at, t, n)
                    if 0 <= i < NU - 1:
                        exponentials(b, j, i + 1)
                if not tiles:
                    for u in range(1, NU):
                        exponentials(b, j, u)

            def attend(b, j):
                for g in range(NG):
                    n = j * NG + g
                    m = min(2, NC - 2 * g)
                    r = rows(2 * g)
                    act.wait_ge(t_full, b * PAIRS + n + 1)
                    act.wait_ge(pt_free, b * PAIRS + n + 1)
                    nc.scalar.activation(pt_hi[0:r, n % NPT, 0:m, :],
                                         t_ps[0:r, n % 2, 0:m * NQ].rearrange("p (c d) -> p c d", c=m),
                                         ACT.Copy).then_inc(t_hi, 1)
                act.wait_ge(pt_free, b * PAIRS + (j + 1) * NG + NPT)
                act.wait_ge(o_out[j % 2], (b * (NKV // 2) + j // 2 + 1) * 16)
                nc.scalar.activation(o_sb[:, j % 2], o_ps[:, j % 2, 0:NQ], ACT.Identity,
                                     bias=bv_sb[:, j:j + 1]).then_inc(o_free, 1)

            def first():
                act.sem_inc(o_free, 2)
                act.sem_inc(o_out[0], 16)
                act.sem_inc(o_out[1], 16)
                act.wait_ge(bias_in, 32)
                for t in range(NT):
                    key_tile(0, 0, t, t)
                softmax_and_project(0, 0, False)

            def group(b, j, last):
                attend(b, j - 1)
                softmax_and_project(b, j, last)

            drive(act, first, group, lambda b: attend(b, NKV - 1))

        @block.vector
        def _(dve):
            def split_ctx(b, t, kc):
                c, w = TILES[t]
                dve.wait_ge(ctx_hi_set, b * NT + t + 1)
                end = nc.vector.tensor_tensor(ctx_lo[:, kc, c:c + w], raw[:, kc, c:c + w],
                                              ctx_hi[:, kc, c:c + w].bitcast(F32), ALU.subtract)
                if kc == KC - 1:
                    end.then_inc(ctx_lo_dve, 1)

            def key_tile(b, j, t, n):
                c, w = TILES[t]
                dve.wait_ge(kv_hi, b * KV_TILES + n + 1)
                nc.vector.scalar_tensor_tensor(
                    out=k_lo[:, c:c + w], in0=kv_ps[:, n % 2, 0:w], scalar=bk_sb[:, j % NKV:j % NKV + 1],
                    in1=k_hi[:, c:c + w].bitcast(F32), op0=ALU.add, op1=ALU.subtract).then_inc(kv_free, 1)

            def value_tile(b, j, g, n):
                m = min(2, NC - 2 * g)
                r = rows(2 * g)
                dve.wait_ge(kv_hi, b * KV_TILES + n + 1)
                nc.vector.tensor_tensor(v_lo[0:r, 2 * g:2 * g + m, :],
                                        kv_ps[0:r, n % 2, 0:m * 2 * D].rearrange("p (c d) -> p c d", c=m),
                                        v_hi[0:r, 2 * g:2 * g + m, :].bitcast(F32),
                                        ALU.subtract).then_inc(kv_free, 1)

            def score_tile(b, j, i):
                u, t = divmod(i, NT)
                c, w = TILES[t]
                w = min(w, S - c)
                n = j * NU * NT + i
                dve.wait_ge(s_full, b * S_TILES + n + 1 + S_TILES)
                nc.vector.tensor_scalar(prob[:, j % 2, u, c:c + w], s_ps[:, n % 2, 0:w], SCALE, None,
                                        ALU.mult, ALU.max,
                                        accum_out=tmax[:, u, t:t + 1]).then_inc(s_free, 1)
                if t == NT - 1:
                    dve.wait_ge(s_free, b * S_TILES + (j * NU + u + 1) * NT + 2)
                    nc.vector.tensor_reduce(nmax[:, u:u + 1], tmax[:, u, :], AX_X, ALU.max,
                                            negate=True).then_inc(nmax_set, 1)

            def normalise(b, j, u):
                n = b * (NKV * NU) + j * NU + u + 1
                dve.wait_ge(exp_done, n)
                nc.vector.reciprocal(rden[:, u:u + 1], den[:, u:u + 1]).then_inc(rden_set, 1)
                dve.wait_ge(rden_set, n)
                nc.vector.tensor_scalar(prob[:, j % 2, u, 0:S], prob[:, j % 2, u, 0:S], rden[:, u:u + 1], None,
                                        ALU.mult).then_inc(prob_set, 1)

            def low_transposed(b, j, g):
                n = j * NG + g
                m = min(2, NC - 2 * g)
                r = rows(2 * g)
                dve.wait_ge(t_hi, b * PAIRS + n + 1)
                nc.vector.tensor_tensor(pt_lo[0:r, n % NPT, 0:m, :],
                                        t_ps[0:r, n % 2, 0:m * NQ].rearrange("p (c d) -> p c d", c=m),
                                        pt_hi[0:r, n % NPT, 0:m, :].bitcast(F32),
                                        ALU.subtract).then_inc(t_free, 1)

            def softmax_and_project(b, j, last):
                normalise(b, j, 0)
                tiles = projections(b, j, last)
                if tiles:
                    assert tiles.pop()[:3] == ("k", j + 1, NT - 1)
                for i, (kind, at, t, n) in enumerate(tiles):
                    (key_tile if kind == "k" else value_tile)(b, at, t, n)
                    if 1 <= i < NU:
                        normalise(b, j, i)
                if not tiles:
                    for u in range(1, NU):
                        normalise(b, j, u)

            def first():
                dve.sem_inc(kv_free, 2)
                dve.sem_inc(s_free, 2)
                dve.sem_inc(t_free, 2)
                dve.wait_ge(bias_in, 32)
                for t in range(NT):
                    key_tile(0, 0, t, t)
                for i in range(NU * NT):
                    score_tile(0, 0, i)
                softmax_and_project(0, 0, False)

            def group(b, j, last):
                ctx_steps = [(t, kc) for t in range(LO_DVE) for kc in range(KC)]
                for i in range(max(NU * NT, NG)):
                    if i < NU * NT:
                        score_tile(b, j, i)
                    if i == 0:
                        key_tile(b, j, NT - 1, kv_tile(j) + NT - 1)
                    if i < NG:
                        low_transposed(b, j - 1, i)
                    if j == NKV - 1 and not last and i % 2 == 1 and ctx_steps:
                        split_ctx(b + 1, *ctx_steps.pop(0))
                if j == NKV - 1 and not last:
                    for t, kc in ctx_steps:
                        split_ctx(b + 1, t, kc)
                softmax_and_project(b, j, last)

            def tail(b):
                for g in range(NG):
                    low_transposed(b, NKV - 1, g)

            drive(dve, first, group, tail)


class Chain:

    def __init__(self, eng, sem, start=0):
        self.eng, self.sem, self.count = eng, sem, start

    def __call__(self, ins):
        self.count += 1
        ins.then_inc(self.sem, 1)
        self.eng.wait_ge(self.sem, self.count)


def layernorm_transposed(nc, name, x_sb, xt_hi, xt_lo, ident, load=None, prepare=None, eps=1e-5):
    _, RT, H = x_sb.shape
    KC = H // P
    with Scope(nc, name) as sc:
        xn = sc.sb("xn", [P, RT, H])
        stats = sc.sb("stats", [P, RT, 6])
        mv = sc.sb("mv", [P, RT, 2])
        std = sc.sb("std", [P, RT])
        rstd = sc.sb("rstd", [P, RT])
        eps_sb = sc.sb("eps", [P, 1])
        t_ps = sc.ps("t_ps", [P, RT, 512])
        first = sc.sb("first", [P, 1])
        own, eps_set, var_set, std_set, rstd_set, xn_set, t_full, hi_set = (
            sc.sem(n) for n in ("own", "eps_set", "var_set", "std_set", "rstd_set", "xn_set", "t_full", "hi_set"))
        block = sc.block()

        @block.sync
        def _(sp):
            if load:
                load(sp)

        @block.gpsimd
        def _(pool):
            if prepare:
                prepare(pool)

        @block.vector
        def _(dve):
            step = Chain(dve, own)
            nc.vector.memset(eps_sb[:, :], eps).then_inc(eps_set, 1)

            def inverse(r):
                dve.wait_ge(std_set, r + 1)
                nc.vector.reciprocal(rstd[:, r:r + 1], std[:, r:r + 1]).then_inc(rstd_set, 1)
                dve.wait_ge(rstd_set, r + 1)
                nc.vector.tensor_scalar(xn[:, r, :], x_sb[:, r, :], mv[:, r, 0:1], rstd[:, r:r + 1],
                                        ALU.subtract, ALU.mult).then_inc(xn_set, 1)

            for r in range(RT):
                step(nc.vector.bn_stats(stats[:, r, :], x_sb[:, r, :]))
                nc.vector.bn_aggr(mv[:, r, :], stats[:, r, :]).then_inc(var_set, 1)
                if r > 0:
                    inverse(r - 1)
            inverse(RT - 1)
            for r in range(RT):
                dve.wait_ge(hi_set, r + 1)
                out = xt_lo[:, :, r * P:(r + 1) * P]
                nc.vector.tensor_tensor(out, t_ps[:, r, :].rearrange("p (k c) -> p k c", k=KC),
                                        xt_hi[:, :, r * P:(r + 1) * P].bitcast(F32), ALU.subtract)

        @block.scalar
        def _(act):
            act.wait_ge(eps_set, 1)
            nc.scalar.activation(first[:, :], eps_sb[:, :], ACT.Sqrt)
            for r in range(RT):
                act.wait_ge(var_set, r + 1)
                nc.scalar.activation(std[:, r:r + 1], mv[:, r, 1:2], ACT.Sqrt, bias=eps_sb[:, 0:1]).then_inc(std_set, 1)
            for r in range(RT):
                act.wait_ge(t_full, r + 1)
                nc.scalar.activation(xt_hi[:, :, r * P:(r + 1) * P],
                                     t_ps[:, r, :].rearrange("p (k c) -> p k c", k=KC),
                                     ACT.Copy).then_inc(hi_set, 1)

        @block.tensor
        def _(pe):
            for r in range(RT):
                pe.wait_ge(xn_set, r + 1)
                for k in range(KC):
                    end = nc.tensor.transpose(t_ps[:, r, k * P:(k + 1) * P], xn[:, r, k * P:(k + 1) * P], ident[:, :])
                end.then_inc(t_full, 1)


def split_on_pool(nc, pool, hi, lo, src, hi_set, count):
    nc.gpsimd.tensor_scalar(hi, src, 1.0, 1.0, ALU.mult, ALU.mult).then_inc(hi_set, 1)
    pool.wait_ge(hi_set, count)
    return nc.gpsimd.tensor_tensor(lo, src, hi.bitcast(F32), ALU.subtract)


def queries(nc, x_sb, ident, xt_hi, xt_lo, wq, bq, q_dram, context):
    NKV, _, KC, GD = wq.shape
    D = P
    G = GD // D
    B = q_dram.shape[0]
    R = xt_hi.shape[2]
    with Scope(nc, "q") as sc:
        raw = sc.sb("raw", [P, 2, KC, GD])
        w_hi, w_lo = sc.sb("w_hi", [P, 2, KC, GD], F32R), sc.sb("w_lo", [P, 2, KC, GD], F32R)
        bq_sb = sc.sb("bq_sb", [P, NKV * G])
        q_sb = sc.sb("q_sb", [P, 2, B, G, R // B])
        bias_in = sc.sem("bias_in")
        w_in = [sc.sem(f"w_in{i}") for i in range(2)]
        w_hi_set, w_lo_set = sc.sem("w_hi_set"), sc.sem("w_lo_set")
        q_full, q_set = sc.sem("q_full"), sc.sem("q_set")
        q_out = [sc.sem(f"q_out{i}") for i in range(2)]

        def load(sp):
            for i in range(2):
                sp.dma_start(raw[:, i], wq[i]).then_inc(w_in[i], 16)
            sp.dma_start(bq_sb[:, :], bq).then_inc(bias_in, 16)

        def prepare(pool):
            pool.wait_ge(w_in[0], 16)
            split_on_pool(nc, pool, w_hi[:, 0], w_lo[:, 0], raw[:, 0], w_hi_set, 1).then_inc(w_lo_set, 1)

        layernorm_transposed(nc, "q_ln", x_sb, xt_hi, xt_lo, ident, load, prepare)
        q_ps = sc.ps("q_ps", [P, 4, 512])
        block = sc.block()

        @block.gpsimd
        def _(pool):
            context.split_first(pool)

        @block.sync
        def _(sp):
            context.load(sp, 0)
            with sp.Fori(0, NKV // 2 - 1) as h:
                for i in range(2):
                    sp.wait_ge(w_lo_set, 2 * h + i + 1)
                    sp.dma_start(raw[:, i], wq[2 * h + 2 + i]).then_inc(w_in[i], 16)

        def evacuate(act, j0, i):
            act.wait_ge(q_out[i], (j0 + 2) * 8)
            for g in range(G):
                n = (j0 + i) * G + g
                act.wait_ge(q_full, n + 1 + 2 * G)
                nc.scalar.activation(q_sb[:, i, :, g, :], q_ps[:, g, :].rearrange("p (b l) -> p b l", b=B),
                                     ACT.Identity, bias=bq_sb[:, bass.ds(n, 1)]).then_inc(q_set, 1)
            act.wait_ge(q_set, (j0 + i + 1) * G + G)
            act.dma_start(q_dram[:, j0 + i].rearrange("b d n -> d b n"),
                          q_sb[:, i].rearrange("p b g l -> p b (g l)")).then_inc(q_out[i], 16)

        @block.scalar
        def _(act):
            act.sem_inc(q_out[0], 16)
            act.sem_inc(q_out[1], 16)
            act.wait_ge(bias_in, 16)
            def weights(j0, i):
                act.wait_ge(w_in[i], (j0 + 2) * 8)
                act.wait_ge(q_full, (j0 + i + 1) * G)
                nc.scalar.activation(w_hi[:, i], raw[:, i], ACT.Copy).then_inc(w_hi_set, 1)

            weights(0, 1)
            with act.Fori(0, NKV // 2 - 1) as h:
                for i in range(2):
                    evacuate(act, 2 * h, i)
                    weights(2 * h + 2, i)
            for i in range(2):
                evacuate(act, NKV - 2, i)
            for i in range(2):
                act.wait_ge(q_out[i], (NKV // 2 + 1) * 16)

        @block.vector
        def _(dve):
            def low(n, i):
                dve.wait_ge(w_hi_set, n + 1)
                nc.vector.tensor_tensor(w_lo[:, i], raw[:, i], w_hi[:, i].bitcast(F32),
                                        ALU.subtract).then_inc(w_lo_set, 1)

            low(1, 1)
            with dve.Fori(1, NKV // 2) as h:
                for i in range(2):
                    low(2 * h + i, i)

        @block.tensor
        def _(pe):
            pe.sem_inc(q_full, 2 * G)
            pe.sem_inc(q_set, G)
            with pe.Fori(0, NKV // 2) as h:
                j0 = 2 * h
                for i in range(2):
                    pe.wait_ge(w_lo_set, j0 + i + 1)
                    for g in range(G):
                        pe.wait_ge(q_set, (j0 + i) * G + g + 1)
                        for k in range(KC):
                            end = product(nc, q_ps[:, g, :],
                                          (w_hi[:, i, k, g * D:(g + 1) * D], w_lo[:, i, k, g * D:(g + 1) * D]),
                                          (xt_hi[:, k, :], xt_lo[:, k, :]), k == 0, k == KC - 1)
                        end.then_inc(q_full, 1)


def attention_output(nc, x_sb, o_dram, wo, bo):
    B, NKV, D, GL = o_dram.shape
    G, H = wo.shape[2:]
    L = GL // G
    RT = B * L // P
    with Scope(nc, "wo") as sc:
        o_raw, w_raw = sc.sb("o_raw", [P, 2, B, GL]), sc.sb("w_raw", [P, 2, G, H])
        o_hi, o_lo = sc.sb("o_hi", [P, 2, G, B * L], F32R), sc.sb("o_lo", [P, 2, G, B * L], F32R)
        w_hi, w_lo = sc.sb("w_hi", [P, 2, G, H], F32R), sc.sb("w_lo", [P, 2, G, H], F32R)
        bo_sb = sc.sb("bo_sb", [P, H])
        ps = sc.ps("ps", [P, RT, 512])
        bias_in = sc.sem("bias_in")
        a_in = [sc.sem(f"a_in{i}") for i in range(2)]
        hi_set, lo_set, used, done, x_set = (sc.sem(n) for n in ("hi_set", "lo_set", "used", "done", "x_set"))
        block = sc.block()

        def spread(i):
            return o_raw[:, i].rearrange("p b (g l) -> p g b l", g=G)

        def heads(t, i):
            return t[:, i].rearrange("p g (b l) -> p g b l", b=B)

        @block.sync
        def _(sp):
            sp.dma_start(bo_sb[:, :], bo.rearrange("(a n) -> a n", a=1).broadcast_to([P, H])).then_inc(bias_in, 16)
            with sp.Fori(0, NKV // 2) as h:
                j0 = 2 * h
                for i in range(2):
                    sp.wait_ge(lo_set, (j0 + i + 1) * G)
                    sp.dma_start(o_raw[:, i], o_dram[:, j0 + i].rearrange("b d n -> d b n")).then_inc(a_in[i], 16)
                    sp.dma_start(w_raw[:, i], wo[j0 + i]).then_inc(a_in[i], 16)

        @block.scalar
        def _(act):
            with act.Fori(0, NKV // 2) as h:
                j0 = 2 * h
                for i in range(2):
                    act.wait_ge(a_in[i], (j0 + 2) * 16)
                    act.wait_ge(used, j0 + i + 1)
                    for g in range(G):
                        nc.scalar.activation(heads(o_hi, i)[:, g], spread(i)[:, g], ACT.Copy)
                        nc.scalar.activation(w_hi[:, i, g], w_raw[:, i, g], ACT.Copy).then_inc(hi_set, 1)

        @block.vector
        def _(dve):
            dve.sem_inc(lo_set, 2 * G)
            with dve.Fori(0, NKV // 2) as h:
                j0 = 2 * h
                for i in range(2):
                    for g in range(G):
                        dve.wait_ge(hi_set, (j0 + i) * G + g + 1)
                        nc.vector.tensor_tensor(heads(o_lo, i)[:, g], spread(i)[:, g],
                                                heads(o_hi, i)[:, g].bitcast(F32), ALU.subtract)
                        nc.vector.tensor_tensor(w_lo[:, i, g], w_raw[:, i, g], w_hi[:, i, g].bitcast(F32),
                                                ALU.subtract).then_inc(lo_set, 1)
            dve.wait_ge(bias_in, 16)
            for r in range(RT):
                nc.vector.tensor_tensor(x_sb[:, r, :], x_sb[:, r, :], bo_sb[:, :], ALU.add).then_inc(x_set, 1)
            for r in range(RT):
                dve.wait_ge(done, r + 1)
                dve.wait_ge(x_set, r + 1)
                nc.vector.tensor_tensor(x_sb[:, r, :], ps[:, r, :], x_sb[:, r, :], ALU.add)

        @block.tensor
        def _(pe):
            pe.sem_inc(used, 2)

            def pair(j0, first, last):
                for i in range(2):
                    for g in range(G):
                        pe.wait_ge(lo_set, (j0 + i + 2) * G + g + 1)
                        for r in range(RT):
                            rs = slice(r * P, (r + 1) * P)
                            end_of_all = last and i == 1 and g == G - 1
                            end = product(nc, ps[:, r, :], (o_hi[:, i, g, rs], o_lo[:, i, g, rs]),
                                          (w_hi[:, i, g, :], w_lo[:, i, g, :]),
                                          first and i == 0 and g == 0, end_of_all)
                            if end_of_all:
                                end.then_inc(done, 1)
                            elif g == G - 1 and r == RT - 1:
                                end.then_inc(used, 1)

            pair(0, True, False)
            with pe.Fori(1, NKV // 2 - 1) as h:
                pair(2 * h, False, False)
            pair(NKV - 2, False, True)


def mamba_project(nc, x_sb, ident, xt_hi, xt_lo, w_in, conv_w, conv_b, w_x, u_sb, gate_sb, ssm_sb, B):
    DC, _, _, KC, _ = w_in.shape
    K = conv_w.shape[2]
    N = w_x.shape[2]
    R = xt_hi.shape[2]
    RT = R // P
    L = R // B
    with Scope(nc, "mp") as sc:
        raw = sc.sb("raw", [P, 2, 2, KC, P])
        w_hi, w_lo = sc.sb("w_hi", [P, 2, 2, KC, P], F32R), sc.sb("w_lo", [P, 2, 2, KC, P], F32R)
        cw, cb = sc.sb("cw", [P, DC, K]), sc.sb("cb", [P, DC])
        wx_raw = sc.sb("wx_raw", [P, DC, N])
        wx_hi, wx_lo = sc.sb("wx_hi", [P, DC, N], F32R), sc.sb("wx_lo", [P, DC, N], F32R)
        xpad = sc.sb("xpad", [P, 2, B, L + K - 1])
        xc = sc.sb("xc", [P, 2, B, L])
        u_hi, u_lo = sc.sb("u_hi", [P, 2, R], F32R), sc.sb("u_lo", [P, 2, R], F32R)
        small_in = sc.sem("small_in")
        w_in_s = [sc.sem(f"w_in{i}") for i in range(2)]
        pad_set, wx_hi_set, wx_set, w_hi_set, w_lo_set = (
            sc.sem(n) for n in ("pad_set", "wx_hi_set", "wx_set", "w_hi_set", "w_lo_set"))
        xg_full, x_read, gate_read, conv, xc_set, u_set, u_hi_set, u_lo_set, ssm_full = (
            sc.sem(n) for n in ("xg_full", "x_read", "gate_read", "conv", "xc_set", "u_set", "u_hi_set", "u_lo_set",
                                "ssm_full"))

        def load(sp):
            for c in range(2):
                sp.dma_start(raw[:, c], w_in[c]).then_inc(w_in_s[c], 16)
            sp.dma_start(cw[:, :, :], conv_w).then_inc(small_in, 16)
            sp.dma_start(cb[:, :], conv_b).then_inc(small_in, 16)
            sp.dma_start(wx_raw[:, :, :], w_x).then_inc(small_in, 16)

        def prepare(pool):
            nc.gpsimd.memset(xpad[:, :, :, 0:K - 1], 0.0).then_inc(pad_set, 1)
            pool.wait_ge(w_in_s[0], 16)
            split_on_pool(nc, pool, w_hi[:, 0], w_lo[:, 0], raw[:, 0], w_hi_set, 1).then_inc(w_lo_set, 1)
            pool.wait_ge(small_in, 48)
            split_on_pool(nc, pool, wx_hi[:, :, :], wx_lo[:, :, :], wx_raw[:, :, :], wx_hi_set, 1).then_inc(wx_set, 1)

        layernorm_transposed(nc, "ln1", x_sb, xt_hi, xt_lo, ident, load, prepare)
        xg_ps = sc.ps("xg_ps", [P, 4, 512])
        ssm_ps = sc.ps("ssm_ps", [P, RT, 512])
        block = sc.block()

        @block.sync
        def _(sp):
            for c in range(2, DC):
                sp.wait_ge(w_lo_set, c - 1)
                sp.dma_start(raw[:, c % 2], w_in[c]).then_inc(w_in_s[c % 2], 16)

        @block.tensor
        def _(pe):
            def ssm(c):
                pe.wait_ge(u_lo_set, c + 1)
                if c == 0:
                    pe.wait_ge(wx_set, 1)
                for r in range(RT):
                    rs = slice(r * P, (r + 1) * P)
                    end = product(nc, ssm_ps[:, r, 0:N], (u_hi[:, c % 2, rs], u_lo[:, c % 2, rs]),
                                  (wx_hi[:, c, :], wx_lo[:, c, :]), c == 0, c == DC - 1)
                end.then_inc(ssm_full, 1)

            for c in range(DC):
                pe.wait_ge(w_lo_set, c + 1)
                for part in range(2):
                    if c >= 2:
                        pe.wait_ge((x_read, gate_read)[part], c - 1)
                    for k in range(KC):
                        end = product(nc, xg_ps[:, 2 * (c % 2) + part, :],
                                      (w_hi[:, c % 2, part, k], w_lo[:, c % 2, part, k]),
                                      (xt_hi[:, k, :], xt_lo[:, k, :]), k == 0, k == KC - 1)
                    end.then_inc(xg_full, 1)
                if c > 1:
                    ssm(c - 2)
            ssm(DC - 2)
            ssm(DC - 1)

        @block.scalar
        def _(act):
            def weights(c):
                act.wait_ge(w_in_s[c % 2], (c // 2 + 1) * 16)
                if c >= 2:
                    act.wait_ge(xg_full, 2 * (c - 1))
                nc.scalar.activation(w_hi[:, c % 2], raw[:, c % 2], ACT.Copy).then_inc(w_hi_set, 1)

            def silu(c):
                act.wait_ge(xc_set, c + 1)
                nc.scalar.activation(u_sb[:, c, :], xc[:, c % 2].rearrange("p b l -> p (b l)"),
                                     ACT.Silu).then_inc(u_set, 1)
                if c >= 2:
                    act.wait_ge(ssm_full, c - 1)
                act.wait_ge(u_set, c + 1)
                nc.scalar.activation(u_hi[:, c % 2], u_sb[:, c, :], ACT.Copy).then_inc(u_hi_set, 1)

            act.wait_ge(pad_set, 1)
            for c in range(DC):
                if c + 1 < DC:
                    weights(c + 1)
                act.wait_ge(xg_full, 2 * c + 1)
                if c >= 2:
                    act.wait_ge(xc_set, c - 1)
                nc.scalar.activation(xpad[:, c % 2, :, K - 1:], xg_ps[:, 2 * (c % 2), :].rearrange("p (b l) -> p b l", b=B),
                                     ACT.Copy).then_inc(x_read, 1)
                act.wait_ge(xg_full, 2 * c + 2)
                nc.scalar.activation(gate_sb[:, c, :], xg_ps[:, 2 * (c % 2) + 1, :], ACT.Silu).then_inc(gate_read, 1)
                if c > 0:
                    silu(c - 1)
            silu(DC - 1)

        @block.vector
        def _(dve):
            step = Chain(dve, conv)

            def u_low(c):
                dve.wait_ge(u_hi_set, c + 1)
                nc.vector.tensor_tensor(u_lo[:, c % 2], u_sb[:, c, :], u_hi[:, c % 2].bitcast(F32),
                                        ALU.subtract).then_inc(u_lo_set, 1)

            dve.wait_ge(small_in, 48)
            for c in range(DC + 1):
                if 0 < c < DC:
                    dve.wait_ge(w_hi_set, c + 1)
                    nc.vector.tensor_tensor(w_lo[:, c % 2], raw[:, c % 2], w_hi[:, c % 2].bitcast(F32),
                                            ALU.subtract).then_inc(w_lo_set, 1)
                if c > 1:
                    u_low(c - 2)
                if c > 0:
                    a = c - 1
                    s = a % 2
                    dve.wait_ge(x_read, a + 1)
                    if a >= 2:
                        dve.wait_ge(u_set, a - 1)
                    step(nc.vector.tensor_scalar(xc[:, s], xpad[:, s, :, 0:L], cw[:, a, 0:1], cb[:, a:a + 1],
                                                 ALU.mult, ALU.add))
                    for j in range(1, K):
                        ins = nc.vector.scalar_tensor_tensor(out=xc[:, s], in0=xpad[:, s, :, j:j + L],
                                                             scalar=cw[:, a, j:j + 1], in1=xc[:, s],
                                                             op0=ALU.mult, op1=ALU.add)
                        if j < K - 1:
                            step(ins)
                        else:
                            ins.then_inc(xc_set, 1)
            u_low(DC - 1)
            dve.wait_ge(ssm_full, DC)
            for r in range(RT):
                nc.vector.tensor_copy(ssm_sb[:, r, :], ssm_ps[:, r, 0:N])


def mamba_parameters(nc, ssm_sb, w_dt, b_dt, ident, b_all, c_all, dt_sb, work, eps=1e-6):
    _, RT, N = ssm_sb.shape
    NS, DC, R = b_all.shape[1], dt_sb.shape[1], dt_sb.shape[2]
    RANK = N - 2 * NS
    assert NS == 2 * DC
    with Scope(nc, "mr") as sc:
        sq = sc.sb("sq", [P, RT, N])
        ms = sc.sb("ms", [P, RT, 3])
        eps_sb = sc.sb("eps", [P, 1])
        nrm = sc.sb("nrm", [P, RT, N])
        n_hi, n_lo = sc.sb("n_hi", [N, R], F32R), sc.sb("n_lo", [N, R], F32R)
        sel = sc.sb("sel", [N, 2 * NS, P], F32R)
        wd_raw = sc.sb("wd_raw", [RANK, DC * P])
        wd_hi, wd_lo = sc.sb("wd_hi", [RANK, DC * P], F32R), sc.sb("wd_lo", [RANK, DC * P], F32R)
        bd = sc.sb("bd", [P, DC])
        t_ps = sc.ps("t_ps", [P, 512])
        bc_ps = sc.ps("bc_ps", [P, 4, 512])
        d_ps = sc.ps("d_ps", [P, 2, 512])
        small_in, own, ms_set, std_set, nrm_set, t_full, n_hi_set, n_lo_set, wd_hi_set, wd_set, sel_b, sel_c = (
            sc.sem(n) for n in ("small_in", "own", "ms_set", "std_set", "nrm_set", "t_full", "n_hi_set", "n_lo_set",
                                "wd_hi_set", "wd_set", "sel_b", "sel_c"))
        bc_full, bc_even, bc_odd, d_full, d_abs, d_read, e_set, ln_set = (
            sc.sem(n) for n in ("bc_full", "bc_even", "bc_odd", "d_full", "d_abs", "d_read", "e_set", "ln_set"))
        block = sc.block()
        segments = [(0, RANK), (RANK, NS), (RANK + NS, NS)]

        def picks(h):
            a = RANK + h * NS
            return sel[:, h * NS:(h + 1) * NS, :], ident[0:N, a:a + NS].unsqueeze(2).broadcast_to([N, NS, P])

        @block.sync
        def _(sp):
            sp.dma_start(wd_raw[:, :], w_dt).then_inc(small_in, 16)
            sp.dma_start(bd[:, :], b_dt).then_inc(small_in, 16)

        @block.gpsimd
        def _(pool):
            pool.wait_ge(small_in, 32)
            nc.gpsimd.tensor_scalar(wd_hi[:, :], wd_raw[:, :], 1.0, 1.0, ALU.mult, ALU.mult).then_inc(wd_hi_set, 1)
            pool.wait_ge(wd_hi_set, 1)
            nc.gpsimd.tensor_tensor(wd_lo[:, :], wd_raw[:, :], wd_hi[:, :].bitcast(F32), ALU.subtract).then_inc(wd_set, 1)
            nc.gpsimd.tensor_scalar(*picks(1), 1.0, 1.0, ALU.mult, ALU.mult).then_inc(sel_c, 1)

        @block.vector
        def _(dve):
            step = Chain(dve, own)
            step(nc.vector.memset(eps_sb[:, :], eps))
            step(nc.vector.tensor_tensor(sq[:, :, :], ssm_sb[:, :, :], ssm_sb[:, :, :], ALU.mult))
            for i, (a, n) in enumerate(segments):
                step(nc.vector.tensor_reduce(ms[:, :, i:i + 1], sq[:, :, a:a + n], AX_X, ALU.add))
                nc.vector.tensor_scalar(ms[:, :, i], ms[:, :, i], 1.0 / n, None, ALU.mult).then_inc(ms_set, 1)
            dve.wait_ge(std_set, 1)
            step(nc.vector.reciprocal(ms[:, :, :], ms[:, :, :]))
            for i, (a, n) in enumerate(segments):
                nc.vector.tensor_tensor(nrm[:, :, a:a + n], ssm_sb[:, :, a:a + n],
                                        ms[:, :, i:i + 1].broadcast_to([P, RT, n]), ALU.mult).then_inc(nrm_set, 1)
            dve.wait_ge(n_hi_set, 1)
            nc.vector.tensor_tensor(n_lo[:, :], t_ps[0:N, :], n_hi[:, :].bitcast(F32), ALU.subtract).then_inc(n_lo_set, 1)

            def softplus(c):
                dve.wait_ge(ln_set, c + 1)
                nc.vector.tensor_tensor(dt_sb[:, c, :], dt_sb[:, c, :], work[:, c, :], ALU.add)

            for i in range(1, 2 * NS, 2):
                c = i // 2
                if c < DC:
                    dve.wait_ge(d_abs, c + 1)
                    nc.vector.tensor_scalar(work[:, c, :], d_ps[:, c % 2, :], bd[:, c:c + 1], 0.0,
                                            ALU.add, ALU.max).then_inc(d_read, 1)
                dve.wait_ge(bc_full, i + 1)
                nc.vector.tensor_copy((b_all, c_all)[i // NS][:, i % NS, :], bc_ps[:, i % 4, :]).then_inc(bc_odd, 1)
                c = i // 2 - DC
                if 0 <= c - 1 < DC:
                    softplus(c - 1)
            softplus(DC - 1)

        @block.tensor
        def _(pe):
            pe.wait_ge(nrm_set, 3)
            for r in range(RT):
                end = nc.tensor.transpose(t_ps[0:N, r * P:(r + 1) * P], nrm[:, r, :], ident[:, :])
            end.then_inc(t_full, 1)
            pe.wait_ge(n_lo_set, 1)
            pe.wait_ge(wd_set, 1)
            for i in range(2 * NS):
                c = i // 2
                if i % 2 == 0 and c < DC:
                    if c >= 2:
                        pe.wait_ge(d_read, c - 1)
                    cs = slice(c * P, (c + 1) * P)
                    product(nc, d_ps[:, c % 2, :], (wd_hi[:, cs], wd_lo[:, cs]), (n_hi[0:RANK, :], n_lo[0:RANK, :]),
                            True, True).then_inc(d_full, 1)
                if i % NS == 0:
                    pe.wait_ge((sel_b, sel_c)[i // NS], 1)
                if i >= 4:
                    pe.wait_ge((bc_even, bc_odd)[i % 2], i // 2 - 1)
                nc.tensor.matmul(bc_ps[:, i % 4, :], sel[:, i, :], n_hi[:, :], start=True, stop=False)
                nc.tensor.matmul(bc_ps[:, i % 4, :], sel[:, i, :], n_lo[:, :], start=False, stop=True).then_inc(bc_full, 1)

        @block.scalar
        def _(act):
            nc.scalar.activation(*picks(0), ACT.Copy).then_inc(sel_b, 1)
            act.wait_ge(ms_set, 3)
            nc.scalar.activation(ms[:, :, :], ms[:, :, :], ACT.Sqrt, bias=eps_sb[:, 0:1]).then_inc(std_set, 1)
            act.wait_ge(t_full, 1)
            nc.scalar.activation(n_hi[:, :], t_ps[0:N, :], ACT.Copy).then_inc(n_hi_set, 1)
            act.wait_ge(small_in, 32)
            for i in range(0, 2 * NS, 2):
                c = i // 2
                if c < DC:
                    act.wait_ge(d_full, c + 1)
                    nc.scalar.activation(dt_sb[:, c, :], d_ps[:, c % 2, :], ACT.Abs, bias=bd[:, c:c + 1]).then_inc(d_abs, 1)
                act.wait_ge(bc_full, i + 1)
                nc.scalar.activation((b_all, c_all)[i // NS][:, i % NS, :], bc_ps[:, i % 4, :], ACT.Copy).then_inc(bc_even, 1)
                c = i // 2 % DC
                if i // 2 < DC:
                    act.wait_ge(d_abs, c + 1)
                    nc.scalar.activation(dt_sb[:, c, :], dt_sb[:, c, :], ACT.Exp, scale=-1.0).then_inc(e_set, 1)
                elif i // 2 < 2 * DC:
                    act.wait_ge(e_set, c + 1)
                    nc.scalar.activation(dt_sb[:, c, :], dt_sb[:, c, :], ACT.Ln, bias=1.0).then_inc(ln_set, 1)


def mamba_scan(nc, u_sb, gate_sb, b_all, c_all, dt_sb, d_a, d_bu, a_log, d_skip, w_out, wo_raw, ident):
    DC, R = dt_sb.shape[1:]
    NS = b_all.shape[1]
    HN = d_a.shape[2]
    NH = NS // HN
    DA, DB = d_a.shape[1], d_bu.shape[1]
    B, L = d_a.shape[3:]
    with Scope(nc, "ms") as sc:
        a_sb, dk = sc.sb("a_sb", [P, DC, NS]), sc.sb("dk", [P, DC])
        dtu = sc.sb("dtu", [P, 2, R])
        y_ps = sc.ps("y_ps", [P, 2, 512])
        small_in, next_in, own, a_exp, a_set, dtu_set, da_set, dbu_set, h_set, hc_set, y_full, y_set = (
            sc.sem(n) for n in ("small_in", "next_in", "own", "a_exp", "a_set", "dtu_set", "da_set", "dbu_set", "h_set", "hc_set",
                                "y_full", "y_set"))
        block = sc.block()

        def flat(t, s):
            return t[:, s].rearrange("p n b l -> p (n b l)")

        def by_state(t, s):
            return t[:, s].rearrange("p n b l -> p n (b l)")

        @block.sync
        def _(sp):
            sp.dma_start(a_sb[:, :, :], a_log).then_inc(small_in, 16)
            sp.dma_start(dk[:, :], d_skip).then_inc(small_in, 16)
            sp.dma_start(wo_raw[:, :, :], w_out).then_inc(next_in, 16)
            sp.wait_ge(next_in, 16)

        @block.scalar
        def _(act):
            act.wait_ge(small_in, 32)
            nc.scalar.activation(a_sb[:, :, :], a_sb[:, :, :], ACT.Exp).then_inc(a_exp, 1)
            act.wait_ge(a_set, 1)
            for i in range(DC * NH):
                c, h = divmod(i, NH)
                if i >= DA:
                    act.wait_ge(h_set, i - DA + 1)
                for n in range(HN):
                    end = nc.scalar.activation(d_a[:, i % DA, n, :, 1:L],
                                               dt_sb[:, c, :].rearrange("p (b l) -> p b l", b=B)[:, :, 1:L],
                                               ACT.Exp, scale=a_sb[:, c, h * HN + n:h * HN + n + 1])
                end.then_inc(da_set, 1)

        @block.gpsimd
        def _(pool):
            for i in range(DC * NH):
                c, h = divmod(i, NH)
                pool.wait_ge(dtu_set, c + 1)
                if i >= DB:
                    pool.wait_ge(y_full, i - DB + 1)
                nc.gpsimd.tensor_tensor(by_state(d_bu, i % DB), b_all[:, h * HN:(h + 1) * HN, :],
                                        dtu[:, c % 2, :].unsqueeze(1).broadcast_to([P, HN, R]),
                                        ALU.mult).then_inc(dbu_set, 1)

        @block.vector
        def _(dve):
            step = Chain(dve, own)
            nc.vector.memset(d_a[:, :, :, :, 0:1], 0.0).then_inc(own, 1)
            step.count = 1
            dve.wait_ge(a_exp, 1)
            nc.vector.tensor_scalar(a_sb[:, :, :], a_sb[:, :, :], -1.0, None, ALU.mult).then_inc(a_set, 1)

            def weigh(c):
                if c >= 2:
                    dve.wait_ge(dbu_set, NH * (c - 1))
                nc.vector.tensor_tensor(dtu[:, c % 2, :], dt_sb[:, c, :], u_sb[:, c, :], ALU.mult).then_inc(dtu_set, 1)

            def output(c):
                dve.wait_ge(y_full, NH * (c + 1))
                step(nc.vector.scalar_tensor_tensor(out=u_sb[:, c, :], in0=u_sb[:, c, :], scalar=dk[:, c:c + 1],
                                                    in1=y_ps[:, c % 2, :], op0=ALU.mult, op1=ALU.add))
                nc.vector.tensor_tensor(gate_sb[:, c, :], gate_sb[:, c, :], u_sb[:, c, :], ALU.mult).then_inc(y_set, 1)

            weigh(0)
            weigh(1)
            for i in range(DC * NH + 1):
                if i < DC * NH:
                    c, h = divmod(i, NH)
                    dve.wait_ge(da_set, i + 1)
                    dve.wait_ge(dbu_set, i + 1)
                    nc.vector.tensor_tensor_scan(flat(d_bu, i % DB), flat(d_a, i % DA), flat(d_bu, i % DB), 0.0,
                                                 ALU.mult, ALU.add).then_inc(h_set, 1)
                    if h == NH // 2 and c > 0:
                        output(c - 1)
                        if c + 1 < DC:
                            weigh(c + 1)
                if i > 0:
                    h = (i - 1) % NH
                    dve.wait_ge(h_set, i)
                    nc.vector.tensor_tensor(by_state(d_bu, (i - 1) % DB), by_state(d_bu, (i - 1) % DB),
                                            c_all[:, h * HN:(h + 1) * HN, :], ALU.mult).then_inc(hc_set, 1)
            output(DC - 1)

        @block.tensor
        def _(pe):
            for i in range(DC * NH):
                c, h = divmod(i, NH)
                pe.wait_ge(hc_set, i + 1)
                if h == 0 and c >= 2:
                    pe.wait_ge(y_set, c - 1)
                for n in range(HN):
                    end = nc.tensor.matmul(y_ps[:, c % 2, :], ident[:, :], by_state(d_bu, i % DB)[:, n, :],
                                           start=h == 0 and n == 0, stop=h == NH - 1 and n == HN - 1)
                end.then_inc(y_full, 1)


def mamba_output(nc, x_sb, y_sb, raw, following):
    DC, R = y_sb.shape[1:]
    H = raw.shape[2]
    RT = R // P
    with Scope(nc, "mo") as sc:
        w_hi, w_lo = sc.sb("w_hi", [P, DC, H], F32R), sc.sb("w_lo", [P, DC, H], F32R)
        y_hi, y_lo = sc.sb("y_hi", [P, DC, R], F32R), sc.sb("y_lo", [P, DC, R], F32R)
        ps = sc.ps("ps", [P, RT, 512])
        hi_set, lo_set, done = (sc.sem(n) for n in ("hi_set", "lo_set", "done"))
        following.place(sc)
        block = sc.block()

        @block.sync
        def _(sp):
            following.load(sp)

        @block.scalar
        def _(act):
            for c in range(DC):
                nc.scalar.activation(y_hi[:, c, :], y_sb[:, c, :], ACT.Copy).then_inc(hi_set, 1)
                nc.scalar.activation(w_hi[:, c, :], raw[:, c, :], ACT.Copy).then_inc(hi_set, 1)

        @block.vector
        def _(dve):
            for c in range(DC):
                dve.wait_ge(hi_set, 2 * c + 2)
                nc.vector.tensor_tensor(y_lo[:, c, :], y_sb[:, c, :], y_hi[:, c, :].bitcast(F32), ALU.subtract)
                nc.vector.tensor_tensor(w_lo[:, c, :], raw[:, c, :], w_hi[:, c, :].bitcast(F32),
                                        ALU.subtract).then_inc(lo_set, 1)
            following.make(dve)
            for r in range(RT):
                dve.wait_ge(done, r + 1)
                nc.vector.tensor_tensor(x_sb[:, r, :], ps[:, r, :], x_sb[:, r, :], ALU.add)

        @block.tensor
        def _(pe):
            for c in range(DC):
                pe.wait_ge(lo_set, c + 1)
                for r in range(RT):
                    rs = slice(r * P, (r + 1) * P)
                    end = product(nc, ps[:, r, :], (y_hi[:, c, rs], y_lo[:, c, rs]), (w_hi[:, c, :], w_lo[:, c, :]),
                                  c == 0, c == DC - 1)
                    if c == DC - 1:
                        end.then_inc(done, 1)


def mamba(nc, x_sb, ident, B, w_in, conv_w, conv_b, w_x, w_dt, b_dt, a_log, d_skip, w_out,
          following):
    RT = x_sb.shape[1]
    H = x_sb.shape[2]
    R = RT * P
    DC = w_in.shape[0]
    NS = a_log.shape[2]
    with Scope(nc, "mamba") as sc:
        u_sb, gate_sb = sc.sb("u", [P, DC, R]), sc.sb("gate", [P, DC, R])
        wo_raw = sc.sb("wo_raw", [P, DC, H])
        with Scope(nc, "mamba_a") as sc1:
            ssm_sb = sc1.sb("ssm", [P, RT, w_x.shape[2]])
            with Scope(nc, "mamba_x") as sc2:
                xt_hi, xt_lo = sc2.sb("xt_hi", [P, H // P, R], F32R), sc2.sb("xt_lo", [P, H // P, R], F32R)
                mamba_project(nc, x_sb, ident, xt_hi, xt_lo, w_in, conv_w, conv_b, w_x, u_sb, gate_sb, ssm_sb, B)
            b_all, c_all = sc1.sb("b_all", [P, NS, R]), sc1.sb("c_all", [P, NS, R])
            dt_sb = sc1.sb("dt", [P, DC, R])
            with Scope(nc, "mamba_w") as sc2:
                work = sc2.sb("work", [P, DC, R])
                mamba_parameters(nc, ssm_sb, w_dt, b_dt, ident, b_all, c_all, dt_sb, work)
            d_a = sc1.sb("d_a", [P, 2, NS // 4, B, R // B])
            d_bu = sc1.sb("d_bu", [P, 5, NS // 4, B, R // B])
            mamba_scan(nc, u_sb, gate_sb, b_all, c_all, dt_sb, d_a, d_bu, a_log, d_skip, w_out, wo_raw,
                       ident)
        mamba_output(nc, x_sb, gate_sb, wo_raw, following)


class TernaryWeights:

    def __init__(self, nc, scope, w, bias):
        self.nc, self.w, self.bias = nc, w, bias
        KC, H = w.shape[1:]
        self.tern_r = scope.sb("tern_r", [P, KC, H], F32R)
        self.tot, self.scale = scope.sb("tot", [P, 2]), scope.sb("scale", [P, 1])
        self.part, self.few = scope.sb("part", [P, 2]), scope.sb("few", [P, 1])
        self.w_in, self.own, self.part_set, self.tot_full = (
            scope.sem(n) for n in ("w_in", "own", "part_set", "tot_full"))

    def place(self, scope):
        self.raw, self.neg, self.tern = (scope.sb(n, list(self.w.shape)) for n in ("raw", "neg", "tern"))

    def load(self, sp):
        sp.dma_start(self.raw[:, :, :], self.w).then_inc(self.w_in, 16)

    def make(self, dve):
        nc, raw, neg, tern, part = self.nc, self.raw, self.neg, self.tern, self.part
        step = Chain(dve, self.own)
        dve.wait_ge(self.w_in, 16)
        step(nc.vector.tensor_scalar(neg[:, :, :], raw[:, :, :], -0.5, None, ALU.is_lt))
        step(nc.vector.scalar_tensor_tensor(out=tern[:, :, :], in0=raw[:, :, :], scalar=0.5, in1=neg[:, :, :],
                                            op0=ALU.is_gt, op1=ALU.subtract))
        nc.vector.tensor_copy(self.tern_r[:, :, :], tern[:, :, :])
        step(nc.vector.tensor_tensor(neg[:, :, :], tern[:, :, :], tern[:, :, :], ALU.mult))
        step(nc.vector.tensor_reduce(part[:, 0:1], neg[:, :, :].rearrange("p k n -> p (k n)"), AX_X, ALU.add))
        step(nc.vector.tensor_tensor(neg[:, :, :], tern[:, :, :], raw[:, :, :], ALU.mult))
        nc.vector.tensor_reduce(part[:, 1:2], neg[:, :, :].rearrange("p k n -> p (k n)"), AX_X,
                                ALU.add).then_inc(self.part_set, 1)

    def totals(self, pe, bank, ones):
        pe.wait_ge(self.part_set, 1)
        self.nc.tensor.matmul(bank[:, 0:2], ones[:, :], self.part[:, :], start=True, stop=True).then_inc(self.tot_full, 1)

    def finish(self, dve, bank, step):
        nc, tot, few, scale = self.nc, self.tot, self.few, self.scale
        dve.wait_ge(self.tot_full, 1)
        step(nc.vector.tensor_copy(tot[:, :], bank[:, 0:2]))
        step(nc.vector.tensor_scalar(few[:, :], tot[:, 0:1], 0.0, None, ALU.is_equal))
        step(nc.vector.tensor_scalar(tot[:, 0:1], tot[:, 0:1], 1.0, None, ALU.max))
        step(nc.vector.reciprocal(scale[:, :], tot[:, 0:1]))
        step(nc.vector.scalar_tensor_tensor(out=scale[:, :], in0=scale[:, :], scalar=tot[:, 1:2], in1=few[:, :],
                                            op0=ALU.mult, op1=ALU.add))


def ternary_linear(nc, x_sb, xt_hi, xt_lo, weights, ones):
    KC, H = weights.w.shape[1:]
    R = xt_hi.shape[2]
    RT = R // P
    with Scope(nc, "tl") as sc:
        tot_ps = sc.ps("tot_ps", [P, 512])
        ps = sc.ps("ps", [P, RT, 512])
        bias_sb = sc.sb("bias", [P, H])
        bias_in, own, done = (sc.sem(n) for n in ("bias_in", "own", "done"))
        block = sc.block()

        @block.sync
        def _(sp):
            bias = weights.bias.rearrange("(a n) -> a n", a=1).broadcast_to([P, H])
            sp.dma_start(bias_sb[:, :], bias).then_inc(bias_in, 16)

        @block.vector
        def _(dve):
            step = Chain(dve, own)
            weights.finish(dve, tot_ps, step)
            dve.wait_ge(bias_in, 16)
            for r in range(RT):
                step(nc.vector.tensor_tensor(x_sb[:, r, :], x_sb[:, r, :], bias_sb[:, :], ALU.add))
            for r in range(RT):
                dve.wait_ge(done, r + 1)
                nc.vector.scalar_tensor_tensor(out=x_sb[:, r, :], in0=ps[:, r, :], scalar=weights.scale[:, 0:1],
                                               in1=x_sb[:, r, :], op0=ALU.mult, op1=ALU.add)

        @block.tensor
        def _(pe):
            weights.totals(pe, tot_ps, ones)
            for r in range(RT):
                rs = slice(r * P, (r + 1) * P)
                for k in range(KC):
                    nc.tensor.matmul(ps[:, r, :], xt_hi[:, k, rs], weights.tern_r[:, k, :], start=k == 0, stop=False)
                    end = nc.tensor.matmul(ps[:, r, :], xt_lo[:, k, rs], weights.tern_r[:, k, :], start=False,
                                           stop=k == KC - 1)
                end.then_inc(done, 1)


def context_attention(nc, x_sb, xt_hi, xt_lo, ctx, ident, c_dram):
    B, S, H = ctx.shape
    KC = xt_hi.shape[1]
    R = xt_hi.shape[2]
    L = R // B
    SE = S + S % 2
    NC = -(-S // P)
    TILES = even_tiles(SE)
    NT = len(TILES)
    NB = -(-NC // 8)
    GROUPS = [(c, min(c + 2, NC)) for c in range(0, NC, 2)]
    if S % P and GROUPS[-1][1] - GROUPS[-1][0] > 1:
        GROUPS[-1:] = [(NC - 2, NC - 1), (NC - 1, NC)]
    NG = len(GROUPS)
    LO_DVE = 3
    EARLY = -(-(TILES[1][0] + TILES[1][1]) // P)

    def rows(c):
        return min(P, S - c * P)

    def group_of(c):
        return [g for g, (a, z) in enumerate(GROUPS) if a <= c < z][0]

    PARTS = [slice(0, 2), slice(2, 3), slice(3, KC)]
    SCORES, late = [], list(range(EARLY, NC))
    for t in range(NT):
        for part in range(len(PARTS)):
            SCORES.append(("s", t, part))
            if late:
                SCORES.append(("t", late.pop(0), None))

    NS = 3

    def slot(c):
        return 1 if c == NC - 1 and c % NS == 0 else c % NS

    def ago(c):
        return min(d for d in range(1, NS + 1) if d == NS or slot((c - d) % NC) == slot(c))

    def drive(eng, step):
        step(0, -1, True, True)
        with eng.Fori(0, (B - 2) // 2) as h:
            step(h, 0, True, True)
            step(h, 1, True, True)
        step((B - 2) // 2, 0, True, False)
        step((B - 2) // 2, 1, False, False)

    with Scope(nc, "ca") as sc:
        nat = sc.sb("nat", [P, 2, NC, H])
        n_hi, n_lo = sc.sb("n_hi", [P, NC, H], F32R), sc.sb("n_lo", [P, NC, H], F32R)
        t_hi, t_lo = sc.sb("t_hi", [P, KC, SE], F32R), sc.sb("t_lo", [P, KC, SE], F32R)
        q_hi, q_lo = sc.sb("q_hi", [P, 2, KC, L], F32R), sc.sb("q_lo", [P, 2, KC, L], F32R)
        prob = sc.sb("prob", [L, SE])
        tmax, nmax = sc.sb("tmax", [L, NT]), sc.sb("nmax", [L, 1])
        den, rden = sc.sb("den", [L, 1]), sc.sb("rden", [L, 1])
        pt = sc.sb("pt", [P, NC, 2, L], F32R)
        c_sb = sc.sb("c_sb", [2 * L, H])
        t_ps = sc.ps("t_ps", [P, NS, 512])
        s_ps = sc.ps("s_ps", [L, 2, 512])
        pt_ps = sc.ps("pt_ps", [P, NB, 512])
        c_ps = sc.ps("c_ps", [2 * L, 512])
        nat_in = [[sc.sem(f"nat_in{i}_{g}") for g in range(NG)] for i in range(2)]
        passed, passed_pe, passed_sp = sc.sem("passed"), sc.sem("passed_pe"), sc.sem("passed_sp")
        c_out = sc.sem("c_out")
        q_set, n_hi_set, lo_dve, lo_pool, t_full, t_hi_set, t_free = (
            sc.sem(n) for n in ("q_set", "n_hi_set", "lo_dve", "lo_pool", "t_full", "t_hi_set", "t_free"))
        s_full, s_free, nmax_set, exp_set, pt_full, pt_hi_set, pt_free = (
            sc.sem(n) for n in ("s_full", "s_free", "nmax_set", "exp_set", "pt_full", "pt_hi_set", "pt_free"))
        pv_done, rden_set, prob_set, c_set, pad_set, own = (
            sc.sem(n) for n in ("pv_done", "rden_set", "prob_set", "c_set", "pad_set", "own"))
        x_in = [sc.sem(f"x_in{r}") for r in range(R // P)]
        block = sc.block()

        def loaded(eng, h, i, g):
            eng.wait_ge(nat_in[i % 2][g], (h + i // 2 + 1) * 16)

        def split_done(eng, h, i, g):
            if g < LO_DVE:
                eng.wait_ge(lo_dve, (2 * h + i) * LO_DVE + g + 1)
            else:
                eng.wait_ge(lo_pool, (2 * h + i) * (NG - LO_DVE) + g - LO_DVE + 1)

        @block.sync
        def _(sp):
            def load(h, i, g):
                a, z = GROUPS[g]
                r = rows(a)
                sp.dma_start(nat[0:r, i % 2, a:z, :],
                             ctx[2 * h + i, a * P:a * P + (z - a) * r].rearrange("(c p) h -> p c h", p=r)
                             ).then_inc(nat_in[i % 2][g], 16)

            for i in range(2):
                for g in range(NG):
                    load(0, i, g)
            with sp.Fori(0, (B - 2) // 2) as h:
                for i in range(2):
                    for g, (a, z) in enumerate(GROUPS):
                        sp.wait_ge(t_full, (2 * h + i) * NC + z)
                        apart(sp, passed_sp)
                        split_done(sp, h, i, g)
                        load(h, i + 2, g)

        @block.gpsimd
        def _(pool):
            def step(h, i, has1, has2):
                i += 1
                if not has1:
                    return
                for g, (a, z) in enumerate(GROUPS):
                    r = rows(a)
                    loaded(pool, h, i, g)
                    pool.wait_ge(pv_done, (2 * h + i) * NG + g + 1)
                    apart(pool, passed)
                    nc.gpsimd.tensor_scalar(n_hi[0:r, a:z, :], nat[0:r, i % 2, a:z, :], 1.0, 1.0,
                                            ALU.mult, ALU.mult).then_inc(n_hi_set, 1)
                for g, (a, z) in enumerate(GROUPS):
                    if g >= LO_DVE:
                        r = rows(a)
                        pool.wait_ge(n_hi_set, (2 * h + i) * NG + g + 1)
                        nc.gpsimd.tensor_tensor(n_lo[0:r, a:z, :], nat[0:r, i % 2, a:z, :],
                                                n_hi[0:r, a:z, :].bitcast(F32), ALU.subtract).then_inc(lo_pool, 1)

            drive(pool, step)

        @block.tensor
        def _(pe):
            pe.sem_inc(pv_done, NG)

            def transpose(h, i, c):
                r = rows(c)
                n = (2 * h + i) * NC + c
                loaded(pe, h, i, group_of(c))
                pe.wait_ge(t_free, n + 1 + NS - ago(c))
                for k in range(KC):
                    end = nc.tensor.transpose(t_ps[:, slot(c), k * P:k * P + r],
                                              nat[0:r, i % 2, c, k * P:(k + 1) * P], ident[0:r, 0:r])
                end.then_inc(t_full, 1)

            def score_part(h, i, t, part):
                n = 2 * h + i
                c, w = TILES[t]
                if part == 0:
                    if t == 0:
                        pe.wait_ge(q_set, n * 2 + 2)
                    pe.wait_ge(t_free, n * NC + min(NC, -(-(c + w) // P)) + NS)
                    pe.wait_ge(s_free, n * NT + t + 1)
                for k in range(KC)[PARTS[part]]:
                    end = product(nc, s_ps[:, t % 2, 0:w], (q_hi[:, i % 2, k, :], q_lo[:, i % 2, k, :]),
                                  (t_hi[:, k, c:c + w], t_lo[:, k, c:c + w]), k == 0, k == KC - 1)
                if part == len(PARTS) - 1:
                    end.then_inc(s_full, 1)

            def pv(h, i, c):
                n = 2 * h + i
                r = rows(c)
                g = group_of(c)
                if c == 0:
                    pe.wait_ge(c_set, n + 1)
                if c % 8 == 0:
                    pe.wait_ge(pt_free, n * NB + c // 8 + 1 + NB)
                if c == GROUPS[g][0]:
                    split_done(pe, h, i, g)
                def both():
                    return nc.tensor.matmul(c_ps[:, :], pt[0:r, c].rearrange("p i l -> p (i l)"), n_hi[0:r, c, :],
                                            start=c == 0, stop=c == NC - 1)

                if c == 0:
                    both()
                end = nc.tensor.matmul(c_ps[0:L, :], pt[0:r, c, 0, :], n_lo[0:r, c, :], start=False, stop=False)
                if c > 0:
                    end = both()
                if c == GROUPS[g][1] - 1:
                    end.then_inc(pv_done, 1)

            def step(h, i, has1, has2):
                if i == -1:
                    for c in range(EARLY):
                        transpose(h, 0, c)
                if has1:
                    for kind, at, part in SCORES:
                        if kind == "s":
                            score_part(h, i + 1, at, part)
                        else:
                            transpose(h, i + 1, at)
                early = list(range(EARLY)) if has2 else []
                for c in range(NC):
                    if i >= 0:
                        pv(h, i, c)
                    if early and c % 2 == 1:
                        transpose(h, i + 2, early.pop(0))
                for c in early:
                    transpose(h, i + 2, c)
                if has1:
                    n = 2 * h + i + 1
                    pe.wait_ge(prob_set, n + 1)
                    for c in range(NC):
                        if c % 8 == 0:
                            pe.wait_ge(pt_free, n * NB + c // 8 + 1)
                            apart(pe, passed_pe)
                        r = rows(c)
                        end = nc.tensor.transpose(pt_ps[0:r, c // 8, (c % 8) * L:(c % 8 + 1) * L],
                                                  prob[:, c * P:c * P + r], ident[0:L, 0:L])
                        if c % 8 == 7 or c == NC - 1:
                            end.then_inc(pt_full, 1)

            drive(pe, step)

        def pt_parts():
            for g in range(NB):
                a, z = 8 * g, min(8 * g + 8, NC)
                if z == NC and rows(NC - 1) < P:
                    yield g, a, z - 1, P, False
                    yield g, z - 1, z, rows(z - 1), True
                else:
                    yield g, a, z, P, True

        def bank(g, a, z, r):
            return pt_ps[0:r, g, (a % 8) * L:(a % 8 + z - a) * L].rearrange("p (c l) -> p c l", l=L)

        def transposed(c, r):
            return t_ps[:, slot(c), :].rearrange("p (k n) -> p k n", k=KC)[:, :, 0:r]

        @block.scalar
        def _(act):
            def high(h, i, c):
                r = rows(c)
                act.wait_ge(t_full, (2 * h + i) * NC + c + 1)
                nc.scalar.activation(t_hi[:, :, c * P:c * P + r], transposed(c, r), ACT.Copy).then_inc(t_hi_set, 1)

            def query(h, i):
                b = 2 * h + i
                nc.scalar.activation(q_hi[:, i % 2], xt_hi[:, :, bass.ds(b * L, L)].bitcast(F32), ACT.Copy).then_inc(q_set, 1)
                nc.scalar.activation(q_lo[:, i % 2], xt_lo[:, :, bass.ds(b * L, L)].bitcast(F32), ACT.Copy).then_inc(q_set, 1)

            def step(h, i, has1, has2):
                if i == -1:
                    query(h, 0)
                    for c in range(EARLY):
                        high(h, 0, c)
                if has1:
                    for c in range(EARLY, NC):
                        high(h, i + 1, c)
                    n = 2 * h + i + 1
                    act.wait_ge(nmax_set, n + 1)
                    nc.scalar.activation(prob[:, 0:S], prob[:, 0:S], ACT.Exp, bias=nmax[:, 0:1],
                                         accum_out=den[:, :]).then_inc(exp_set, 1)
                if has2:
                    query(h, i + 2)
                    for c in range(EARLY):
                        high(h, i + 2, c)
                if has1:
                    for g, a, z, r, last in pt_parts():
                        act.wait_ge(pt_full, (2 * h + i + 1) * NB + g + 1)
                        nc.scalar.activation(pt[0:r, a:z, 0, :], bank(g, a, z, r), ACT.Copy).then_inc(pt_hi_set, 1)
                if i >= 0:
                    if not has1:
                        act.wait_ge(c_out, B * 16)
                        act.wait_ge(pv_done, B * NG)
                        for b in range(B - 1):
                            back(b, c_dram[b])
                    act.wait_ge(c_set, 2 * h + i + 2)
                    if has1:
                        act.dma_start(c_dram[2 * h + i], c_sb[:, :]).then_inc(c_out, 16)
                    else:
                        back(B - 1, c_sb)

            def back(b, c):
                r, at = divmod(b, P // L)
                for part in range(2):
                    act.dma_start(nat[at * L:(at + 1) * L, 0, 2 * r + part, :],
                                  c[part * L:(part + 1) * L, :]).then_inc(x_in[r], 16)

            act.sem_inc(c_out, 16)
            drive(act, step)

        @block.vector
        def _(dve):
            parts = list(pt_parts())
            step_x = Chain(dve, own)

            def low(h, i, c):
                r = rows(c)
                dve.wait_ge(t_hi_set, (2 * h + i) * NC + c + 1)
                nc.vector.tensor_tensor(t_lo[:, :, c * P:c * P + r], transposed(c, r),
                                        t_hi[:, :, c * P:c * P + r].bitcast(F32), ALU.subtract).then_inc(t_free, 1)

            def natural_low(h, i, g):
                a, z = GROUPS[g]
                r = rows(a)
                dve.wait_ge(n_hi_set, (2 * h + i) * NG + g + 1)
                nc.vector.tensor_tensor(n_lo[0:r, a:z, :], nat[0:r, i % 2, a:z, :],
                                        n_hi[0:r, a:z, :].bitcast(F32), ALU.subtract).then_inc(lo_dve, 1)

            def maximum(h, i, t):
                c, w = TILES[t]
                w = min(w, S - c)
                dve.wait_ge(s_full, (2 * h + i) * NT + t + 1)
                nc.vector.tensor_scalar(prob[:, c:c + w], s_ps[:, t % 2, 0:w], 1.0, None, ALU.mult, ALU.max,
                                        accum_out=tmax[:, t:t + 1]).then_inc(s_free, 1)

            def normalise(n):
                dve.wait_ge(exp_set, n + 1)
                nc.vector.reciprocal(rden[:, :], den[:, :]).then_inc(rden_set, 1)
                dve.wait_ge(rden_set, n + 1)
                nc.vector.tensor_scalar(prob[:, 0:S], prob[:, 0:S], rden[:, 0:1], None, ALU.mult).then_inc(prob_set, 1)

            def step(h, i, has1, has2):
                if i == -1:
                    for c in range(EARLY):
                        low(h, 0, c)
                if has1:
                    n = 2 * h + i + 1
                    for kind, at, part in SCORES:
                        if kind == "t":
                            low(h, i + 1, at)
                        elif part == len(PARTS) - 1:
                            maximum(h, i + 1, at)
                            if at == NT // 2 and i >= 0:
                                natural_low(h, i, LO_DVE - 1)
                    dve.wait_ge(s_free, n * NT + NT + 2)
                    nc.vector.tensor_reduce(nmax[:, :], tmax[:, :], AX_X, ALU.max, negate=True).then_inc(nmax_set, 1)
                elif i >= 0:
                    natural_low(h, i, LO_DVE - 1)
                if has2:
                    for c in range(EARLY):
                        low(h, i + 2, c)
                        if c == 1:
                            normalise(n)
                        if c in (3, 5):
                            natural_low(h, i + 1, (c - 3) // 2)
                elif has1:
                    normalise(n)
                    natural_low(h, i + 1, 0)
                    natural_low(h, i + 1, 1)
                if not has1:
                    for r in range(R // P - 1):
                        dve.wait_ge(x_in[r], 32 * (P // L))
                        for part in range(2):
                            step_x(nc.vector.tensor_tensor(x_sb[:, r, :], x_sb[:, r, :], nat[:, 0, 2 * r + part, :], ALU.add))
                if i >= 0:
                    b = 2 * h + i
                    dve.wait_ge(pv_done, b * NG + 2 * NG)
                    dve.wait_ge(c_out, b * 16 + 16)
                    nc.vector.tensor_copy(c_sb[:, :], c_ps[:, :]).then_inc(c_set, 1)
                if has1:
                    for at, (g, a, z, r, last) in enumerate(parts):
                        dve.wait_ge(pt_hi_set, n * len(parts) + at + (1 if last else 2))
                        ins = nc.vector.tensor_tensor(pt[0:r, a:z, 1, :], bank(g, a, z, r),
                                                      pt[0:r, a:z, 0, :].bitcast(F32), ALU.subtract)
                        if last:
                            ins.then_inc(pt_free, 1)

            dve.sem_inc(t_free, NS)
            dve.sem_inc(s_free, 2)
            dve.sem_inc(pt_free, NB)
            dve.sem_inc(c_set, 1)
            if SE > S:
                nc.vector.memset(t_hi[:, :, S:SE].bitcast(F32), 0.0).then_inc(pad_set, 1)
                nc.vector.memset(t_lo[:, :, S:SE].bitcast(F32), 0.0).then_inc(pad_set, 1)
            drive(dve, step)
            r = R // P - 1
            dve.wait_ge(x_in[r], 32 * (P // L))
            for part in range(2):
                step_x(nc.vector.tensor_tensor(x_sb[:, r, :], x_sb[:, r, :], nat[:, 0, 2 * r + part, :], ALU.add))


class OctonionWeights:

    def __init__(self, nc, scope, given):
        self.nc, self.given = nc, given
        _, _, O = given["w_gate"].shape
        D8 = given["w_down"].shape[2]
        REST_CHUNKS = given["w_rest"].shape[1]
        KC = given["sign_in"].shape[1]
        self.O, self.D8, self.KC, self.MAIN = O, D8, KC, given["w_down"].shape[0]
        self.LEFT = O - self.MAIN
        self.PARTS = P // self.LEFT
        self.F = 8 * O
        self.FC = 8 + REST_CHUNKS
        self.WIDEST = max(self.F, REST_CHUNKS * 8 * D8)
        self.tern = [scope.sb(f"tern{i}", [P, KC * 8 * O], F32R) for i in range(2)]
        self.down, self.rest = scope.sb("down", [P, 8, D8]), scope.sb("rest", [P, REST_CHUNKS, 8, D8])
        self.sign_in, self.sign_down, self.sign_rest = (
            scope.sb("sign_in", [P, KC, 8]), scope.sb("sign_down", [P, 8, 8]), scope.sb("sign_rest", [P, REST_CHUNKS, 8]))
        self.part, self.tot = scope.sb("part", [P, 4]), scope.sb("tot", [P, 4])
        self.scale, self.half, self.nhalf = (scope.sb(n, [P, 3]) for n in ("scale", "half", "nhalf"))
        self.w_in = [scope.sem(f"w_in{i}") for i in range(4)]
        self.sign_in_set, self.zero_set, self.part_set, self.tot_full, self.own, self.own_up, \
            self.own_down, self.tern_set, self.down_tern, self.down_set = (
            scope.sem(n) for n in ("sign_in_set", "zero_set", "part_set", "tot_full", "own", "own_up",
                                 "own_down", "tern_set", "down_tern", "down_set"))

    def width(self, c):
        return self.MAIN if c < 8 else min(self.PARTS, 8 - (c - 8) * self.PARTS) * self.LEFT

    def main(self, i):
        return self.tern[i][:, 0:self.KC * 8 * self.MAIN].rearrange("p (c k o) -> p c k o", c=self.KC, k=8)

    def left(self, i):
        return self.tern[i][:, self.KC * 8 * self.MAIN:].rearrange("p (c k o) -> p c k o", c=self.KC, k=8)

    def columns(self, i, kc, c):
        if c < 8:
            return self.main(i)[:, kc, c, :]
        a = (c - 8) * self.PARTS * self.LEFT
        return self.left(i)[:, kc].rearrange("p k o -> p (k o)")[:, a:a + self.width(c)]

    def place(self, scope):
        self.raw = [scope.sb(f"raw{i}", [P, 8, self.O])[:, :, :] for i in range(2)]

    def zero(self, eng):
        eng.memset(self.rest[:, :, :, :], 0.0).then_inc(self.zero_set, 1)

    def load(self, sp):
        g = self.given
        sp.dma_start(self.sign_in[:, :, :], g["sign_in"]).then_inc(self.sign_in_set, 16)
        sp.dma_start(self.sign_down[:, :, :], g["sign_down"]).then_inc(self.sign_in_set, 16)
        sp.dma_start(self.sign_rest[:, :, :], g["sign_rest"]).then_inc(self.sign_in_set, 16)
        sp.dma_start(self.raw[0], g["w_gate"]).then_inc(self.w_in[0], 16)
        sp.dma_start(self.raw[1], g["w_up"]).then_inc(self.w_in[1], 16)
        sp.dma_start(self.down[:, :, :], g["w_down"]).then_inc(self.w_in[2], 16)
        sp.wait_ge(self.zero_set, 1)
        for c in range(8, self.FC):
            w = self.width(c)
            sp.dma_start(self.rest[0:w, c - 8], g["w_rest"][0:w, c - 8]).then_inc(self.w_in[3], 16)

    def magnitudes(self, act, spare):
        for i, w in enumerate((self.raw[0], self.raw[1], self.down[:, :, :], self.rest[:, :, :, :])):
            act.wait_ge(self.w_in[i], 16 if i < 3 else 16 * (self.FC - 8))
            w = w.rearrange("p k o -> p (k o)") if i < 3 else w.rearrange("p c k o -> p (c k o)")
            if i > 0:
                act.wait_ge(self.part_set, i)
            self.nc.scalar.activation(spare[:, 0:w.shape[1]], w, ACT.Abs,
                                      accum_out=self.part[:, i:i + 1]).then_inc(self.part_set, 1)

    def totals(self, pe, bank, ones):
        pe.wait_ge(self.part_set, 4)
        self.nc.tensor.matmul(bank[:, 0:4], ones[:, :], self.part[:, :], start=True, stop=True).then_inc(self.tot_full, 1)

    def scales(self, dve, bank):
        nc, step = self.nc, Chain(dve, self.own)
        dve.wait_ge(self.tot_full, 1)
        step(nc.vector.tensor_copy(self.tot[:, :], bank[:, 0:4]))
        step(nc.vector.tensor_scalar(self.scale[:, 0:2], self.tot[:, 0:2], 0.5 / (self.F * self.D8), None, ALU.mult))
        step(nc.vector.scalar_tensor_tensor(out=self.scale[:, 2:3], in0=self.tot[:, 3:4], scalar=0.125,
                                            in1=self.tot[:, 2:3], op0=ALU.mult, op1=ALU.add))
        step(nc.vector.tensor_scalar(self.scale[:, 2:3], self.scale[:, 2:3], 1.0 / (self.F * self.D8), None, ALU.mult))
        step(nc.vector.tensor_scalar(self.half[:, :], self.scale[:, :], 0.5, None, ALU.mult))
        step(nc.vector.tensor_scalar(self.nhalf[:, :], self.scale[:, :], -0.5, None, ALU.mult))

    def ternary(self, dve, spare, down):
        nc, step = self.nc, Chain(dve, self.own_down if down else self.own_up)
        if down:
            todo = [(self.down[:, :, :].rearrange("p k o -> p (k o)"), 2),
                    (self.rest[:, :, :, :].rearrange("p c k o -> p (c k o)"), 2)]
        else:
            todo = [(self.raw[i].rearrange("p k o -> p (k o)"), i) for i in (1, 0)]
        for w, at in todo:
            m = spare[:, 0:w.shape[1]]
            step(nc.vector.tensor_scalar(m, w, self.nhalf[:, at:at + 1], None, ALU.is_lt))
            step(nc.vector.scalar_tensor_tensor(out=w, in0=w, scalar=self.half[:, at:at + 1], in1=m,
                                                op0=ALU.is_gt, op1=ALU.subtract))
            dve.sem_inc(self.down_tern if down else self.tern_set, 1)

    def permuted(self, eng, out, src, sign, mask):
        n = out.shape[2]
        if mask == 0:
            return eng.tensor_tensor(out, src, sign.unsqueeze(2).broadcast_to([out.shape[0], 8, n]), ALU.mult)
        o, s = (t.rearrange("p (a b c) o -> p a b c o", a=2, b=2) for t in (out, src))
        g = sign.rearrange("p (a b c) -> p a b c", a=2, b=2)
        bits = [mask >> 2 & 1, mask >> 1 & 1, mask & 1]
        for v in range(8):
            v = [v >> 2 & 1, v >> 1 & 1, v & 1]
            if any(x and not b for x, b in zip(v, bits)):
                continue
            to = (slice(None), *(x if b else slice(None) for x, b in zip(v, bits)))
            frm = (slice(None), *(1 - x if b else slice(None) for x, b in zip(v, bits)))
            sg = g[to]
            end = eng.tensor_tensor(o[to], s[frm], sg.unsqueeze(len(sg.shape)).broadcast_to([*sg.shape, n]), ALU.mult)
        return end

    def spread(self, eng, i):
        for kc in range(self.KC):
            for out, a, z in ((self.main(i), 0, self.MAIN), (self.left(i), self.MAIN, self.O)):
                self.permuted(eng, out[:, kc], self.raw[i][:, :, a:z], self.sign_in[:, kc, :], 2 * kc)

    def spread_down(self, eng, waits, out):
        waits.wait_ge(self.down_tern, 1)
        for c in range(8):
            self.permuted(eng, out[:, c], self.down[:, :, :], self.sign_down[:, c, :], c).then_inc(self.down_set, 1)
        waits.wait_ge(self.down_tern, 2)
        for c in range(8, self.FC):
            self.permuted(eng, out[:, c], self.rest[:, c - 8], self.sign_rest[:, c - 8, :], 0).then_inc(self.down_set, 1)


def self_attention(nc, x_sb, xt_hi, xt_lo, w_qkv, w_o, rotary, head_mask, causal, ident, ones, B, NH, weights):
    RT, H = x_sb.shape[1:]
    KC = H // P
    R = RT * P
    L = R // B
    BR = P // L
    HD = H // NH
    HC = P // HD
    HP = P // L
    SCALE = float(HD) ** -0.5
    with Scope(nc, "sa") as top:
        qz_hi, qz_lo = (t[:, 0:RT * KC * BR * P].rearrange("p (r k b c) -> p r k b c", r=RT, k=KC, b=BR)
                        for t in weights.tern)
        kt_hi, kt_lo = (top.sb(n, [P, RT, KC, P], F32R) for n in ("kt_hi", "kt_lo"))
        v_hi, v_lo = (top.sb(n, [P, B, H], F32R) for n in ("v_hi", "v_lo"))
        hm, cm = top.sb("hm", [P, HC]), top.sb("cm", [P, L])

        with Scope(nc, "sa1") as sc:
            raw = sc.sb("raw", [P, 2, KC, H])
            w_hi, w_lo = sc.sb("w_hi", [P, 3, KC, H], F32R), sc.sb("w_lo", [P, 3, KC, H], F32R)
            rot = sc.sb("rot", [P, 3])
            w_in = [sc.sem(f"w_in{i}") for i in range(3)]
            small_in, w_hi_set, w_lo_set, p_full, a_set, r_set, zero_set, t_full, t_hi_set, t_free = (
                sc.sem(n) for n in ("small_in", "w_hi_set", "w_lo_set", "p_full", "a_set", "r_set",
                                    "zero_set", "t_full", "t_hi_set", "t_free"))
            xd_set, v_full, v_hi_set, v_free = (sc.sem(n) for n in ("xd_set", "v_full", "v_hi_set", "v_free"))

            def load(sp):
                for i in range(2):
                    sp.dma_start(raw[:, i], w_qkv[i]).then_inc(w_in[i], 16)
                sp.dma_start(rot[:, :], rotary).then_inc(small_in, 16)
                sp.dma_start(hm[:, :], head_mask).then_inc(small_in, 16)
                sp.dma_start(cm[:, :], causal).then_inc(small_in, 16)

            def prepare(pool):
                pool.wait_ge(w_in[0], 16)
                split_on_pool(nc, pool, w_hi[:, 0], w_lo[:, 0], raw[:, 0], w_hi_set, 1).then_inc(w_lo_set, 1)

            layernorm_transposed(nc, "sa_ln", x_sb, xt_hi, xt_lo, ident, load, prepare)
            xd = sc.sb("xd", [P, 2, 2, KC, HP, L], F32R)
            a_sb = sc.sb("a_sb", [P, 2, H])
            r_sb = sc.sb("r_sb", [P, 2, H])
            p_ps = sc.ps("p_ps", [P, 2, 512])
            v_ps = sc.ps("v_ps", [P, 2, 512])
            t_ps = sc.ps("t_ps", [P, 2, 512])
            block = sc.block()
            units = [(i, r) for r in range(RT) for i in range(2)]

            def of_part(t, h):
                return t[h * L:(h + 1) * L].rearrange("p (m h d) -> p m h d", h=HP, d=HD)[:, :, h]

            @block.sync
            def _(sp):
                sp.wait_ge(w_lo_set, 1)
                sp.dma_start(raw[:, 0], w_qkv[2]).then_inc(w_in[2], 16)

            @block.gpsimd
            def _(pool):
                nc.gpsimd.memset(qz_hi[:, :, :, :, :].bitcast(F32), 0.0).then_inc(zero_set, 1)
                nc.gpsimd.memset(qz_lo[:, :, :, :, :].bitcast(F32), 0.0).then_inc(zero_set, 1)
                nc.gpsimd.memset(v_hi[:, :, :].bitcast(F32), 0.0).then_inc(zero_set, 1)
                nc.gpsimd.memset(v_lo[:, :, :].bitcast(F32), 0.0).then_inc(zero_set, 1)
                for b in range(B):
                    if b >= 2:
                        pool.wait_ge(v_full, b - 1)
                    for i, t in enumerate((xt_hi, xt_lo)):
                        nc.gpsimd.tensor_scalar(xd[:, b % 2, i], t[:, :, b * L:(b + 1) * L].bitcast(F32).unsqueeze(2)
                                                .broadcast_to([P, KC, HP, L]), 1.0, 1.0,
                                                ALU.mult, ALU.mult).then_inc(xd_set, 1)

            @block.tensor
            def _(pe):
                def transposes(n):
                    pe.wait_ge(r_set, 2 * n + 2)
                    if n >= 2:
                        pe.wait_ge(t_free, n - 1)
                    for k in range(KC):
                        end = nc.tensor.transpose(t_ps[:, n % 2, k * P:(k + 1) * P], r_sb[:, n % 2, k * P:(k + 1) * P],
                                                  ident[:, :])
                    end.then_inc(t_full, 1)

                for n, (i, r) in enumerate(units):
                    pe.wait_ge(w_lo_set, i + 1)
                    if n >= 2:
                        pe.wait_ge(r_set, 2 * n - 2)
                    for k in range(KC):
                        rs = slice(r * P, (r + 1) * P)
                        end = product(nc, p_ps[:, n % 2, :], (xt_hi[:, k, rs], xt_lo[:, k, rs]),
                                      (w_hi[:, i, k, :], w_lo[:, i, k, :]), k == 0, k == KC - 1)
                    end.then_inc(p_full, 1)
                    if n > 0:
                        transposes(n - 1)
                transposes(len(units) - 1)
                pe.wait_ge(w_lo_set, 3)
                for b in range(B):
                    if b >= 2:
                        pe.wait_ge(v_free, b - 1)
                    pe.wait_ge(xd_set, 2 * b + 2)
                    for k in range(KC):
                        rows = [xd[:, b % 2, i, k].rearrange("p h l -> p (h l)") for i in range(2)]
                        end = product(nc, v_ps[:, b % 2, :], rows,
                                      (w_hi[:, 2, k, :], w_lo[:, 2, k, :]), k == 0, k == KC - 1)
                    end.then_inc(v_full, 1)

            def turned(n, bank):
                i, r = units[n]
                if i:
                    return [(kt_hi[:, r], kt_lo[:, r], bank.rearrange("p (k c) -> p k c", k=KC))]
                v = bank.rearrange("p (k b l) -> p b k l", k=KC, b=BR)
                return [(qz_hi[:, r, :, b, b * L:(b + 1) * L], qz_lo[:, r, :, b, b * L:(b + 1) * L], v[:, b])
                        for b in range(BR)]

            @block.scalar
            def _(act):
                for i in range(1, 3):
                    act.wait_ge(w_in[i], 16)
                    nc.scalar.activation(w_hi[:, i], raw[:, i % 2], ACT.Copy).then_inc(w_hi_set, 1)
                act.wait_ge(small_in, 48)
                act.wait_ge(zero_set, 2)

                def high(n):
                    act.wait_ge(t_full, n + 1)
                    for hi, _, src in turned(n, t_ps[:, n % 2, :]):
                        end = nc.scalar.activation(hi, src, ACT.Copy)
                    end.then_inc(t_hi_set, 1)

                for n in range(len(units)):
                    act.wait_ge(p_full, n + 1)
                    if n >= 2:
                        act.wait_ge(r_set, 2 * n - 2)
                    nc.scalar.activation(a_sb[:, n % 2, :], p_ps[:, n % 2, :], ACT.Copy,
                                         scale=rot[:, 0:1]).then_inc(a_set, 1)
                    if n > 0:
                        high(n - 1)
                high(len(units) - 1)
                act.wait_ge(zero_set, 4)
                for b in range(B):
                    act.wait_ge(v_full, b + 1)
                    for h in range(HP):
                        end = nc.scalar.activation(of_part(v_hi[:, b, :], h), of_part(v_ps[:, b % 2, :], h), ACT.Copy)
                    end.then_inc(v_hi_set, 1)

            @block.vector
            def _(dve):
                for i in range(1, 3):
                    dve.wait_ge(w_hi_set, i + 1)
                    nc.vector.tensor_tensor(w_lo[:, i], raw[:, i % 2], w_hi[:, i].bitcast(F32),
                                            ALU.subtract).then_inc(w_lo_set, 1)
                dve.wait_ge(small_in, 48)

                def low_part(n):
                    dve.wait_ge(t_hi_set, n + 1)
                    for hi, lo, src in turned(n, t_ps[:, n % 2, :]):
                        end = nc.vector.tensor_tensor(lo, src, hi.bitcast(F32), ALU.subtract)
                    end.then_inc(t_free, 1)

                for n in range(len(units)):
                    src = p_ps[:, n % 2, :].rearrange("p (m e) -> p e m", e=2)
                    a = a_sb[:, n % 2, :].rearrange("p (m e) -> p e m", e=2)
                    out = r_sb[:, n % 2, :].rearrange("p (m e) -> p e m", e=2)
                    dve.wait_ge(a_set, n + 1)
                    if n >= 2:
                        dve.wait_ge(t_full, n - 1)
                    nc.vector.scalar_tensor_tensor(out=out[:, 0], in0=src[:, 1], scalar=rot[:, 2:3], in1=a[:, 0],
                                                   op0=ALU.mult, op1=ALU.add).then_inc(r_set, 1)
                    nc.vector.scalar_tensor_tensor(out=out[:, 1], in0=src[:, 0], scalar=rot[:, 1:2], in1=a[:, 1],
                                                   op0=ALU.mult, op1=ALU.add).then_inc(r_set, 1)
                    if n > 0:
                        low_part(n - 1)
                low_part(len(units) - 1)
                for b in range(B):
                    dve.wait_ge(v_hi_set, b + 1)
                    for h in range(HP):
                        end = nc.vector.tensor_tensor(of_part(v_lo[:, b, :], h), of_part(v_ps[:, b % 2, :], h),
                                                      of_part(v_hi[:, b, :], h).bitcast(F32), ALU.subtract)
                    end.then_inc(v_free, 1)

        o_sb = top.sb("o_sb", [L, B, H])
        weights.place(top)
        wo_hi, wo_lo = top.sb("wo_hi", [P, KC, H], F32R), top.sb("wo_lo", [P, KC, H], F32R)

        with Scope(nc, "sa2") as sc:
            kb_hi, kb_lo = (sc.sb(n, [P, 2, BR, HC, L], F32R) for n in ("kb_hi", "kb_lo"))
            NS = 3
            s_sb = sc.sb("s_sb", [P, NS, HC, L])
            nmx, sm, rs_ = sc.sb("nmx", [P, 2, HC]), sc.sb("sm", [P, 2, HC]), sc.sb("rs", [P, 2, HC])
            pt_hi, pt_lo = (sc.sb(n, [P, 2, HC // HP, P], F32R) for n in ("pt_hi", "pt_lo"))
            s_ps = sc.ps("s_ps", [P, 2, 512])
            t_ps = sc.ps("t_ps", [P, 2, 512])
            o_ps = sc.ps("o_ps", [L, 2, BR, 512])
            kb_hi_set, kb_lo_set, s_full, s_read, d_set, e_set, r_set, p_set, t_full, t_hi_set, t_lo_set = (
                sc.sem(n) for n in ("kb_hi_set", "kb_lo_set", "s_full", "s_read", "d_set", "e_set", "r_set",
                                    "p_set", "t_full", "t_hi_set", "t_lo_set"))
            o_full, o_free = sc.sem("o_full"), sc.sem("o_free")
            wo_in, wo_hi_set, wo_lo_set = sc.sem("wo_in"), sc.sem("wo_hi_set"), sc.sem("wo_lo_set")
            wo_raw = sc.sb("wo_raw", [P, KC, H])
            block = sc.block()
            units = [(r, c) for r in range(RT) for c in range(KC)]
            NU = len(units)

            def wide(t):
                return t.unsqueeze(2).broadcast_to([P, HC, L])

            def blocks(eng, out, kt, n, sem):
                r, c = units[n]
                for b in range(BR):
                    end = eng.tensor_tensor(out[:, n % 2, b], kt[:, r, c, b * L:(b + 1) * L].bitcast(F32).unsqueeze(1)
                                            .broadcast_to([P, HC, L]), wide(hm[:, :]), ALU.mult)
                end.then_inc(sem, 1)

            @block.sync
            def _(sp):
                sp.dma_start(wo_raw[:, :, :], w_o).then_inc(wo_in, 16)
                weights.load(sp)

            @block.gpsimd
            def _(pool):
                blocks(nc.gpsimd, kb_hi, kt_hi, 0, kb_hi_set)
                weights.zero(nc.gpsimd)
                for n in range(NU + 1):
                    if n + 1 < NU:
                        if n >= 1:
                            pool.wait_ge(s_full, n)
                        blocks(nc.gpsimd, kb_hi, kt_hi, n + 1, kb_hi_set)
                    if n > 0:
                        m = n - 1
                        pool.wait_ge(r_set, m + 1)
                        nc.gpsimd.tensor_tensor(s_sb[:, m % NS], s_sb[:, m % NS], wide(rs_[:, m % 2, :]),
                                                ALU.mult).then_inc(p_set, 1)
                    if 2 <= n < 2 + KC:
                        k = n - 2
                        pool.wait_ge(wo_hi_set, 1)
                        nc.gpsimd.tensor_tensor(wo_lo[:, k, :], wo_raw[:, k, :], wo_hi[:, k, :].bitcast(F32),
                                                ALU.subtract).then_inc(wo_lo_set, 1)

            @block.tensor
            def _(pe):
                def scores(n):
                    r, c = units[n]
                    pe.wait_ge(kb_hi_set, n + 1)
                    pe.wait_ge(kb_lo_set, n + 1)
                    if n >= 2:
                        pe.wait_ge(s_read, n - 1)
                    for b in range(BR):
                        end = product(nc, s_ps[:, n % 2, :], (qz_hi[:, r, c, b, :], qz_lo[:, r, c, b, :]),
                                      (kb_hi[:, n % 2, b].rearrange("p h l -> p (h l)"),
                                       kb_lo[:, n % 2, b].rearrange("p h l -> p (h l)")), b == 0, b == BR - 1)
                    end.then_inc(s_full, 1)

                def attend(n):
                    r, c = units[n]
                    pe.wait_ge(p_set, n + 1)
                    if n >= 2:
                        pe.wait_ge(t_lo_set, n - 1)
                    for i in range(HC // HP):
                        end = nc.tensor.transpose(t_ps[:, n % 2, i * P:(i + 1) * P],
                                                  s_sb[:, n % NS, i * HP:(i + 1) * HP, :].rearrange("p h l -> p (h l)"),
                                                  ident[:, :])
                    end.then_inc(t_full, 1)

                def values(n):
                    r, c = units[n]
                    pe.wait_ge(t_lo_set, n + 1)
                    if c == 0 and r > 1:
                        pe.wait_ge(o_free, r - 1)
                    for b in range(BR):
                        for i in range(HC // HP):
                            cs = slice(c * P + i * HP * HD, c * P + (i + 1) * HP * HD)
                            ls = slice(b * L, (b + 1) * L)
                            end = product(nc, o_ps[:, r % 2, b, cs], (pt_hi[:, n % 2, i, ls], pt_lo[:, n % 2, i, ls]),
                                          (v_hi[:, r * BR + b, cs], v_lo[:, r * BR + b, cs]), True, True)
                    end.then_inc(o_full, 1)

                scores(0)
                for n in range(NU + 2):
                    if n + 1 < NU:
                        scores(n + 1)
                    if 1 <= n <= NU:
                        attend(n - 1)
                    if n >= 2:
                        values(n - 2)

            def high(act, n):
                act.wait_ge(t_full, n + 1)
                if n >= 2:
                    act.wait_ge(o_full, n - 1)
                nc.scalar.activation(pt_hi[:, n % 2].rearrange("p i c -> p (i c)"), t_ps[:, n % 2, :],
                                     ACT.Copy).then_inc(t_hi_set, 1)

            @block.scalar
            def _(act):
                act.wait_ge(wo_in, 16)
                nc.scalar.activation(wo_hi[:, :, :], wo_raw[:, :, :], ACT.Copy).then_inc(wo_hi_set, 1)
                for n in range(NU):
                    act.wait_ge(d_set, n + 1)
                    for h in range(HC):
                        s = s_sb[:, n % NS, h, :]
                        end = nc.scalar.activation(s, s, ACT.Exp, bias=nmx[:, n % 2, h:h + 1],
                                                   accum_out=sm[:, n % 2, h:h + 1])
                    end.then_inc(e_set, 1)
                    if n > 0:
                        high(act, n - 1)
                high(act, NU - 1)
                act.wait_ge(wo_lo_set, KC)
                weights.magnitudes(act, wo_raw[:, :, :].rearrange("p k h -> p (k h)"))

            @block.vector
            def _(dve):
                def softmax(n):
                    s = s_sb[:, n % NS]
                    dve.wait_ge(s_full, n + 1)
                    if n >= NS:
                        dve.wait_ge(t_full, n - NS + 1)
                    ins = nc.vector.scalar_tensor_tensor(
                        out=s, in0=s_ps[:, n % 2, :].rearrange("p (h l) -> p h l", h=HC), scalar=SCALE,
                        in1=cm[:, :].unsqueeze(1).broadcast_to([P, HC, L]), op0=ALU.mult, op1=ALU.add)
                    ins.then_inc(s_read, 1)
                    dve.wait_ge(s_read, n + 1)
                    nc.vector.tensor_reduce(nmx[:, n % 2, :], s, AX_X, ALU.max, negate=True).then_inc(d_set, 1)

                def sums(n):
                    dve.wait_ge(e_set, n + 1)
                    nc.vector.reciprocal(rs_[:, n % 2, :], sm[:, n % 2, :]).then_inc(r_set, 1)

                def low(n):
                    dve.wait_ge(t_hi_set, n + 1)
                    nc.vector.tensor_tensor(pt_lo[:, n % 2].rearrange("p i c -> p (i c)"), t_ps[:, n % 2, :],
                                            pt_hi[:, n % 2].rearrange("p i c -> p (i c)").bitcast(F32),
                                            ALU.subtract).then_inc(t_lo_set, 1)

                def output(r):
                    dve.wait_ge(o_full, (r + 1) * KC)
                    nc.vector.tensor_copy(o_sb[:, r * BR:(r + 1) * BR, :], o_ps[:, r % 2]).then_inc(o_free, 1)

                blocks(nc.vector, kb_lo, kt_lo, 0, kb_lo_set)
                for n in range(NU + 2):
                    if n + 1 < NU:
                        if n >= 1:
                            dve.wait_ge(s_full, n)
                        blocks(nc.vector, kb_lo, kt_lo, n + 1, kb_lo_set)
                    if n < NU:
                        softmax(n)
                    if n > KC and n % KC == 2 % KC:
                        output(n // KC - 1)
                    if 1 <= n <= NU:
                        sums(n - 1)
                    if n >= 2:
                        low(n - 2)
                output(RT - 1)

        with Scope(nc, "sa3") as sc:
            ot_hi, ot_lo = sc.sb("ot_hi", [P, KC, R], F32R), sc.sb("ot_lo", [P, KC, R], F32R)
            t_ps = sc.ps("t_ps", [P, RT, 512])
            ps = sc.ps("ps", [P, RT, 512])
            spare = sc.sb("spare", [P, weights.WIDEST])
            t_full, hi_set, lo_set, done = (sc.sem(n) for n in ("t_full", "hi_set", "lo_set", "done"))
            block = sc.block()

            @block.gpsimd
            def _(pool):
                pool.wait_ge(weights.tern_set, 1)
                weights.spread(nc.gpsimd, 1)

            @block.tensor
            def _(pe):
                for r in range(RT):
                    for k in range(KC):
                        for b in range(BR):
                            o = k * P + b * L
                            end = nc.tensor.transpose(t_ps[:, r, o:o + L], o_sb[:, r * BR + b, k * P:(k + 1) * P],
                                                      ident[0:L, 0:L])
                    end.then_inc(t_full, 1)
                for r in range(RT):
                    pe.wait_ge(lo_set, r + 1)
                    if r == 0:
                        weights.totals(pe, t_ps[:, 0, :], ones)
                    rs = slice(r * P, (r + 1) * P)
                    for k in range(KC):
                        end = product(nc, ps[:, r, :], (ot_hi[:, k, rs], ot_lo[:, k, rs]),
                                      (wo_hi[:, k, :], wo_lo[:, k, :]), k == 0, k == KC - 1)
                    end.then_inc(done, 1)

            @block.scalar
            def _(act):
                for r in range(RT):
                    act.wait_ge(t_full, r + 1)
                    nc.scalar.activation(ot_hi[:, :, r * P:(r + 1) * P], t_ps[:, r, :].rearrange("p (k c) -> p k c", k=KC),
                                         ACT.Copy).then_inc(hi_set, 1)

            @block.vector
            def _(dve):
                for r in range(RT):
                    dve.wait_ge(hi_set, r + 1)
                    rs = slice(r * P, (r + 1) * P)
                    nc.vector.tensor_tensor(ot_lo[:, :, rs], t_ps[:, r, :].rearrange("p (k c) -> p k c", k=KC),
                                            ot_hi[:, :, rs].bitcast(F32), ALU.subtract).then_inc(lo_set, 1)
                dve.wait_ge(weights.sign_in_set, 48)
                weights.scales(dve, t_ps[:, 0, :])
                weights.ternary(dve, spare, False)
                weights.spread(nc.vector, 0)
                for r in range(RT):
                    dve.wait_ge(done, r + 1)
                    nc.vector.tensor_tensor(x_sb[:, r, :], ps[:, r, :], x_sb[:, r, :], ALU.add)


def octonion_ffn(nc, x_sb, xt_hi, xt_lo, weights):
    RT, H = x_sb.shape[1:]
    KC, FC, width, scale = weights.KC, weights.FC, weights.width, weights.scale
    R = RT * P

    with Scope(nc, "fo") as sc:
        g_sb, h_sb = sc.sb("g_sb", [P, 2, R]), sc.sb("h_sb", [P, 2, R])
        h_hi, h_lo = sc.sb("h_hi", [P, 2, R], F32R), sc.sb("h_lo", [P, 2, R], F32R)
        spare = sc.sb("spare", [P, weights.WIDEST])
        tern_d = sc.sb("tern_d", [P, FC, 8, weights.D8], F32R)
        gu_ps = sc.ps("gu_ps", [P, 4, 512])
        ps = sc.ps("ps", [P, RT, 512])
        gu_full, g_set, u_read, h_hi_set, h_lo_set, used, done = (
            sc.sem(n) for n in ("gu_full", "g_set", "u_read", "h_hi_set", "h_lo_set", "used", "done"))
        block = sc.block()

        @block.gpsimd
        def _(pool):
            weights.spread_down(nc.gpsimd, pool, tern_d)

        @block.tensor
        def _(pe):
            def down(c):
                w = width(c)
                pe.wait_ge(h_lo_set, c + 1)
                pe.wait_ge(weights.down_set, c + 1)
                for r in range(RT):
                    rs = slice(r * P, (r + 1) * P)
                    t = tern_d[0:w, c].rearrange("p k o -> p (k o)")
                    nc.tensor.matmul(ps[:, r, :], h_hi[0:w, c % 2, rs], t, start=c == 0, stop=False)
                    end = nc.tensor.matmul(ps[:, r, :], h_lo[0:w, c % 2, rs], t, start=False, stop=c == FC - 1)
                    if c == FC - 1:
                        end.then_inc(done, 1)
                if c < FC - 1:
                    end.then_inc(used, 1)

            for c in range(FC):
                w = width(c)
                for i in range(2):
                    if c >= 2:
                        pe.wait_ge((g_set, u_read)[i], c - 1)
                    for k in range(KC):
                        o = gu_ps[0:w, 2 * (c % 2) + i, :]
                        t = weights.columns(i, k, c)
                        nc.tensor.matmul(o, t, xt_hi[:, k, :], start=k == 0, stop=False)
                        end = nc.tensor.matmul(o, t, xt_lo[:, k, :], start=False, stop=k == KC - 1)
                    end.then_inc(gu_full, 1)
                if c > 1:
                    down(c - 2)
            down(FC - 2)
            down(FC - 1)

        @block.scalar
        def _(act):
            def high(c):
                w = width(c)
                act.wait_ge(u_read, c + 1)
                if c >= 2:
                    act.wait_ge(used, c - 1)
                nc.scalar.activation(h_hi[0:w, c % 2, :], h_sb[0:w, c % 2, :], ACT.Copy).then_inc(h_hi_set, 1)

            for c in range(FC):
                w = width(c)
                act.wait_ge(gu_full, 2 * c + 1)
                if c >= 2:
                    act.wait_ge(u_read, c - 1)
                nc.scalar.activation(g_sb[0:w, c % 2, :], gu_ps[0:w, 2 * (c % 2), :], ACT.Silu,
                                     scale=scale[0:w, 0:1]).then_inc(g_set, 1)
                if c > 0:
                    high(c - 1)
            high(FC - 1)

        @block.vector
        def _(dve):
            weights.ternary(dve, spare, True)

            def low(c):
                w = width(c)
                dve.wait_ge(h_hi_set, c + 1)
                nc.vector.tensor_tensor(h_lo[0:w, c % 2, :], h_sb[0:w, c % 2, :], h_hi[0:w, c % 2, :].bitcast(F32),
                                        ALU.subtract).then_inc(h_lo_set, 1)

            for c in range(FC):
                w = width(c)
                dve.wait_ge(g_set, c + 1)
                dve.wait_ge(gu_full, 2 * c + 2)
                if c >= 2:
                    dve.wait_ge(h_lo_set, c - 1)
                nc.vector.scalar_tensor_tensor(out=h_sb[0:w, c % 2, :], in0=gu_ps[0:w, 2 * (c % 2) + 1, :],
                                               scalar=scale[0:w, 1:2], in1=g_sb[0:w, c % 2, :],
                                               op0=ALU.mult, op1=ALU.mult).then_inc(u_read, 1)
                if c > 0:
                    low(c - 1)
            low(FC - 1)
            for r in range(RT):
                dve.wait_ge(done, r + 1)
                nc.vector.scalar_tensor_tensor(out=x_sb[:, r, :], in0=ps[:, r, :], scalar=scale[:, 2:3],
                                               in1=x_sb[:, r, :], op0=ALU.mult, op1=ALU.add)


def attention_constants(L, HD):
    step = np.arange(P) % L
    angle = step.astype(np.float32)
    return {
        "rotary": np.stack([np.cos(angle), np.sin(angle), -np.sin(angle)], 1),
        "head_mask": (np.arange(P)[:, None] // HD == np.arange(P // HD)).astype(np.float32),
        "causal": np.where(np.arange(L) <= step[:, None], np.float32(0), np.float32(-1e30)),
    }


def octonion_signs():
    s = np.zeros((8, 8, 8), np.float32)
    s[0, 0, 0] = 1
    for i in range(1, 8):
        s[0, i, i] = s[i, 0, i] = 1
        s[i, i, 0] = -1
    for a, b, c in [(1, 2, 3), (1, 4, 5), (1, 7, 6), (2, 4, 6), (2, 5, 7), (3, 4, 7), (3, 6, 5)]:
        for x, y, z in ((a, b, c), (b, c, a), (c, a, b)):
            s[x, y, z], s[y, x, z] = 1, -1
    return s.sum(0)


def perceiver(nc, x, ctx, ctx_t, identity, xa, ma, fl, sa, of, out):
    B = ctx.shape[0]
    _, RT, H = x.shape
    R = RT * P
    NKV = xa["wk"].shape[0]
    GL = xa["wq"].shape[3] * (R // B) // P
    q_dram = nc.dram_tensor("q_scratch", (B, NKV, P, GL), F32, kind="Internal").ap()
    o_dram = nc.dram_tensor("o_scratch", (B, NKV, P, GL), F32, kind="Internal").ap()
    c_dram = nc.dram_tensor("c_scratch", (B, 2 * R // B, H), F32, kind="Internal").ap()
    with Scope(nc, "all") as sc:
        x_sb, ident, ones = sc.sb("x", [P, RT, H]), sc.sb("ident", [P, P]), sc.sb("ones", [P, P])
        x_in, x_out = sc.sem("x_in"), sc.sem("x_out")
        with nc.Block() as block:
            @block.gpsimd
            def _(pool):
                nc.gpsimd.memset(ones[:, :], 1.0)

            @block.sync
            def _(sp):
                sp.dma_start(x_sb[:, :, :], x).then_inc(x_in, 16)
                sp.dma_start(ident[:, :], identity).then_inc(x_in, 16)
                sp.wait_ge(x_in, 32)

        def normalised(name, stage, plain=True):
            with Scope(nc, name) as s:
                xt_hi, xt_lo = s.sb("xt_hi", [P, H // P, R], F32R), s.sb("xt_lo", [P, H // P, R], F32R)
                if plain:
                    layernorm_transposed(nc, f"{name}_ln", x_sb, xt_hi, xt_lo, ident)
                stage(xt_hi, xt_lo)

        with Scope(nc, "ctx") as s:
            context = Context(nc, s, ctx_t)
            normalised("n0", lambda hi, lo: queries(nc, x_sb, ident, hi, lo, xa["wq"], xa["bq"], q_dram, context), False)
            cross_attention(nc, context, xa["wk"], xa["wv"], xa["bk"], xa["bv"], ident, q_dram, o_dram)
        attention_output(nc, x_sb, o_dram, xa["wo"], xa["bo"])
        with Scope(nc, "fl") as s:
            ternary = TernaryWeights(nc, s, fl["w"], fl["bias"])
            mamba(nc, x_sb, ident, B, **ma, following=ternary)
            normalised("n2", lambda hi, lo: ternary_linear(nc, x_sb, hi, lo, ternary, ones))
        normalised("n3", lambda hi, lo: context_attention(nc, x_sb, hi, lo, ctx, ident, c_dram))
        with Scope(nc, "of") as s:
            weights = OctonionWeights(nc, s, of)
            normalised("n4", lambda hi, lo: self_attention(nc, x_sb, hi, lo, sa["w_qkv"], sa["w_o"], sa["rotary"],
                                                           sa["head_mask"], sa["causal"], ident, ones, B, 32, weights),
                       False)
            normalised("n5", lambda hi, lo: octonion_ffn(nc, x_sb, hi, lo, weights))
        with nc.Block() as block:
            @block.sync
            def _(sp):
                sp.dma_start(out, x_sb[:, :, :]).then_inc(x_out, 16)
                sp.wait_ge(x_out, 16)


def kernel(**inputs):
    import numpy as np
    import concourse.bacc as bacc
    from concourse.bass_utils import run_bass_kernel_spmd

    def lay(a):
        return np.ascontiguousarray(a)

    def rows(w, shape=None):
        w = np.asarray(w)
        return lay(w.reshape(-1, P, *w.shape[1:]).swapaxes(0, 1))

    i = {k: np.asarray(v) for k, v in inputs.items()}
    B, L, H = i["x"].shape
    S = i["ctx_4096"].shape[1]
    NKV, D, NH = 8, 128, 32
    G = NH // NKV
    KD = NKV * D
    wkv = i["L0_xattn_Wkv"]
    sign = octonion_signs()
    O, D8 = i["L1_ffn_w_gate"].shape[1:]
    MAIN = min(O, P)
    LEFT = O - MAIN
    PARTS = P // LEFT
    REST_CHUNKS = -(-8 // PARTS)

    def halves(w):
        return lay(np.concatenate([w[np.arange(8) ^ p].transpose(2, 0, 1) for p in range(P // D8)]))

    def rest(t):
        out = np.zeros((REST_CHUNKS * PARTS, *t.shape[1:]), t.dtype)
        out[:8] = t
        out = out.reshape(REST_CHUNKS, PARTS * LEFT, *t.shape[2:]).swapaxes(0, 1)
        return lay(np.concatenate([out, np.zeros((P - len(out), *out.shape[1:]), t.dtype)]))

    pick = np.arange(8)[:, None] ^ np.arange(8)
    down = i["L1_ffn_w_down"].transpose(2, 0, 1)

    groups = {
        "xa": {
            "wq": lay(i["L0_xattn_Wq"].reshape(H // P, P, NKV, G * D).transpose(2, 1, 0, 3)),
            "bq": lay(i["L0_xattn_bq"].reshape(NH, D).T),
            "wk": lay(wkv[:, :KD].reshape(H // P, P, NKV, D).transpose(2, 1, 0, 3)),
            "wv": lay(wkv[:, KD:].reshape(H // P, P, NKV // 2, 2 * D).transpose(2, 1, 0, 3)),
            "bk": lay(i["L0_xattn_bkv"][:KD].reshape(NKV, D).T),
            "bv": lay(i["L0_xattn_bkv"][KD:].reshape(NKV, D).T),
            "wo": lay(i["L0_xattn_Wo"].reshape(NKV, G, D, H).transpose(0, 2, 1, 3)),
            "bo": lay(i["L0_xattn_bo"]),
        },
        "ma": {
            "w_in": lay(i["L0_attn_W_in"].T.reshape(H // P, P, 2, -1, P).transpose(3, 1, 2, 0, 4)),
            "conv_w": rows(i["L0_attn_conv_w"]),
            "conv_b": rows(i["L0_attn_conv_b"]),
            "w_x": rows(i["L0_attn_W_x"].T),
            "w_dt": lay(i["L0_attn_W_dt"].T),
            "b_dt": rows(i["L0_attn_b_dt"]),
            "a_log": rows(i["L0_attn_A_log"]),
            "d_skip": rows(i["L0_attn_D"]),
            "w_out": rows(i["L0_attn_W_out"].T),
        },
        "fl": {"w": rows(i["L0_ffn_weight"].T), "bias": lay(i["L0_ffn_bias"])},
        "sa": {
            "w_qkv": np.stack([rows(i[f"L1_attn_w{n}"].T) for n in "qkv"]),
            "w_o": rows(i["L1_attn_wo"].T),
            **attention_constants(L, H // NH),
        },
        "of": {
            "w_gate": halves(i["L1_ffn_w_gate"]),
            "w_up": halves(i["L1_ffn_w_up"]),
            "w_down": lay(down[:MAIN]),
            "w_rest": rest(down[MAIN:][:, pick].swapaxes(0, 1)),
            "sign_in": rows(np.repeat(sign, D8, 0)),
            "sign_down": lay(np.broadcast_to(sign, (P, 8, 8))),
            "sign_rest": rest(np.repeat(sign[:, None], LEFT, 1)),
        },
    }
    alone = {
        "x": rows(i["x"].reshape(B * L, H)),
        "ctx": lay(i["ctx_4096"]),
        "ctx_t": lay(i["ctx_4096"].transpose(0, 2, 1).reshape(B, H // P, P, S).swapaxes(1, 2)),
        "identity": np.eye(P, dtype=np.float32),
    }

    nc = bacc.Bacc("TRN2", target_bir_lowering=False, num_devices=1)
    arrays = {}

    def given(name, a):
        arrays[f"in_{name}"] = a
        return nc.dram_tensor(f"in_{name}", a.shape, mybir.dt.from_np(a.dtype), kind="ExternalInput").ap()

    args = {n: given(n, a) for n, a in alone.items()}
    args |= {g: {n: given(f"{g}_{n}", a) for n, a in m.items()} for g, m in groups.items()}
    out = nc.dram_tensor("out", alone["x"].shape, F32, kind="ExternalOutput").ap()
    perceiver(nc, out=out, **args)
    r = run_bass_kernel_spmd(nc, [arrays], core_ids=[0])
    return np.asarray(r.results[0]["out"]).swapaxes(0, 1).reshape(B, L, H)
```
